# Optimizing a Trainium2 kernel written in Bass

```python
import numpy as np
import jax
import jax.numpy as jnp

def _softmax(x, axis=-1):
    return jax.nn.softmax(x, axis=axis)

def _gelu(x):
    return jax.nn.gelu(x, approximate=True)

def _silu(x):
    return jax.nn.silu(x)

def _sigmoid(x):
    return jax.nn.sigmoid(x)

def _layernorm(x, axis=-1, eps=1e-05):
    m = jnp.mean(x, axis=axis, keepdims=True)
    v = jnp.var(x, axis=axis, keepdims=True)
    return (x - m) / jnp.sqrt(v + eps)

def _scatter_add(tgt, idx, src, axis=0):
    return tgt.at[idx].add(src)

def _segment_sum(src, seg, n):
    return jax.ops.segment_sum(src, seg, n)
kernel_name = 'mk_gnn_preln_d2_gnn_r32_430687'

def setup_inputs(seed: int=0):
    np.random.seed(seed)
    _w = jnp.asarray

    def _rec_inputs():
        import jax
        import jax.numpy as jnp
        _gk = jax.random.key(seed)
        x = -0.0005121 + 1.001 * jax.random.normal(jax.random.fold_in(_gk, 1), (3125, 64), jnp.float32)
        _s = jax.random.randint(jax.random.fold_in(_gk, 2), (50000,), 0, 3125, jnp.int32)
        _d = jax.random.randint(jax.random.fold_in(_gk, 3), (50000,), 0, 3125, jnp.int32)
        _loop = jnp.arange(3125, dtype=jnp.int32)
        src = jnp.concatenate([_s, _d, _loop])
        dst = jnp.concatenate([_d, _s, _loop])
        _o = jnp.argsort(dst, stable=True)
        src = src[_o]
        dst = dst[_o]
        edge_attr_64 = -9.77346e-05 + 0.999888 * jax.random.normal(jax.random.fold_in(_gk, 12), (103125, 64), jnp.float32)
        edge_weight = jax.random.uniform(jax.random.fold_in(_gk, 14), (103125,), jnp.float32, 0.0, 0.999998)
        return (x, src, dst, edge_attr_64, edge_weight)
    x, src, dst, edge_attr_64, edge_weight = _rec_inputs()

    def _L0_gnn_setup():
        import jax, jax.numpy as jnp
        import numpy as np
        N_NODES = 50000
        N_EDGES = 25000
        ATOM_F = 64
        NBR_F = 64
        EPS = 1e-05

        def batch_norm(x, gamma, beta):
            mu = x.mean(axis=0)
            var = x.var(axis=0)
            return gamma * (x - mu) * jax.lax.rsqrt(var + EPS) + beta
        key = jax.random.key(seed)
        ks = jax.random.split(key, 8)
        d_in = 2 * ATOM_F + NBR_F
        d_out = 2 * ATOM_F
        return {'atom_in_fea': jax.random.normal(ks[0], (N_NODES, ATOM_F), dtype=jnp.float32), 'nbr_fea': jax.random.normal(ks[1], (N_EDGES, NBR_F), dtype=jnp.float32), 'edge_src': jax.random.randint(ks[2], (N_EDGES,), 0, N_NODES), 'edge_dst': jax.random.randint(ks[3], (N_EDGES,), 0, N_NODES), 'W_full': jax.random.normal(ks[4], (d_in, d_out), dtype=jnp.float32) / np.sqrt(d_in), 'b_full': jnp.zeros((d_out,), dtype=jnp.float32), 'bn1_g': jnp.ones((d_out,), dtype=jnp.float32), 'bn1_b': jnp.zeros((d_out,), dtype=jnp.float32), 'bn2_g': jnp.ones((ATOM_F,), dtype=jnp.float32), 'bn2_b': jnp.zeros((ATOM_F,), dtype=jnp.float32)}
    _L0_gnn_all = _L0_gnn_setup()
    _L0_gnn_in = {k: v for k, v in _L0_gnn_all.items() if k in ('W_full', 'b_full', 'bn1_g', 'bn1_b', 'bn2_g', 'bn2_b')}
    del _L0_gnn_all

    def _L1_gnn_setup():
        import jax, jax.numpy as jnp
        import numpy as np
        N, E, DIN, DOUT = (50000, 25000, 64, 64)
        key = jax.random.key(seed)
        k1, k2, k3, k4, k5 = jax.random.split(key, 5)
        x = jax.random.normal(k1, (N, DIN), dtype=jnp.float32)
        edge_index = jax.random.randint(k2, (2, E), 0, N, dtype=jnp.int64)
        edge_attr = jax.random.uniform(k3, (E,), dtype=jnp.float32)
        W = jax.random.normal(k4, (DIN, DOUT), dtype=jnp.float32) / np.sqrt(DIN)
        b = jax.random.normal(k5, (DOUT,), dtype=jnp.float32) * 0.01
        return {'x': x, 'edge_index': edge_index, 'edge_attr': edge_attr, 'return_attention_weights': 0, 'W': W, 'b': b}
    _L1_gnn_all = _L1_gnn_setup()
    _L1_gnn_in = {k: v for k, v in _L1_gnn_all.items() if k in ('W', 'b')}
    del _L1_gnn_all
    return {'x': x, 'src': src, 'dst': dst, 'edge_attr_64': edge_attr_64, 'edge_weight': edge_weight, 'L0_gnn_W_full': _L0_gnn_in['W_full'], 'L0_gnn_b_full': _L0_gnn_in['b_full'], 'L0_gnn_bn1_g': _L0_gnn_in['bn1_g'], 'L0_gnn_bn1_b': _L0_gnn_in['bn1_b'], 'L0_gnn_bn2_g': _L0_gnn_in['bn2_g'], 'L0_gnn_bn2_b': _L0_gnn_in['bn2_b'], 'L1_gnn_W': _L1_gnn_in['W'], 'L1_gnn_b': _L1_gnn_in['b']}

def reference(x, src, dst, edge_attr_64, edge_weight, L0_gnn_W_full, L0_gnn_b_full, L0_gnn_bn1_g, L0_gnn_bn1_b, L0_gnn_bn2_g, L0_gnn_bn2_b, L1_gnn_W, L1_gnn_b):
    import jax
    import jax.numpy as jnp

    def _L0_gnn_ref(atom_in_fea, nbr_fea, edge_src, edge_dst, W_full, b_full, bn1_g, bn1_b, bn2_g, bn2_b):
        import jax, jax.numpy as jnp
        import numpy as np
        N_NODES = 50000
        N_EDGES = 25000
        ATOM_F = 64
        NBR_F = 64
        EPS = 1e-05

        def batch_norm(x, gamma, beta):
            mu = x.mean(axis=0)
            var = x.var(axis=0)
            return gamma * (x - mu) * jax.lax.rsqrt(var + EPS) + beta
        atom_src = atom_in_fea[edge_src]
        atom_dst = atom_in_fea[edge_dst]
        total = jnp.concatenate([atom_src, atom_dst, nbr_fea], axis=1)
        total = batch_norm(total @ W_full + b_full, bn1_g, bn1_b)
        filter_fea, core_fea = jnp.split(total, 2, axis=1)
        nbr_msg = jax.nn.sigmoid(filter_fea) * jax.nn.softplus(core_fea)
        atom_update = jax.ops.segment_sum(nbr_msg, edge_dst, num_segments=atom_in_fea.shape[0])
        return jax.nn.softplus(atom_in_fea + batch_norm(atom_update, bn2_g, bn2_b))

    def _L1_gnn_ref(x, edge_index, edge_attr, return_attention_weights, W, b):
        import jax, jax.numpy as jnp
        import numpy as np
        N, E, DIN, DOUT = (50000, 25000, 64, 64)
        n = x.shape[0]
        src, dst = (edge_index[0], edge_index[1])
        deg = jax.ops.segment_sum(jnp.ones_like(src, dtype=x.dtype), dst, num_segments=n)
        dis = jnp.where(deg > 0, jax.lax.rsqrt(jnp.maximum(deg, 1)), jnp.zeros_like(deg))
        norm = dis[src] * dis[dst]
        h = x @ W
        msg = h[src] * norm[:, None]
        out = jax.ops.segment_sum(msg, dst, num_segments=n) + b
        return out
    edge_index = jnp.stack([src, dst])
    h = jnp.maximum(_layernorm(x, axis=-1), 0.0)
    x = x + _L0_gnn_ref(h, edge_attr_64, src, dst, L0_gnn_W_full, L0_gnn_b_full, L0_gnn_bn1_g, L0_gnn_bn1_b, L0_gnn_bn2_g, L0_gnn_bn2_b)
    h = jnp.maximum(_layernorm(x, axis=-1), 0.0)
    x = x + _L1_gnn_ref(h, edge_index, edge_weight, 0, L1_gnn_W, L1_gnn_b)
    return x

_drawn_inputs = setup_inputs


def setup_inputs(seed=0):
    import zlib

    import numpy as np

    out = dict(_drawn_inputs(seed))
    spreads = {'L0_gnn_b_full': (0.0, 0.8),
     'L0_gnn_bn1_g': (1.0, 0.2),
     'L0_gnn_bn1_b': (0.0, 0.8),
     'L0_gnn_bn2_g': (1.0, 0.2),
     'L0_gnn_bn2_b': (0.0, 0.1)}
    factors = {'L1_gnn_b': 8.0}
    for name, (base, spread) in spreads.items():
        noise = np.random.default_rng([zlib.crc32(name.encode()), seed]).standard_normal(out[name].shape)
        drawn = base * np.exp(spread * noise) if base else spread * noise
        out[name] = jnp.asarray(drawn.astype(out[name].dtype))
    for name, factor in factors.items():
        out[name] = (out[name] * factor).astype(out[name].dtype)
    return out
```

```python
import numpy as np

import concourse.bass as bass
from concourse import mybir
from contextlib import ExitStack

P = 128
SLOTS = 8
GROUP = P * SLOTS
HALF = GROUP // 2
WIN = 64
WINB = 128
EPS = 1e-5
CAP = 40.0


def build_gnn(nc, x, src, dst, edge_attr, w_full, b_full, bn1_g, bn1_b, bn2_g, bn2_b, w1, b1, out):
    fp32, i32 = mybir.dt.float32, mybir.dt.int32
    ALU, ACT, AX = mybir.AluOpType, mybir.ActivationFunctionType, mybir.AxisListType

    N, F = x.shape
    E = src.shape[0]
    D = 2 * F
    NG = -(-E // GROUP)
    NFULL = E // GROUP
    TAIL = E - NFULL * GROUP
    PAIRS = NFULL // 2
    assert NFULL % 2 == 0 and 0 < TAIL and NG == NFULL + 1 and NG <= P
    NT = 25
    NP = N // NT
    assert NP * NT == N and NP <= P
    NW, NWB = -(-N // WIN), -(-N // WINB)
    TP, TR = TAIL // SLOTS, TAIL % SLOTS
    tail_valid = [-(-(TAIL - s) // SLOTS) for s in range(SLOTS)]

    tail_parts, at = [[], []], 2 * NFULL
    for h in range(2):
        s = 4 * h
        while s < 4 * h + 4:
            last = s
            while last + 1 < 4 * h + 4 and tail_valid[last + 1] == tail_valid[s]:
                last += 1
            tail_parts[h].append((s - 4 * h, last - 4 * h, tail_valid[s], at))
            s, at = last + 1, at + 1
    n_stats = at
    ds = bass.ds

    h_tab = nc.dram_tensor("h_tab", (N, F), fp32).ap()
    b_tab = nc.dram_tensor("b_tab", (N + WINB, D), fp32).ap()
    total_d = nc.dram_tensor("total_d", (D, NG * GROUP), fp32).ap()
    affine_d = nc.dram_tensor("affine_d", (D, 3), fp32).ap()
    g_tab = nc.dram_tensor("g_tab", (N, F), fp32).ap()

    ctx = ExitStack()
    with ctx:
        def sb(name, shape, dt=fp32, scope=None):
            return (scope or ctx).enter_context(nc.sbuf_tensor(name, shape, dt))

        def psum(name, shape, scope):
            return scope.enter_context(nc.psum_tensor(name, shape, fp32))

        def sem(name):
            return ctx.enter_context(nc.semaphore(name))

        X = sb("X", [NP, NT, F])
        H = sb("H", [NP, NT, F])
        ident = sb("ident", [P, P])
        base_bc = sb("base_bc", [P, NG])
        base_p = sb("base_p", [P, NG])
        win_p = sb("win_p", [P, NWB])
        win_c = sb("win_c", [P, NW])
        base_i = sb("base_i", [1, NG], i32)
        fits_i = sb("fits_i", [1, 1], i32)
        iota_w = sb("iota_w", [P, WIN])
        w_edge = sb("w_edge", [D, D])
        agg = sb("agg", [F + 1, N + WIN])
        agg2 = sb("agg2", [F, N + WIN])
        stats = sb("stats", [D, n_stats, 6])

        passed = sem("passed")

        def settle(eng):
            eng.sem_inc(passed, 1)

        def when_fits(eng, emit):
            fits = eng.value_load(fits_i[0:1, 0:1], min_val=0, max_val=1)
            with eng.If(fits == 1):
                emit(False)
            with eng.Else():
                emit(True)

        with ExitStack() as st:
            d_rows = sb("d_rows", [NG, GROUP], i32, st)
            w_dst = sb("w_dst", [F + 1, D], fp32, st)
            sq = sb("sq", [NP, NT, F], fp32, st)
            row = sb("row", [NP, 4, NT], fp32, st)
            HT = sb("HT", [F + 1, NT, NP], fp32, st)
            Brows = sb("Brows", [NP, NT, D], fp32, st)
            zero_rows = sb("zero_rows", [WINB, D], fp32, st)
            lo_hi = sb("lo_hi", [NG, 3], fp32, st)
            spread = sb("spread", [NG, 2, P], fp32, st)
            part = sb("part", [P, 1], fp32, st)
            flag = sb("flag", [P, 2], fp32, st)
            ps_t = [psum(f"ps_t{i}", [F, 4, NP], st) for i in range(2)]
            ps_b = [psum(f"ps_b{i}", [NP, 4, D], st) for i in range(2)]
            ps_g = psum("ps_g", [P, 2, NG], st)

            x_in, d_in, w_in = sem("x_in"), sem("d_in"), sem("w_in")
            consts, dve, act_ln, act_ht = sem("consts"), sem("dve"), sem("act_ln"), sem("act_ht")
            h_ready, ht_ps, b_ps, b_sb = sem("h_ready"), sem("ht_ps"), sem("b_ps"), sem("b_sb")
            spread_ready, spread_ps, tabs_out = sem("spread_ready"), sem("spread_ps"), sem("tabs_out")
            zero_ready, ones_ready = sem("zero_ready"), sem("ones_ready")
            chunks = [(c, min(4, NT - 4 * c)) for c in range(-(-NT // 4))]

            with nc.Block() as block:
                @block.sync
                def _(sp):
                    sp.dma_start(X[:, :, :], x.rearrange("(p t) f -> p t f", t=NT)).then_inc(x_in, 16)
                    sp.dma_start(d_rows[0:NFULL, :], dst[0:NFULL * GROUP].rearrange("(g e) -> g e", e=GROUP)).then_inc(d_in, 16)
                    sp.dma_start(d_rows[NFULL:NG, 0:TAIL], dst[NFULL * GROUP:E].rearrange("(g e) -> g e", g=1)).then_inc(d_in, 16)
                    fill = min(TAIL, GROUP - TAIL)
                    assert TAIL + fill == GROUP
                    sp.dma_start(d_rows[NFULL:NG, TAIL:GROUP], dst[E - fill:E].rearrange("(g e) -> g e", g=1)).then_inc(d_in, 16)
                    sp.dma_start(w_dst[0:F, :], w_full[F:2 * F, :]).then_inc(w_in, 16)
                    sp.dma_start(w_dst[F:F + 1, :], b_full.rearrange("(a f) -> a f", a=1)).then_inc(w_in, 16)
                    sp.dma_start(w_edge[0:F, :], w_full[0:F, :]).then_inc(w_in, 16)
                    sp.dma_start(w_edge[F:D, :], w_full[2 * F:3 * F, :]).then_inc(w_in, 16)
                    sp.wait_ge(zero_ready, 1)
                    sp.dma_start(b_tab[N:N + WINB, :], zero_rows[:, :]).then_inc(tabs_out, 16)
                    sp.wait_ge(h_ready, 1)
                    sp.dma_start(h_tab.rearrange("(p t) f -> p t f", t=NT), H[:, :, :]).then_inc(tabs_out, 16)
                    sp.wait_ge(b_sb, len(chunks))
                    sp.dma_start(b_tab[0:N, :].rearrange("(p t) f -> p t f", t=NT), Brows[:, :, :]).then_inc(tabs_out, 16)
                    sp.wait_ge(tabs_out, 48)

                @block.gpsimd
                def _(pool):
                    nc.gpsimd.memset(zero_rows[:, :], 0.0).then_inc(zero_ready, 1)
                    nc.gpsimd.memset(ident[:, :], 0.0).then_inc(consts, 1)
                    nc.gpsimd.iota(part[:, :], pattern=[[0, 1]], base=0, channel_multiplier=1,
                                   allow_small_or_imprecise_dtypes=True).then_inc(consts, 1)
                    nc.gpsimd.iota(iota_w[:, :], pattern=[[1, WIN]], base=0, channel_multiplier=0,
                                   allow_small_or_imprecise_dtypes=True).then_inc(consts, 1)
                    nc.gpsimd.iota(win_p[:, :], pattern=[[WINB, NWB]], base=0, channel_multiplier=1,
                                   allow_small_or_imprecise_dtypes=True).then_inc(consts, 1)
                    nc.gpsimd.iota(win_c[:, :], pattern=[[WIN, NW]], base=0, channel_multiplier=0,
                                   allow_small_or_imprecise_dtypes=True).then_inc(consts, 1)
                    nc.gpsimd.memset(agg2[:, :], 0.0).then_inc(consts, 1)
                    nc.gpsimd.memset(agg[:, :], 0.0).then_inc(consts, 1)
                    pool.wait_ge(consts, 7)
                    nc.gpsimd.affine_select(out=ident[:, :], in_=ident[:, :], compare_op=ALU.not_equal, fill=1.0,
                                            base=0, pattern=[[-1, P]], channel_multiplier=1).then_inc(consts, 1)

                @block.vector
                def _(v):
                    done = [0]

                    def step(ins):
                        done[0] += 1
                        ins.then_inc(dve, 1)
                        v.wait_ge(dve, done[0])

                    def per_node(k):
                        return row[:, k, :].unsqueeze(2).to_broadcast([NP, NT, F])

                    nc.vector.memset(HT[F:F + 1, :, :], 1.0).then_inc(ones_ready, 1)
                    v.wait_ge(x_in, 16)
                    step(nc.vector.reduce_sum(row[:, 0, :], X[:, :, :], axis=AX.X))
                    step(nc.vector.tensor_scalar(row[:, 1, :], row[:, 0, :], 1.0 / F, None, ALU.mult))
                    step(nc.vector.tensor_tensor(H[:, :, :], X[:, :, :], per_node(1), ALU.subtract))
                    step(nc.vector.tensor_tensor(sq[:, :, :], H[:, :, :], H[:, :, :], ALU.mult))
                    step(nc.vector.reduce_sum(row[:, 0, :], sq[:, :, :], axis=AX.X))
                    step(nc.vector.tensor_scalar(row[:, 2, :], row[:, 0, :], 1.0 / F, EPS, ALU.mult, ALU.add))
                    v.wait_ge(act_ln, 1)
                    step(nc.vector.reciprocal(row[:, 3, :], row[:, 1, :]))
                    step(nc.vector.tensor_tensor(sq[:, :, :], H[:, :, :], per_node(3), ALU.mult))
                    nc.vector.tensor_scalar(H[:, :, :], sq[:, :, :], 0.0, None, ALU.max).then_inc(h_ready, 1)
                    v.wait_ge(d_in, 48)
                    step(nc.vector.tensor_reduce(lo_hi[:, 0:1], d_rows[:, :], axis=AX.X, op=ALU.min))
                    step(nc.vector.tensor_reduce(lo_hi[:, 1:2], d_rows[:, :], axis=AX.X, op=ALU.max))
                    step(nc.vector.tensor_tensor(lo_hi[:, 2:3], lo_hi[:, 1:2], lo_hi[:, 0:1], ALU.subtract))
                    nc.vector.tensor_copy(spread[:, 0, :], lo_hi[:, 0:1].to_broadcast([NG, P])).then_inc(spread_ready, 1)
                    nc.vector.tensor_copy(spread[:, 1, :], lo_hi[:, 2:3].to_broadcast([NG, P])).then_inc(spread_ready, 1)
                    v.wait_ge(spread_ps, 2)
                    v.wait_ge(consts, 8)
                    step(nc.vector.tensor_copy(base_bc[:, :], ps_g[:, 0, :]))
                    step(nc.vector.tensor_scalar(base_p[:, :], base_bc[:, :], part[:, 0:1], None, ALU.add))
                    step(nc.vector.tensor_copy(base_i[:, :], base_bc[0:1, :]))
                    step(nc.vector.reduce_max(flag[:, 0:1], ps_g[:, 1, :], axis=AX.X))
                    step(nc.vector.tensor_scalar(flag[:, 1:2], flag[:, 0:1], float(WIN) - 0.5, None, ALU.is_lt))
                    step(nc.vector.tensor_copy(fits_i[:, :], flag[0:1, 1:2]))

                @block.scalar
                def _(a):
                    a.wait_ge(dve, 6)
                    nc.scalar.activation(row[:, 1, :], row[:, 2, :], ACT.Sqrt).then_inc(act_ln, 1)
                    for c, k in chunks:
                        a.wait_ge(ht_ps, c + 1)
                        nc.scalar.activation(HT[0:F, 4 * c:4 * c + k, :], ps_t[c % 2][:, 0:k, :], ACT.Copy).then_inc(act_ht, 1)
                        a.wait_ge(b_ps, c + 1)
                        nc.scalar.activation(Brows[:, 4 * c:4 * c + k, :], ps_b[c % 2][:, 0:k, :], ACT.Copy).then_inc(b_sb, 1)

                @block.tensor
                def _(pe):
                    pe.wait_ge(consts, 8)
                    pe.wait_ge(ones_ready, 1)
                    pe.wait_ge(w_in, 64)
                    pe.wait_ge(h_ready, 1)
                    for c, k in chunks:
                        if c >= 2:
                            pe.wait_ge(act_ht, c - 1)
                        for t in range(k):
                            last = nc.tensor.transpose(ps_t[c % 2][:, t, :], H[:, 4 * c + t, :], ident[0:NP, 0:NP])
                        last.then_inc(ht_ps, 1)
                        pe.wait_ge(act_ht, c + 1)
                        if c >= 2:
                            pe.wait_ge(b_sb, c - 1)
                        for t in range(k):
                            last = nc.tensor.matmul(ps_b[c % 2][:, t, :], HT[:, 4 * c + t, :], w_dst[:, :],
                                                    start=True, stop=True)
                        last.then_inc(b_ps, 1)
                    pe.wait_ge(spread_ready, 2)
                    for k in range(2):
                        nc.tensor.matmul(ps_g[:, k, :], spread[:, k, :], ident[0:NG, 0:NG],
                                         start=True, stop=True).then_inc(spread_ps, 1)

        with ExitStack() as st:
            idx = sb("idx", [P, 2, SLOTS], i32, st)
            Z = sb("Z", [P, 2, SLOTS, D], fp32, st)
            ZT = sb("ZT", [D, 2, HALF], fp32, st)
            d_row = sb("d_row", [P, 2, GROUP], i32, st)
            hot_t = sb("hot_t", [WINB, 2, GROUP], fp32, st)
            B_win = sb("B_win", [WINB, 2, D], fp32, st)
            tot = sb("tot", [D, 2, GROUP], fp32, st)
            ps_z = [psum(f"ps_z{h}", [D, HALF], st) for h in range(2)]
            ps_tot = [[psum(f"ps_tot{u}{h}", [D, HALF], st) for h in range(2)] for u in range(2)]

            idx_in = [sem(f"idx_in{u}") for u in range(2)]
            edge_in = [sem(f"edge_in{u}") for u in range(2)]
            drow_in = [sem(f"drow_in{u}") for u in range(2)]
            bwin_in = [sem(f"bwin_in{u}") for u in range(2)]
            gathered = [sem(f"gathered{u}") for u in range(2)]
            tot_out = [sem(f"tot_out{u}") for u in range(2)]
            zt_ps, zt_sb, zt_used = sem("zt_ps"), sem("zt_sb"), sem("zt_used")
            hot_ready, win_used, tail_set = sem("hot_ready"), sem("win_used"), sem("tail_set")
            tot_ps, tot_sb, tot_bn = sem("tot_ps"), sem("tot_sb"), sem("tot_bn")
            LEAD = 4

            def groups(eng, group):
                with eng.Fori(0, PAIRS) as i:
                    for u in range(2):
                        group(i, u, 2 * i + u, False)
                group(PAIRS, 0, NFULL, True)

            with nc.Block() as block:
                @block.sync
                def _(sp):
                    def stage(general):
                        def group(i, u, g, tail):
                            e0 = g * GROUP
                            d_cols = TAIL if tail else GROUP
                            sp.wait_ge(zt_used, 2 * g + 2)
                            if tail:
                                sp.wait_ge(tail_set, 3)
                                sp.dma_start(idx[0:TP, u, :], src[e0:e0 + TP * SLOTS].rearrange("(p s) -> p s", s=SLOTS)).then_inc(idx_in[u], 16)
                                sp.dma_start(idx[TP:TP + 1, u, 0:TR], src[e0 + TP * SLOTS:E].rearrange("(p s) -> p s", p=1)).then_inc(idx_in[u], 16)
                                sp.dma_start(Z[0:TP, u, :, F:D], edge_attr[e0:e0 + TP * SLOTS, :].rearrange("(p s) f -> p s f", s=SLOTS)).then_inc(edge_in[u], 16)
                                sp.dma_start(Z[TP:TP + 1, u, 0:TR, F:D], edge_attr[e0 + TP * SLOTS:E, :].rearrange("(p s) f -> p s f", p=1)).then_inc(edge_in[u], 16)
                            else:
                                sp.dma_start(idx[:, u, :], src[ds(e0, GROUP)].rearrange("(p s) -> p s", s=SLOTS)).then_inc(idx_in[u], 16)
                                sp.dma_start(Z[:, u, :, F:D], edge_attr[ds(e0, GROUP), :].rearrange("(p s) f -> p s f", s=SLOTS)).then_inc(edge_in[u], 16)
                            sp.wait_ge(tot_ps, 2 * g + 2)
                            sp.dma_start(d_row[:, u, 0:d_cols], dst[ds(e0, d_cols)].unsqueeze(0).to_broadcast([P, d_cols])).then_inc(drow_in[u], 16)
                            if general:
                                with sp.Fori(0, NWB) as r:
                                    sp.wait_ge(win_used, g * NWB + r + 1)
                                    sp.dma_start(B_win[:, 0, :], b_tab[ds(r * WINB, WINB), :]).then_inc(bwin_in[0], 16)
                            else:
                                first = sp.value_load(base_i[0:1, ds(g, 1)], min_val=0, max_val=N - 1)
                                sp.dma_start(B_win[:, u, :], b_tab[ds(first, WINB), :]).then_inc(bwin_in[u], 16)
                        groups(sp, group)
                    when_fits(sp, stage)

                @block.gpsimd
                def _(pool):
                    def group(i, u, g, tail):
                        pool.wait_ge(idx_in[u], 16 * i + (32 if tail else 16))
                        settle(pool)
                        for s in range(SLOTS):
                            pool.indirect_dma_start(Z[:, u, s, 0:F], None, h_tab[:, :],
                                                    bass.IndirectOffsetOnAxis(ap=idx[:, u, s:s + 1], axis=0)).then_inc(gathered[u], 16)
                    groups(pool, group)

                @block.vector
                def _(v):
                    v.sem_inc(tot_bn, LEAD)

                    def stage(general):
                        def hot(scalar, u, place):
                            return nc.vector.tensor_scalar(hot_t[:, place, :], d_row[:, u, :], scalar, None, ALU.is_equal)

                        def group(i, u, g, tail):
                            if tail:
                                v.wait_ge(zt_used, 2 * g + 2)
                                nc.vector.memset(idx[:, u, :], 0).then_inc(tail_set, 1)
                                nc.vector.memset(Z[:, u, :, F:D], 0.0).then_inc(tail_set, 1)
                                nc.vector.memset(d_row[:, u, TAIL:GROUP], -1).then_inc(tail_set, 1)
                                v.wait_ge(tail_set, 3)
                            v.wait_ge(drow_in[u], 16 * i + 16)
                            if general:
                                settle(v)
                                with v.Fori(0, NWB) as r:
                                    v.wait_ge(win_used, g * NWB + r + 1)
                                    hot(win_p[:, ds(r, 1)], u, 0).then_inc(hot_ready, 1)
                            else:
                                v.wait_ge(tot_ps, 2 * g + 2)
                                hot(base_p[:, ds(g, 1)], u, u).then_inc(hot_ready, 1)
                            for h in range(2):
                                v.wait_ge(tot_sb, 2 * g + h + 1 + LEAD)
                                half = tot[:, u, h * HALF:(h + 1) * HALF]
                                if tail:
                                    half = half.rearrange("f (s p) -> f s p", p=P)
                                    for first, last, valid, at in tail_parts[h]:
                                        done = nc.vector.bn_stats(stats[:, at, :], half[:, first:last + 1, 0:valid])
                                    done.then_inc(tot_bn, 1)
                                else:
                                    nc.vector.bn_stats(stats[:, 2 * g + h, :], half).then_inc(tot_bn, 1)
                        groups(v, group)
                    when_fits(v, stage)

                @block.scalar
                def _(a):
                    a.sem_inc(tot_sb, LEAD)
                    for u in range(2):
                        a.sem_inc(tot_out[u], 16)

                    def group(i, u, g, tail):
                        for h in range(2):
                            a.wait_ge(zt_ps, 2 * g + h + 1)
                            a.wait_ge(zt_used, 2 * g + h - 1 + LEAD)
                            nc.scalar.activation(ZT[:, h, :], ps_z[h][:, :], ACT.Copy).then_inc(zt_sb, 1)
                        a.wait_ge(tot_out[u], 16 * i + 16)
                        a.wait_ge(tot_bn, 2 * g + 2)
                        for h in range(2):
                            a.wait_ge(tot_ps, 2 * g + h + 1 + LEAD)
                            nc.scalar.activation(tot[:, u, h * HALF:(h + 1) * HALF], ps_tot[u][h][:, :], ACT.Copy).then_inc(tot_sb, 1)
                        a.wait_ge(tot_sb, 2 * g + 2 + LEAD)
                        a.dma_start(total_d[:, ds(g * GROUP, GROUP)], tot[:, u, :]).then_inc(tot_out[u], 16)
                    groups(a, group)
                    a.wait_ge(tot_out[0], 16 * (PAIRS + 2))
                    a.wait_ge(tot_out[1], 16 * (PAIRS + 1))

                @block.tensor
                def _(pe):
                    pe.sem_inc(zt_used, LEAD)
                    pe.sem_inc(tot_ps, LEAD)
                    pe.sem_inc(win_used, 1)

                    def stage(general):
                        def rows_at_dst(u, place, h, stop):
                            edges = hot_t[:, place, :].rearrange("w (p s) -> w s p", s=SLOTS)[:, 4 * h:4 * h + 4, :]
                            return nc.tensor.matmul(ps_tot[u][h][:, :], B_win[:, place, :], edges, start=False, stop=stop)

                        def group(i, u, g, tail):
                            pe.wait_ge(gathered[u], 16 * SLOTS * i + 16 * SLOTS)
                            pe.wait_ge(edge_in[u], 16 * i + (32 if tail else 16))
                            for h in range(2):
                                for s in range(4):
                                    last = nc.tensor.transpose(ps_z[h][:, s * P:(s + 1) * P], Z[:, u, 4 * h + s, :], ident[:, :])
                                last.then_inc(zt_ps, 1)
                            for h in range(2):
                                pe.wait_ge(zt_sb, 2 * g + h + 1)
                                pe.wait_ge(tot_sb, 2 * g + h + 1)
                                nc.tensor.matmul(ps_tot[u][h][:, :], w_edge[:, :], ZT[:, h, :], start=True, stop=False).then_inc(zt_used, 1)
                            if general:
                                def window(r, stop):
                                    pe.wait_ge(hot_ready, g * NWB + r + 1)
                                    pe.wait_ge(bwin_in[0], 16 * (g * NWB + r) + 16)
                                    rows_at_dst(u, 0, 0, stop)
                                    rows_at_dst(u, 0, 1, stop).then_inc(win_used, 1)

                                settle(pe)
                                with pe.Fori(0, NWB - 1) as r:
                                    window(r, False)
                                window(NWB - 1, True)
                                pe.wait_ge(win_used, g * NWB + NWB + 1)
                                pe.sem_inc(tot_ps, 2)
                            else:
                                pe.wait_ge(hot_ready, g + 1)
                                pe.wait_ge(bwin_in[u], 16 * i + 16)
                                for h in range(2):
                                    rows_at_dst(u, u, h, True).then_inc(tot_ps, 1)
                        groups(pe, group)
                    when_fits(pe, stage)

        filt, core = sb("filt", [P, 3]), sb("core", [P, 3])
        with ExitStack() as st:
            mv = sb("mv", [D, 2], fp32, st)
            gb = sb("gb", [D, 2], fp32, st)
            tmp = sb("tmp", [D, 4], fp32, st)
            aff = sb("aff", [D, 3], fp32, st)
            gb_in, bn, rt, aff_out, aff_in = sem("gb_in"), sem("bn"), sem("rt"), sem("aff_out"), sem("aff_in")
            with nc.Block() as block:
                @block.sync
                def _(sp):
                    sp.dma_start(gb[:, 0:1], bn1_g.rearrange("(f a) -> f a", a=1)).then_inc(gb_in, 16)
                    sp.dma_start(gb[:, 1:2], bn1_b.rearrange("(f a) -> f a", a=1)).then_inc(gb_in, 16)
                    sp.wait_ge(bn, 8)
                    sp.dma_start(affine_d[:, :], aff[:, :]).then_inc(aff_out, 16)
                    sp.wait_ge(aff_out, 16)
                    for k in range(2):
                        sp.dma_start(filt[k * F:(k + 1) * F, :], affine_d[0:F, :]).then_inc(aff_in, 16)
                        sp.dma_start(core[k * F:(k + 1) * F, :], affine_d[F:D, :]).then_inc(aff_in, 16)
                    sp.wait_ge(aff_in, 64)

                @block.vector
                def _(v):
                    def step(n, ins):
                        ins.then_inc(bn, 1)
                        v.wait_ge(bn, n)

                    step(1, nc.vector.bn_aggr(mv[:, :], stats[:, :, :].rearrange("f k s -> f (k s)")))
                    step(2, nc.vector.tensor_scalar(tmp[:, 0:1], mv[:, 1:2], EPS, None, ALU.add))
                    v.wait_ge(rt, 1)
                    step(3, nc.vector.reciprocal(tmp[:, 2:3], tmp[:, 1:2]))
                    v.wait_ge(gb_in, 32)
                    step(4, nc.vector.tensor_tensor(aff[:, 0:1], tmp[:, 2:3], gb[:, 0:1], ALU.mult))
                    step(5, nc.vector.tensor_tensor(tmp[:, 3:4], mv[:, 0:1], aff[:, 0:1], ALU.mult))
                    step(6, nc.vector.tensor_tensor(aff[:, 1:2], gb[:, 1:2], tmp[:, 3:4], ALU.subtract))
                    step(7, nc.vector.tensor_scalar(aff[0:F, 0:2], aff[0:F, 0:2], -1.0, None, ALU.mult))
                    step(8, nc.vector.tensor_scalar(aff[:, 2:3], aff[:, 1:2], -1.0, CAP, ALU.mult, ALU.add))

                @block.scalar
                def _(a):
                    a.wait_ge(bn, 2)
                    nc.scalar.activation(tmp[:, 1:2], tmp[:, 0:1], ACT.Sqrt).then_inc(rt, 1)

        class WindowSums:

            def __init__(self, name, st, into, rows):
                self.into, self.rows = into, rows
                self.d_e = sb(name + "_d_e", [P, 2, SLOTS], i32, st)
                self.rel = sb(name + "_rel", [P, 2, SLOTS], fp32, st)
                self.hot = sb(name + "_hot", [P, 2, SLOTS, WIN], fp32, st)
                self.ps = [psum(f"{name}_ps{u}", [rows, WIN], st) for u in range(2)]
                self.d_in = [sem(f"{name}_d_in{u}") for u in range(2)]
                self.d_set, self.d_used = sem(name + "_d_set"), sem(name + "_d_used")
                self.rel_ready, self.hot_ready = sem(name + "_rel_ready"), sem(name + "_hot_ready")
                self.summed, self.added = sem(name + "_summed"), sem(name + "_added")

            def start_vector(self, v):
                v.sem_inc(self.d_used, 2)
                v.sem_inc(self.added, 2)

            def start_tensor(self, pe):
                pe.sem_inc(self.summed, 2)

            def load_dst(self, sp, u, g, tail):
                e0 = g * GROUP
                sp.wait_ge(self.d_used, g + 1)
                if tail:
                    sp.wait_ge(self.d_set, 1)
                    sp.dma_start(self.d_e[0:TP, u, :], dst[e0:e0 + TP * SLOTS].rearrange("(p s) -> p s", s=SLOTS)).then_inc(self.d_in[u], 16)
                    sp.dma_start(self.d_e[TP:TP + 1, u, 0:TR], dst[e0 + TP * SLOTS:E].rearrange("(p s) -> p s", p=1)).then_inc(self.d_in[u], 16)
                else:
                    sp.dma_start(self.d_e[:, u, :], dst[ds(e0, GROUP)].rearrange("(p s) -> p s", s=SLOTS)).then_inc(self.d_in[u], 16)

            def one_hot(self, v, u, place, base, count):
                nc.vector.tensor_scalar(self.rel[:, place, :], self.d_e[:, u, :], base, None, ALU.subtract).then_inc(self.rel_ready, 1)
                v.wait_ge(self.rel_ready, count + 1)
                return nc.vector.tensor_tensor(self.hot[:, place, :, :],
                                               iota_w[:, :].unsqueeze(1).to_broadcast([P, SLOTS, WIN]),
                                               self.rel[:, place, :].unsqueeze(2).to_broadcast([P, SLOTS, WIN]),
                                               ALU.is_equal)

            def dst_arrived(self, v, i, u, g, tail):
                if tail:
                    v.wait_ge(self.d_used, g + 1)
                    nc.vector.memset(self.d_e[:, u, :], -1).then_inc(self.d_set, 1)
                v.wait_ge(self.d_in[u], 16 * i + (32 if tail else 16))

            def hots_fit(self, v, i, u, g, tail):
                self.dst_arrived(v, i, u, g, tail)
                v.wait_ge(self.summed, g + 1)
                self.one_hot(v, u, u, base_bc[:, ds(g, 1)], g).then_inc(self.hot_ready, 1)
                v.sem_inc(self.d_used, 1)

            def adds_fit(self, v, u, g):
                first = v.value_load(base_i[0:1, ds(g, 1)], min_val=0, max_val=N - 1)
                v.wait_ge(self.summed, g + 3)
                v.wait_ge(self.added, g + 2)
                window = self.into[:, ds(first, WIN)]
                nc.vector.tensor_tensor(window, window, self.ps[u][:, :], ALU.add).then_inc(self.added, 1)

            def all_windows(self, v, i, u, g, tail):
                self.dst_arrived(v, i, u, g, tail)
                settle(v)
                with v.Fori(0, NW) as r:
                    k = g * NW + r
                    v.wait_ge(self.added, k + 2)
                    self.one_hot(v, u, 0, win_c[:, ds(r, 1)], k).then_inc(self.hot_ready, 1)
                    v.wait_ge(self.summed, k + 3)
                    window = self.into[:, ds(r * WIN, WIN)]
                    nc.vector.tensor_tensor(window, window, self.ps[0][:, :], ALU.add).then_inc(self.added, 1)
                v.sem_inc(self.d_used, 1)

            def products(self, pe, general, lhs, g, u):
                def tiles(place):
                    for s in range(SLOTS):
                        last = nc.tensor.matmul(self.ps[place][:, :], lhs(s), self.hot[:, place, s, :],
                                                start=(s == 0), stop=(s == SLOTS - 1))
                    return last

                if general:
                    settle(pe)
                    with pe.Fori(0, NW) as r:
                        pe.wait_ge(self.hot_ready, g * NW + r + 1)
                        pe.wait_ge(self.added, g * NW + r + 2)
                        tiles(0).then_inc(self.summed, 1)
                else:
                    pe.wait_ge(self.hot_ready, g + 1)
                    pe.wait_ge(self.added, g + 1)
                    tiles(u).then_inc(self.summed, 1)

        with ExitStack() as st:
            W2 = [P, 2, 2, HALF]
            Ft, Ct = sb("Ft", W2, fp32, st), sb("Ct", W2, fp32, st)
            low_f, low_c = sb("low_f", W2, fp32, st), sb("low_c", W2, fp32, st)
            y = sb("y", W2, fp32, st)
            sig, soft = sb("sig", W2, fp32, st), sb("soft", W2, fp32, st)
            msg_t = sb("msg_t", W2, fp32, st)
            msg = sb("msg", [P, 2, SLOTS, F + 1], fp32, st)
            ps_m = [psum(f"ps_m{u}", [P, 4, P], st) for u in range(2)]
            sums = WindowSums("b", st, agg, F + 1)

            total_in = [sem(f"total_in{b}") for b in range(2)]
            low_f_r, low_c_r, y_r = sem("low_f_r"), sem("low_c_r"), sem("y_r")
            exp_f, exp_c, ln_f, ln_c = sem("exp_f"), sem("exp_c"), sem("ln_f"), sem("ln_c")
            sig_r, soft_r, msg_t_r = sem("sig_r"), sem("soft_r"), sem("msg_t_r")
            msg_ps, msg_sb, ones_set = sem("msg_ps"), sem("msg_sb"), sem("ones_set")

            def pipelined(eng, parts):
                def step(parity, half, k_of):
                    for fn, lag in parts:
                        b = (parity - lag) % 2
                        fn(half + (parity - lag - b) // 2, b, k_of - lag, 2)

                for k in range(2):
                    for fn, lag in parts:
                        if k >= lag:
                            fn((k - lag) // 2, (k - lag) % 2, k - lag, 2)
                with eng.Fori(1, PAIRS // 2) as j:
                    for parity in range(2):
                        step(parity, j, 2 * j + parity)
                for k in range(PAIRS, PAIRS + 3):
                    for fn, lag in parts:
                        if k - lag <= PAIRS:
                            fn((k - lag) // 2, (k - lag) % 2, k - lag, 2 if k - lag < PAIRS else 1)

            assert PAIRS % 2 == 0 and PAIRS >= 4

            with nc.Block() as block:
                @block.sync
                def _(sp):
                    def load(n, b, k, nu):
                        sp.wait_ge(y_r, k + 1)
                        for tile, f0 in ((Ft, 0), (Ct, F)):
                            for h in range(2):
                                from_ = total_d[f0:f0 + F, ds(k * (2 * GROUP), nu * GROUP)].rearrange("f (u h e) -> f h u e", u=nu, h=2)
                                sp.dma_start(tile[h * F:(h + 1) * F, b, 0:nu, :], from_[:, h, :, :]).then_inc(total_in[b], 16)

                    def load_dst(n, b, k, nu):
                        for u in range(nu):
                            sums.load_dst(sp, u, 2 * k + u, nu == 1)
                    pipelined(sp, [(load, 0), (load_dst, 1)])

                @block.vector
                def _(v):
                    v.sem_inc(y_r, 2)
                    v.sem_inc(soft_r, 2)
                    sums.start_vector(v)

                    def stage(general):
                        def affine(n, b, k, nu):
                            v.wait_ge(total_in[b], 64 * n + 64)
                            v.wait_ge(exp_c, k + 1)
                            v.wait_ge(soft_r, k + 1)
                            nc.vector.tensor_scalar(low_f[:, b, 0:nu, :], Ft[:, b, 0:nu, :], filt[:, 0:1], filt[:, 2:3],
                                                    ALU.mult, ALU.min).then_inc(low_f_r, 1)
                            nc.vector.tensor_scalar(low_c[:, b, 0:nu, :], Ct[:, b, 0:nu, :], core[:, 0:1], core[:, 2:3],
                                                    ALU.mult, ALU.min).then_inc(low_c_r, 1)
                            nc.vector.tensor_scalar(y[:, b, 0:nu, :], Ct[:, b, 0:nu, :], core[:, 0:1], core[:, 1:2],
                                                    ALU.mult, ALU.add).then_inc(y_r, 1)

                        def hots(n, b, k, nu):
                            if not general:
                                for u in range(nu):
                                    sums.hots_fit(v, k, u, 2 * k + u, nu == 1)

                        def softplus(n, b, k, nu):
                            v.wait_ge(ln_c, k + 1)
                            v.wait_ge(y_r, k + 3)
                            nc.vector.tensor_tensor(soft[:, b, 0:nu, :], y[:, b, 0:nu, :], soft[:, b, 0:nu, :],
                                                    ALU.max).then_inc(soft_r, 1)

                        def add(n, b, k, nu):
                            for u in range(nu):
                                if general:
                                    sums.all_windows(v, k, u, 2 * k + u, nu == 1)
                                else:
                                    sums.adds_fit(v, u, 2 * k + u)
                        pipelined(v, [(add, 2), (affine, 0), (softplus, 1), (hots, 1)])
                    when_fits(v, stage)

                @block.scalar
                def _(a):
                    a.sem_inc(exp_c, 2)
                    a.sem_inc(msg_sb, 2)

                    def functions(n, b, k, nu):
                        at = (slice(None), b, slice(0, nu), slice(None))
                        a.wait_ge(low_f_r, k + 1)
                        a.wait_ge(msg_t_r, k + 1)
                        nc.scalar.activation(sig[at], low_f[at], ACT.Exp, bias=filt[:, 1:2]).then_inc(exp_f, 1)
                        a.wait_ge(low_c_r, k + 1)
                        nc.scalar.activation(soft[at], low_c[at], ACT.Exp, bias=core[:, 1:2]).then_inc(exp_c, 1)
                        a.wait_ge(exp_f, k + 1)
                        nc.scalar.activation(sig[at], sig[at], ACT.Ln, bias=1.0).then_inc(ln_f, 1)
                        a.wait_ge(exp_c, k + 3)
                        nc.scalar.activation(soft[at], soft[at], ACT.Ln, bias=1.0).then_inc(ln_c, 1)
                        a.wait_ge(ln_f, k + 1)
                        nc.scalar.activation(sig[at], sig[at], ACT.Exp, scale=-1.0).then_inc(sig_r, 1)

                    def by_edge(n, b, k, nu):
                        for u in range(nu):
                            a.wait_ge(msg_ps, 2 * k + u + 5)
                            nc.scalar.activation(msg[:, u, :, 0:F].rearrange("p (h c) f -> p c h f", h=2),
                                                 ps_m[u][:, :, :].rearrange("p c (h f) -> p c h f", h=2), ACT.Copy).then_inc(msg_sb, 1)
                    pipelined(a, [(functions, 0), (by_edge, 1)])

                @block.gpsimd
                def _(pool):
                    pool.sem_inc(msg_t_r, 2)
                    nc.gpsimd.memset(msg[:, :, :, F:F + 1], 1.0).then_inc(ones_set, 1)

                    def multiply(n, b, k, nu):
                        at = (slice(None), b, slice(0, nu), slice(None))
                        pool.wait_ge(sig_r, k + 1)
                        pool.wait_ge(soft_r, k + 3)
                        pool.wait_ge(msg_ps, 2 * k + 2)
                        nc.gpsimd.tensor_tensor(msg_t[at], sig[at], soft[at], ALU.mult).then_inc(msg_t_r, 1)
                    pipelined(pool, [(multiply, 0)])

                @block.tensor
                def _(pe):
                    pe.sem_inc(msg_ps, 4)
                    sums.start_tensor(pe)

                    def stage(general):
                        pe.wait_ge(ones_set, 1)

                        def pair(n, b, k, nu):
                            pe.wait_ge(msg_t_r, k + 3)
                            for u in range(nu):
                                pe.wait_ge(msg_sb, 2 * k + u + 1)
                                for c in range(4):
                                    last = nc.tensor.transpose(ps_m[u][:, c, :], msg_t[:, b, u, c * P:(c + 1) * P], ident[:, :])
                                last.then_inc(msg_ps, 1)
                            for u in range(nu):
                                pe.wait_ge(msg_sb, 2 * k + u + 3)
                                sums.products(pe, general, lambda s: msg[:, u, s, :], 2 * k + u, u)
                        pipelined(pe, [(pair, 0)])
                    when_fits(pe, stage)

        dis = sb("dis", [NP, NT])
        out_b = sb("out_b", [NP, NT, F])
        with ExitStack() as st:
            U = sb("U", [F + 1, N], fp32, st)
            V = sb("V", [NP, NT, F + 1], fp32, st)
            T1, T2 = sb("T1", [NP, NT, F], fp32, st), sb("T2", [NP, NT, F], fp32, st)
            X1 = sb("X1", [NP, NT, F], fp32, st)
            nrow = sb("nrow", [NP, 6, NT], fp32, st)
            ab = sb("ab", [F + 1, 2], fp32, st)
            mv2 = sb("mv2", [F, 6], fp32, st)
            gb2 = sb("gb2", [F, 2], fp32, st)
            b1_bc = sb("b1_bc", [NP, F], fp32, st)
            NSTAT = -(-N // 512)
            cuts = [N * k // NSTAT for k in range(NSTAT + 1)]
            stats2 = sb("stats2", [F, NSTAT, 6], fp32, st)
            ps_v = [psum(f"ps_v{k}", [NP, 7, F + 1], st) for k in range(4)]
            vchunks = [(c, min(7, NT - 7 * c)) for c in range(-(-NT // 7))]
            assert len(vchunks) <= 4
            p_in, nd, na, v_ps, v_sb, g_out, g_ready = (sem(n) for n in ("p_in", "nd", "na", "v_ps", "v_sb", "g_out", "g_ready"))

            with nc.Block() as block:
                @block.sync
                def _(sp):
                    sp.dma_start(gb2[:, 0:1], bn2_g.rearrange("(f a) -> f a", a=1)).then_inc(p_in, 16)
                    sp.dma_start(gb2[:, 1:2], bn2_b.rearrange("(f a) -> f a", a=1)).then_inc(p_in, 16)
                    sp.dma_start(b1_bc[:, :], b1.unsqueeze(0).to_broadcast([NP, F])).then_inc(p_in, 16)
                    sp.wait_ge(g_ready, 1)
                    sp.dma_start(g_tab.rearrange("(p t) f -> p t f", t=NT), T2[:, :, :]).then_inc(g_out, 16)
                    sp.wait_ge(g_out, 16)

                @block.vector
                def _(v):
                    done = [0]

                    def step(ins):
                        done[0] += 1
                        ins.then_inc(nd, 1)
                        v.wait_ge(nd, done[0])

                    def per_node(k):
                        return nrow[:, k, :].unsqueeze(2).to_broadcast([NP, NT, F])

                    step(nc.vector.memset(ab[:, 0:1], 1.0))
                    step(nc.vector.memset(ab[:, 1:2], 0.0))
                    for k in range(NSTAT):
                        last = nc.vector.bn_stats(stats2[:, k, :], agg[0:F, cuts[k]:cuts[k + 1]])
                    step(last)
                    step(nc.vector.bn_aggr(mv2[:, 0:2], stats2[:, :, :].rearrange("f k s -> f (k s)")))
                    step(nc.vector.tensor_scalar(mv2[:, 2:3], mv2[:, 1:2], EPS, None, ALU.add))
                    v.wait_ge(na, 1)
                    step(nc.vector.reciprocal(mv2[:, 4:5], mv2[:, 3:4]))
                    v.wait_ge(p_in, 48)
                    step(nc.vector.tensor_tensor(ab[0:F, 0:1], mv2[:, 4:5], gb2[:, 0:1], ALU.mult))
                    step(nc.vector.tensor_tensor(mv2[:, 5:6], mv2[:, 0:1], ab[0:F, 0:1], ALU.mult))
                    step(nc.vector.tensor_tensor(ab[0:F, 1:2], gb2[:, 1:2], mv2[:, 5:6], ALU.subtract))
                    step(nc.vector.tensor_scalar(U[:, :], agg[:, 0:N], ab[:, 0:1], ab[:, 1:2], ALU.mult, ALU.add))
                    v.wait_ge(v_sb, len(vchunks))
                    step(nc.vector.tensor_tensor(T1[:, :, :], V[:, :, 0:F], H[:, :, :], ALU.add))
                    step(nc.vector.tensor_scalar(T2[:, :, :], T1[:, :, :], CAP, None, ALU.min))
                    step(nc.vector.tensor_scalar(nrow[:, 0, :], V[:, :, F], 1.0, None, ALU.max))
                    step(nc.vector.tensor_scalar(nrow[:, 1, :], V[:, :, F], 0.5, None, ALU.is_gt))
                    v.wait_ge(na, 3)
                    step(nc.vector.tensor_tensor(T1[:, :, :], T1[:, :, :], T2[:, :, :], ALU.max))
                    step(nc.vector.tensor_tensor(X1[:, :, :], X[:, :, :], T1[:, :, :], ALU.add))
                    v.wait_ge(na, 4)
                    step(nc.vector.reciprocal(nrow[:, 3, :], nrow[:, 2, :]))
                    step(nc.vector.tensor_tensor(dis[:, :], nrow[:, 3, :], nrow[:, 1, :], ALU.mult))
                    step(nc.vector.reduce_sum(nrow[:, 0, :], X1[:, :, :], axis=AX.X))
                    step(nc.vector.tensor_scalar(nrow[:, 1, :], nrow[:, 0, :], 1.0 / F, None, ALU.mult))
                    step(nc.vector.tensor_tensor(T1[:, :, :], X1[:, :, :], per_node(1), ALU.subtract))
                    step(nc.vector.tensor_tensor(T2[:, :, :], T1[:, :, :], T1[:, :, :], ALU.mult))
                    step(nc.vector.reduce_sum(nrow[:, 0, :], T2[:, :, :], axis=AX.X))
                    step(nc.vector.tensor_scalar(nrow[:, 3, :], nrow[:, 0, :], 1.0 / F, EPS, ALU.mult, ALU.add))
                    v.wait_ge(na, 5)
                    step(nc.vector.reciprocal(nrow[:, 5, :], nrow[:, 4, :]))
                    step(nc.vector.tensor_tensor(T2[:, :, :], T1[:, :, :], per_node(5), ALU.mult))
                    step(nc.vector.tensor_scalar(T1[:, :, :], T2[:, :, :], 0.0, None, ALU.max))
                    nc.vector.tensor_tensor(T2[:, :, :], T1[:, :, :], dis[:, :].unsqueeze(2).to_broadcast([NP, NT, F]),
                                            ALU.mult).then_inc(g_ready, 1)
                    nc.vector.tensor_tensor(out_b[:, :, :], X1[:, :, :], b1_bc[:, :].unsqueeze(1).to_broadcast([NP, NT, F]),
                                            ALU.add)

                @block.scalar
                def _(a):
                    a.wait_ge(nd, 5)
                    nc.scalar.activation(mv2[:, 3:4], mv2[:, 2:3], ACT.Sqrt).then_inc(na, 1)
                    for c, k in vchunks:
                        a.wait_ge(v_ps, c + 1)
                        nc.scalar.activation(V[:, 7 * c:7 * c + k, :], ps_v[c][:, 0:k, :], ACT.Copy).then_inc(v_sb, 1)
                    a.wait_ge(nd, 12)
                    nc.scalar.activation(T2[:, :, :], T2[:, :, :], ACT.Exp).then_inc(na, 1)
                    a.wait_ge(na, 2)
                    nc.scalar.activation(T2[:, :, :], T2[:, :, :], ACT.Ln, bias=1.0).then_inc(na, 1)
                    a.wait_ge(nd, 13)
                    nc.scalar.activation(nrow[:, 2, :], nrow[:, 0, :], ACT.Sqrt).then_inc(na, 1)
                    a.wait_ge(nd, 24)
                    nc.scalar.activation(nrow[:, 4, :], nrow[:, 3, :], ACT.Sqrt).then_inc(na, 1)

                @block.tensor
                def _(pe):
                    pe.wait_ge(nd, 10)
                    nodes = U[:, :].rearrange("f (p t) -> f t p", t=NT)
                    for c, k in vchunks:
                        for t in range(k):
                            last = nc.tensor.transpose(ps_v[c][:, t, :], nodes[:, 7 * c + t, :], ident[0:F + 1, 0:F + 1])
                        last.then_inc(v_ps, 1)

        with ExitStack() as st:
            idx2 = sb("idx2", [P, 2, SLOTS], i32, st)
            R = sb("R", [P, 2, SLOTS, F], fp32, st)
            sums = WindowSums("c", st, agg2, F)
            idx2_in = [sem(f"idx2_in{u}") for u in range(2)]
            rows_in = [sem(f"rows_in{u}") for u in range(2)]
            rows_used, idx2_set = sem("rows_used"), sem("idx2_set")

            with nc.Block() as block:
                @block.sync
                def _(sp):
                    def group(i, u, g, tail):
                        e0 = g * GROUP
                        sp.wait_ge(rows_used, g + 1)
                        if tail:
                            sp.wait_ge(idx2_set, 1)
                            sp.dma_start(idx2[0:TP, u, :], src[e0:e0 + TP * SLOTS].rearrange("(p s) -> p s", s=SLOTS)).then_inc(idx2_in[u], 16)
                            sp.dma_start(idx2[TP:TP + 1, u, 0:TR], src[e0 + TP * SLOTS:E].rearrange("(p s) -> p s", p=1)).then_inc(idx2_in[u], 16)
                        else:
                            sp.dma_start(idx2[:, u, :], src[ds(e0, GROUP)].rearrange("(p s) -> p s", s=SLOTS)).then_inc(idx2_in[u], 16)
                        sums.load_dst(sp, u, g, tail)
                    groups(sp, group)

                @block.gpsimd
                def _(pool):
                    def group(i, u, g, tail):
                        pool.wait_ge(idx2_in[u], 16 * i + (32 if tail else 16))
                        settle(pool)
                        for s in range(SLOTS):
                            pool.indirect_dma_start(R[:, u, s, :], None, g_tab[:, :],
                                                    bass.IndirectOffsetOnAxis(ap=idx2[:, u, s:s + 1], axis=0)).then_inc(rows_in[u], 16)
                    groups(pool, group)

                @block.vector
                def _(v):
                    sums.start_vector(v)

                    def stage(general):
                        def group(i, u, g, tail):
                            if tail:
                                v.wait_ge(rows_used, g + 1)
                                nc.vector.memset(idx2[:, u, :], 0).then_inc(idx2_set, 1)
                            if general:
                                sums.all_windows(v, i, u, g, tail)
                            else:
                                sums.hots_fit(v, i, u, g, tail)
                                sums.adds_fit(v, u, g)
                        groups(v, group)
                    when_fits(v, stage)

                @block.tensor
                def _(pe):
                    pe.sem_inc(rows_used, 2)
                    sums.start_tensor(pe)

                    def stage(general):
                        def group(i, u, g, tail):
                            pe.wait_ge(rows_in[u], 16 * SLOTS * i + 16 * SLOTS)
                            sums.products(pe, general, lambda s: R[:, u, s, :], g, u)
                            pe.wait_ge(sums.summed, (g * NW + NW if general else g + 1) + 2)
                            pe.sem_inc(rows_used, 1)
                        groups(pe, group)
                    when_fits(pe, stage)

        with ExitStack() as st:
            W1 = sb("W1", [F, F], fp32, st)
            O = sb("O", [NP, NT, F], fp32, st)
            ps_o = [psum(f"ps_o{k}", [NP, 8, F], st) for k in range(4)]
            ochunks = [(c, min(8, NT - 8 * c)) for c in range(-(-NT // 8))]
            assert len(ochunks) <= 4
            w1_in, o_ps, o_mul, o_sb, stored = (sem(n) for n in ("w1_in", "o_ps", "o_mul", "o_sb", "stored"))

            with nc.Block() as block:
                @block.sync
                def _(sp):
                    sp.dma_start(W1[:, :], w1[:, :]).then_inc(w1_in, 16)
                    sp.wait_ge(o_sb, len(ochunks))
                    sp.dma_start(out.rearrange("(p t) f -> p t f", t=NT), O[:, :, :]).then_inc(stored, 16)
                    sp.wait_ge(stored, 16)

                @block.vector
                def _(v):
                    for c, k in ochunks:
                        at = (slice(None), slice(8 * c, 8 * c + k), slice(None))
                        v.wait_ge(o_ps, c + 1)
                        nc.vector.tensor_tensor(O[at], ps_o[c][:, 0:k, :],
                                                dis[:, 8 * c:8 * c + k].unsqueeze(2).to_broadcast([NP, k, F]), ALU.mult).then_inc(o_mul, 1)
                        v.wait_ge(o_mul, c + 1)
                        nc.vector.tensor_tensor(O[at], O[at], out_b[at], ALU.add).then_inc(o_sb, 1)

                @block.tensor
                def _(pe):
                    pe.wait_ge(w1_in, 16)
                    nodes = agg2[:, 0:N].rearrange("f (p t) -> f t p", t=NT)
                    for c, k in ochunks:
                        for t in range(k):
                            last = nc.tensor.matmul(ps_o[c][:, t, :], nodes[:, 8 * c + t, :], W1[:, :], start=True, stop=True)
                        last.then_inc(o_ps, 1)


INPUTS = ["x", "src", "dst", "edge_attr_64", "L0_gnn_W_full", "L0_gnn_b_full", "L0_gnn_bn1_g", "L0_gnn_bn1_b",
          "L0_gnn_bn2_g", "L0_gnn_bn2_b", "L1_gnn_W", "L1_gnn_b"]


def kernel(**inputs):
    import concourse.bacc as bacc
    from concourse.bass_utils import run_bass_kernel_spmd as run

    nc = bacc.Bacc("TRN2", target_bir_lowering=False, num_devices=1)
    arrays = {"in_" + k: np.ascontiguousarray(inputs[k]) for k in INPUTS}
    args = [nc.dram_tensor(k, v.shape, mybir.dt.from_np(v.dtype), kind="ExternalInput").ap() for k, v in arrays.items()]
    result = nc.dram_tensor("out_0", inputs["x"].shape, mybir.dt.float32, kind="ExternalOutput").ap()
    build_gnn(nc, *args, result)
    r = run(nc, [arrays], core_ids=[0])
    return r.results[0]["out_0"]
```

```python
import numpy as np

import concourse.bass as bass
from concourse import mybir
from contextlib import ExitStack

P = 128
SLOTS = 8
GROUP = P * SLOTS
HALF = GROUP // 2
WIN = 64
WINB = 64
WINH = 32
EPS = 1e-5
CAP = 40.0


def build_gnn(nc, x, src, dst, edge_attr, w_full, b_full, bn1_g, bn1_b, bn2_g, bn2_b, w1, b1, out):
    fp32, i32, bf16, i16, u8 = (mybir.dt.float32, mybir.dt.int32, mybir.dt.bfloat16, mybir.dt.int16, mybir.dt.uint8)
    ALU, ACT, AX = mybir.AluOpType, mybir.ActivationFunctionType, mybir.AxisListType

    N, F = x.shape
    E = src.shape[0]
    D = 2 * F
    NG = -(-E // GROUP)
    NFULL = E // GROUP
    TAIL = E - NFULL * GROUP
    PAIRS = NFULL // 2
    assert NFULL % 2 == 0 and 0 < TAIL and NG == NFULL + 1 and NG <= P
    NT = 25
    NP = N // NT
    assert NP * NT == N and NP <= P
    NW, NWB = -(-N // WIN), -(-N // WINB)
    tail_halves = [(n, n // 4, n % 4) for n in (min(HALF, TAIL), max(0, TAIL - HALF))]
    tail_valid = [-(-max(0, tail_halves[s // 4][0] - s % 4) // 4) for s in range(SLOTS)]
    assert tail_halves[1][0] > 0
    HI = -(-N // P)
    SHIFT = (P // WINH).bit_length() - 1
    assert P == WINH << SHIFT

    tail_parts, at = [[], []], 2 * NFULL
    for h in range(2):
        s = 4 * h
        while s < 4 * h + 4:
            last = s
            while last + 1 < 4 * h + 4 and tail_valid[last + 1] == tail_valid[s]:
                last += 1
            tail_parts[h].append((s - 4 * h, last - 4 * h, tail_valid[s], at))
            s, at = last + 1, at + 1
    n_stats = at
    ds = bass.ds

    def pipelined(eng, parts, full):
        longest = max(lag for _, lag in parts)
        fill = max(2, longest + longest % 2)
        assert full % 2 == 0 and full > fill

        def straight(steps):
            for k in steps:
                for fn, lag in parts:
                    if 0 <= k - lag <= full:
                        fn((k - lag) // 2, (k - lag) % 2, k - lag, k - lag == full)

        straight(range(fill))
        with eng.Fori(fill // 2, full // 2) as j:
            for parity in range(2):
                for fn, lag in parts:
                    u = (parity - lag) % 2
                    fn(j + (parity - lag - u) // 2, u, 2 * j + (parity - lag), False)
        straight(range(full, full + 1 + longest))

    def load_by_edge(sp, place, source, g, tail, signal):
        if not tail:
            if len(source.shape) == 1:
                v = source[ds(g * GROUP, GROUP)].rearrange("(h p s) -> p h s", h=2, s=4)
                sp.dma_start(place(slice(0, P), slice(0, 2), slice(0, 4)), v).then_inc(signal, 16)
                return
            for h in range(2):
                v = source[ds(g * GROUP + h * HALF, HALF), :].rearrange("(p s) f -> p s f", s=4)
                sp.dma_start(place(slice(0, P), h, slice(0, 4)), v).then_inc(signal, 16)
            return
        for h, (n, full, rest) in enumerate(tail_halves):
            e0 = g * GROUP + h * HALF
            for p0, p1, k in ((0, full, 4), (full, full + 1, rest)):
                if k and p1 > p0:
                    v = source[e0 + 4 * p0:e0 + 4 * p0 + (p1 - p0) * k]
                    v = v.rearrange("(p s) -> p s", s=k) if len(source.shape) == 1 else v.rearrange("(p s) f -> p s f", s=k)
                    sp.dma_start(place(slice(p0, p1), h, slice(0, k)), v).then_inc(signal, 16)

    TAIL_LOADS = sum((full > 0) + (rest > 0) for _, full, rest in tail_halves)

    h_tab = nc.dram_tensor("h_tab", (N, F), fp32).ap()
    b_tab = nc.dram_tensor("b_tab", (N + WINB, D), fp32).ap()
    total_d = nc.dram_tensor("total_d", (D, NG * GROUP), fp32).ap()
    affine_d = nc.dram_tensor("affine_d", (D, 3), fp32).ap()
    g_tab = nc.dram_tensor("g_tab", (N, F), fp32).ap()

    ctx = ExitStack()
    with ctx:
        def sb(name, shape, dt=fp32, scope=None):
            return (scope or ctx).enter_context(nc.sbuf_tensor(name, shape, dt))

        def psum(name, shape, scope):
            return scope.enter_context(nc.psum_tensor(name, shape, fp32))

        def sem(name):
            return ctx.enter_context(nc.semaphore(name))

        X = sb("X", [NP, NT, F])
        H = sb("H", [NP, NT, F])
        ident = sb("ident", [P, P])
        base_bc = sb("base_bc", [P, NG, 2])
        base_p = sb("base_p", [P, NG])
        win_p = sb("win_p", [P, NWB])
        win_c = sb("win_c", [P, NW])
        base_i = sb("base_i", [1, NG * 2], i32)
        fits_i = sb("fits_i", [1, 1], i32)
        counted_i = sb("counted_i", [1, 1], i32)
        count = sb("count", [P, HI, -(-(N + WINH) // 4) * 4], u8)
        iota_w = sb("iota_w", [P, WIN])
        w_edge = sb("w_edge", [D, D])
        agg = sb("agg", [F + 1, N + WIN])
        stats = sb("stats", [D, n_stats, 6])

        passed = sem("passed")

        def settle(eng):
            eng.sem_inc(passed, 1)

        def when_fits(eng, emit, flag=fits_i):
            fits = eng.value_load(flag[0:1, 0:1], min_val=0, max_val=1)
            with eng.If(fits == 1):
                emit(False)
            with eng.Else():
                emit(True)

        with ExitStack() as st:
            d_rows = sb("d_rows", [NG, GROUP], i32, st)
            w_dst = sb("w_dst", [F + 1, D], fp32, st)
            sq = sb("sq", [NP, NT, F], fp32, st)
            row = sb("row", [NP, 4, NT], fp32, st)
            HT = sb("HT", [F + 1, NT, NP], fp32, st)
            Brows = sb("Brows", [NP, NT, D], fp32, st)
            zero_rows = sb("zero_rows", [WINB, D], fp32, st)
            lo_hi = sb("lo_hi", [NG, 2, 2], fp32, st)
            spread = sb("spread", [NG, 4, P], fp32, st)
            ends = sb("ends", [P, 2, 2 * NG], fp32, st)
            gaps = sb("gaps", [P, 3, 2 * NG], fp32, st)
            part = sb("part", [P, 1], fp32, st)
            flag = sb("flag", [P, 4], fp32, st)
            ps_t = [psum(f"ps_t{i}", [F, 4, NP], st) for i in range(2)]
            ps_b = [psum(f"ps_b{i}", [NP, 4, D], st) for i in range(2)]
            ps_g = psum("ps_g", [P, 4, NG], st)

            x_in, d_in, w_in = sem("x_in"), sem("d_in"), sem("w_in")
            consts, dve, act_ln, act_ht = sem("consts"), sem("dve"), sem("act_ln"), sem("act_ht")
            h_ready, ht_ps, b_ps, b_sb = sem("h_ready"), sem("ht_ps"), sem("b_ps"), sem("b_sb")
            spread_ready, spread_ps, tabs_out = sem("spread_ready"), sem("spread_ps"), sem("tabs_out")
            zero_ready, ones_ready = sem("zero_ready"), sem("ones_ready")
            fills = [(at, min(tail_halves[1][0], GROUP - at)) for at in range(TAIL, GROUP, tail_halves[1][0])]
            chunks = [(c, min(4, NT - 4 * c)) for c in range(-(-NT // 4))]

            with nc.Block() as block:
                @block.sync
                def _(sp):
                    sp.dma_start(X[:, :, :], x.rearrange("(p t) f -> p t f", t=NT)).then_inc(x_in, 16)
                    sp.dma_start(d_rows[0:NFULL, :], dst[0:NFULL * GROUP].rearrange("(g e) -> g e", e=GROUP)).then_inc(d_in, 16)
                    sp.dma_start(d_rows[NFULL:NG, 0:TAIL], dst[NFULL * GROUP:E].rearrange("(g e) -> g e", g=1)).then_inc(d_in, 16)
                    for at, n in fills:
                        sp.dma_start(d_rows[NFULL:NG, at:at + n], dst[E - n:E].rearrange("(g e) -> g e", g=1)).then_inc(d_in, 16)
                    sp.dma_start(w_dst[0:F, :], w_full[F:2 * F, :]).then_inc(w_in, 16)
                    sp.dma_start(w_dst[F:F + 1, :], b_full.rearrange("(a f) -> a f", a=1)).then_inc(w_in, 16)
                    sp.dma_start(w_edge[0:F, :], w_full[0:F, :]).then_inc(w_in, 16)
                    sp.dma_start(w_edge[F:D, :], w_full[2 * F:3 * F, :]).then_inc(w_in, 16)
                    sp.wait_ge(zero_ready, 1)
                    sp.dma_start(b_tab[N:N + WINB, :], zero_rows[:, :]).then_inc(tabs_out, 16)
                    sp.wait_ge(h_ready, 1)
                    sp.dma_start(h_tab.rearrange("(p t) f -> p t f", t=NT), H[:, :, :]).then_inc(tabs_out, 16)
                    sp.wait_ge(b_sb, len(chunks))
                    sp.dma_start(b_tab[0:N, :].rearrange("(p t) f -> p t f", t=NT), Brows[:, :, :]).then_inc(tabs_out, 16)
                    sp.wait_ge(tabs_out, 48)

                @block.gpsimd
                def _(pool):
                    nc.gpsimd.memset(zero_rows[:, :], 0.0).then_inc(zero_ready, 1)
                    nc.gpsimd.memset(ident[:, :], 0.0).then_inc(consts, 1)
                    nc.gpsimd.iota(part[:, :], pattern=[[0, 1]], base=0, channel_multiplier=1,
                                   allow_small_or_imprecise_dtypes=True).then_inc(consts, 1)
                    nc.gpsimd.iota(iota_w[:, :], pattern=[[1, WIN]], base=0, channel_multiplier=0,
                                   allow_small_or_imprecise_dtypes=True).then_inc(consts, 1)
                    nc.gpsimd.iota(win_p[:, :], pattern=[[WINB, NWB]], base=0, channel_multiplier=1,
                                   allow_small_or_imprecise_dtypes=True).then_inc(consts, 1)
                    nc.gpsimd.iota(win_c[:, :], pattern=[[WIN, NW]], base=0, channel_multiplier=0,
                                   allow_small_or_imprecise_dtypes=True).then_inc(consts, 1)
                    nc.gpsimd.memset(count[:, :, :].bitcast(i32), 0).then_inc(consts, 1)
                    nc.gpsimd.memset(agg[:, :], 0.0).then_inc(consts, 1)
                    pool.wait_ge(consts, 7)
                    nc.gpsimd.affine_select(out=ident[:, :], in_=ident[:, :], compare_op=ALU.not_equal, fill=1.0,
                                            base=0, pattern=[[-1, P]], channel_multiplier=1).then_inc(consts, 1)

                @block.vector
                def _(v):
                    done = [0]

                    def step(ins):
                        done[0] += 1
                        ins.then_inc(dve, 1)
                        v.wait_ge(dve, done[0])

                    def per_node(k):
                        return row[:, k, :].unsqueeze(2).to_broadcast([NP, NT, F])

                    nc.vector.memset(HT[F:F + 1, :, :], 1.0).then_inc(ones_ready, 1)
                    v.wait_ge(x_in, 16)
                    step(nc.vector.reduce_sum(row[:, 0, :], X[:, :, :], axis=AX.X))
                    step(nc.vector.tensor_scalar(row[:, 1, :], row[:, 0, :], 1.0 / F, None, ALU.mult))
                    step(nc.vector.tensor_tensor(H[:, :, :], X[:, :, :], per_node(1), ALU.subtract))
                    step(nc.vector.tensor_tensor(sq[:, :, :], H[:, :, :], H[:, :, :], ALU.mult))
                    step(nc.vector.reduce_sum(row[:, 0, :], sq[:, :, :], axis=AX.X))
                    step(nc.vector.tensor_scalar(row[:, 2, :], row[:, 0, :], 1.0 / F, EPS, ALU.mult, ALU.add))
                    v.wait_ge(act_ln, 1)
                    step(nc.vector.reciprocal(row[:, 3, :], row[:, 1, :]))
                    step(nc.vector.tensor_tensor(sq[:, :, :], H[:, :, :], per_node(3), ALU.mult))
                    nc.vector.tensor_scalar(H[:, :, :], sq[:, :, :], 0.0, None, ALU.max).then_inc(h_ready, 1)
                    v.wait_ge(d_in, 16 * (2 + len(fills)))
                    halves = d_rows[:, :].rearrange("g (h e) -> g h e", h=2)
                    nc.vector.tensor_reduce(lo_hi[:, 0, :], halves, axis=AX.X, op=ALU.min)
                    step(nc.vector.tensor_reduce(lo_hi[:, 1, :], halves, axis=AX.X, op=ALU.max))
                    nc.vector.tensor_copy(spread[:, :, :], lo_hi[:, :, :].rearrange("g k h -> g (k h)").unsqueeze(2).to_broadcast([NG, 4, P])).then_inc(spread_ready, 1)
                    v.wait_ge(spread_ps, 1)
                    v.wait_ge(consts, 8)
                    for k in range(2):
                        last = nc.vector.tensor_copy(ends[:, k, :].rearrange("p (g h) -> p h g", h=2), ps_g[:, 2 * k:2 * k + 2, :])
                    step(last)
                    nc.vector.tensor_copy(base_bc[:, :, :], ends[:, 0, :].rearrange("p (g h) -> p g h", h=2))
                    nc.vector.tensor_scalar(base_p[:, :], ends[:, 0, :].rearrange("p (g h) -> p g h", h=2)[:, :, 0], part[:, 0:1], None, ALU.add)
                    nc.vector.tensor_copy(base_i[:, :], ends[0:1, 0, :])
                    step(nc.vector.memset(gaps[:, :, :], 0.0))
                    nc.vector.tensor_tensor(gaps[:, 0, :], ends[:, 1, :], ends[:, 0, :], ALU.subtract)
                    nc.vector.tensor_tensor(gaps[:, 1, 0:NG], ends[:, 1, :].rearrange("p (g h) -> p g h", h=2)[:, :, 1],
                                            ends[:, 0, :].rearrange("p (g h) -> p g h", h=2)[:, :, 0], ALU.subtract)
                    step(nc.vector.tensor_tensor(gaps[:, 2, 1:], ends[:, 1, 0:2 * NG - 1], ends[:, 0, 1:], ALU.subtract))
                    step(nc.vector.tensor_reduce(flag[:, 0:3], gaps[:, :, :], axis=AX.X, op=ALU.max))
                    for k, limit in enumerate((WINH - 0.5, WIN - 0.5, 0.5)):
                        last = nc.vector.tensor_scalar(flag[:, k:k + 1], flag[:, k:k + 1], float(limit), None, ALU.is_lt)
                    step(last)
                    step(nc.vector.tensor_tensor(flag[:, 0:1], flag[:, 0:1], flag[:, 1:2], ALU.mult))
                    step(nc.vector.tensor_tensor(flag[:, 1:2], flag[:, 0:1], flag[:, 2:3], ALU.mult))
                    step(nc.vector.tensor_copy(fits_i[:, :], flag[0:1, 1:2]))

                @block.scalar
                def _(a):
                    a.wait_ge(dve, 6)
                    nc.scalar.activation(row[:, 1, :], row[:, 2, :], ACT.Sqrt).then_inc(act_ln, 1)
                    for c, k in chunks:
                        a.wait_ge(ht_ps, c + 1)
                        nc.scalar.activation(HT[0:F, 4 * c:4 * c + k, :], ps_t[c % 2][:, 0:k, :], ACT.Copy).then_inc(act_ht, 1)
                        a.wait_ge(b_ps, c + 1)
                        nc.scalar.activation(Brows[:, 4 * c:4 * c + k, :], ps_b[c % 2][:, 0:k, :], ACT.Copy).then_inc(b_sb, 1)

                @block.tensor
                def _(pe):
                    pe.wait_ge(consts, 8)
                    pe.wait_ge(ones_ready, 1)
                    pe.wait_ge(w_in, 64)
                    pe.wait_ge(h_ready, 1)
                    for c, k in chunks:
                        if c >= 2:
                            pe.wait_ge(act_ht, c - 1)
                        for t in range(k):
                            last = nc.tensor.transpose(ps_t[c % 2][:, t, :], H[:, 4 * c + t, :], ident[0:NP, 0:NP])
                        last.then_inc(ht_ps, 1)
                        pe.wait_ge(act_ht, c + 1)
                        if c >= 2:
                            pe.wait_ge(b_sb, c - 1)
                        for t in range(k):
                            last = nc.tensor.matmul(ps_b[c % 2][:, t, :], HT[:, 4 * c + t, :], w_dst[:, :],
                                                    start=True, stop=True)
                        last.then_inc(b_ps, 1)
                    pe.wait_ge(spread_ready, 1)
                    for k in range(4):
                        last = nc.tensor.matmul(ps_g[:, k, :], spread[:, k, :], ident[0:NG, 0:NG], start=True, stop=True)
                    last.then_inc(spread_ps, 1)

        with ExitStack() as st:
            idx = sb("idx", [P, 2, SLOTS], i32, st)
            Z = sb("Z", [P, 2, SLOTS, D], fp32, st)
            ZT = sb("ZT", [D, 2, HALF], fp32, st)
            d_row = sb("d_row", [WINB, 2, GROUP], i32, st)
            hot_t = sb("hot_t", [WINB, 2, GROUP], fp32, st)
            B_win = sb("B_win", [WINB, 2, D], fp32, st)
            tot = sb("tot", [D, 2, GROUP], fp32, st)
            ps_z = [psum(f"ps_z{h}", [D, HALF], st) for h in range(2)]
            ps_tot = [psum(f"ps_tot{h}", [D, HALF], st) for h in range(2)]
            iota_lo, iota_key = sb("iota_lo", [P, P], i16, st), sb("iota_key", [P, HI * WINH], i16, st)
            d_edge = sb("d_edge", [P, 2, SLOTS], i32, st)
            src_bits = sb("src_bits", [P, 2, 2, SLOTS], i32, st)
            lo_f = sb("lo_f", [P, 2, SLOTS], fp32, st)
            key = sb("key", [P, 2, 2, SLOTS], fp32, st)
            hot_lo = sb("hot_lo", [P, 2, 4, P], bf16, st)
            hot_key = sb("hot_key", [P, 2, 4, HI * WINH], bf16, st)
            HSPLIT = [(0, (HI + 1) // 2), ((HI + 1) // 2, HI)]
            ps_cnt = [[psum(f"ps_cnt{h}{k}", [P, b - a, WINH], st) for k, (a, b) in enumerate(HSPLIT)] for h in range(2)]
            dedge_in = [sem(f"dedge_in{u}") for u in range(2)]
            iotas, bits, rel_d, key_r, hot_c = sem("iotas"), sem("bits"), sem("rel_d"), sem("key_r"), sem("hot_c")
            cnt_ps, cnt_fix, cnt_sb = sem("cnt_ps"), sem("cnt_fix"), sem("cnt_sb")

            idx_in = [sem(f"idx_in{u}") for u in range(2)]
            edge_in = [sem(f"edge_in{u}") for u in range(2)]
            drow_in = [sem(f"drow_in{u}") for u in range(2)]
            bwin_in = [sem(f"bwin_in{u}") for u in range(2)]
            gathered = [sem(f"gathered{u}") for u in range(2)]
            tot_out = [sem(f"tot_out{u}") for u in range(2)]
            zt_ps, zt_sb, zt_used = sem("zt_ps"), sem("zt_sb"), sem("zt_used")
            hot_ready, win_used, tail_set = sem("hot_ready"), sem("win_used"), sem("tail_set")
            tot_ps, tot_sb, tot_bn = sem("tot_ps"), sem("tot_sb"), sem("tot_bn")
            LEAD = 4

            def by_half(tile, u):
                return tile[:, u, :].rearrange("p (h s) -> p h s", h=2)

            def groups(eng, group):
                with eng.Fori(0, PAIRS) as i:
                    for u in range(2):
                        group(i, u, 2 * i + u, False)
                group(PAIRS, 0, NFULL, True)

            with nc.Block() as block:
                @block.sync
                def _(sp):
                    def stage(general):
                        def group(i, u, g, tail):
                            e0 = g * GROUP
                            d_cols = TAIL if tail else GROUP
                            if not (isinstance(i, int) and i == 0):
                                sp.wait_ge(gathered[u], 16 * SLOTS * i)
                                settle(sp)
                            if not general:
                                sp.wait_ge(key_r, g + 1)
                                settle(sp)
                            if tail:
                                sp.wait_ge(tail_set, 4)
                            load_by_edge(sp, lambda p, h, q: by_half(idx, u)[p, h, q], src, g, tail, idx_in[u])
                            if not general:
                                load_by_edge(sp, lambda p, h, q: by_half(d_edge, u)[p, h, q], dst, g, tail, dedge_in[u])
                            sp.wait_ge(zt_ps, 2 * g + 2)
                            settle(sp)
                            load_by_edge(sp, lambda p, h, q: Z[:, u, :, F:D].rearrange("p (h q) f -> p h q f", h=2)[p, h, q], edge_attr, g, tail, edge_in[u])
                            sp.wait_ge(tot_ps, 2 * g + 2)
                            settle(sp)
                            sp.dma_start(d_row[:, u, 0:d_cols], dst[ds(e0, d_cols)].unsqueeze(0).to_broadcast([WINB, d_cols])).then_inc(drow_in[u], 16)
                            if general:
                                with sp.Fori(0, NWB) as r:
                                    sp.wait_ge(win_used, g * NWB + r + 1)
                                    settle(sp)
                                    sp.dma_start(B_win[:, 0, :], b_tab[ds(r * WINB, WINB), :]).then_inc(bwin_in[0], 16)
                            else:
                                first = sp.value_load(base_i[0:1, ds(g * 2, 1)], min_val=0, max_val=N - 1)
                                sp.dma_start(B_win[:, u, :], b_tab[ds(first, WINB), :]).then_inc(bwin_in[u], 16)
                        pipelined(sp, [(group, 0)], NFULL)
                    when_fits(sp, stage)

                @block.gpsimd
                def _(pool):
                    def group(i, u, g, tail):
                        pool.wait_ge(zt_ps, 2 * g + 2)
                        pool.wait_ge(idx_in[u], 16 * i + 16 * (TAIL_LOADS if tail else 1))
                        settle(pool)
                        for s in range(SLOTS):
                            pool.indirect_dma_start(Z[:, u, s, 0:F], None, h_tab[:, :],
                                                    bass.IndirectOffsetOnAxis(ap=idx[:, u, s:s + 1], axis=0)).then_inc(gathered[u], 16)
                    nc.gpsimd.iota(iota_lo[:, :], pattern=[[1, P]], base=0, channel_multiplier=0).then_inc(iotas, 1)
                    nc.gpsimd.iota(iota_key[:, :], pattern=[[1, HI * WINH]], base=0, channel_multiplier=0).then_inc(iotas, 1)
                    groups(pool, group)

                @block.vector
                def _(v):
                    v.sem_inc(tot_bn, LEAD)
                    v.sem_inc(key_r, 2)
                    v.wait_ge(iotas, 2)

                    def keys(i, u, g, tail):
                        loads = 16 * (TAIL_LOADS if tail else 1)
                        v.wait_ge(idx_in[u], 16 * i + loads)
                        v.wait_ge(dedge_in[u], 16 * i + loads)
                        nc.vector.tensor_scalar(src_bits[:, u, 0, :], idx[:, u, :], P - 1, None, ALU.bitwise_and)
                        nc.vector.tensor_scalar(src_bits[:, u, 1, :], idx[:, u, :], SHIFT, (1 << 30) - WINH,
                                                ALU.logical_shift_right, ALU.bitwise_and)
                        nc.vector.tensor_tensor(key[:, u, 0, :].rearrange("p (h s) -> p h s", h=2), by_half(d_edge, u),
                                                base_bc[:, ds(g, 1), :].rearrange("p a h -> p (a h)").unsqueeze(2).to_broadcast([P, 2, 4]),
                                                ALU.subtract).then_inc(bits, 1)
                        v.wait_ge(bits, g + 1)
                        nc.vector.tensor_copy(lo_f[:, u, :], src_bits[:, u, 0, :])
                        nc.vector.tensor_tensor(key[:, u, 1, :], key[:, u, 0, :], src_bits[:, u, 1, :], ALU.add).then_inc(key_r, 1)

                    def hots(h):
                        def part(i, u, g, tail):
                            v.wait_ge(key_r, g + 3)
                            v.wait_ge(cnt_ps, 2 * g + h + 1)
                            for s in range(4):
                                nc.vector.tensor_scalar(hot_lo[:, h, s, :], iota_lo[:, :], lo_f[:, u, 4 * h + s:4 * h + s + 1], None, ALU.is_equal)
                                done = nc.vector.tensor_scalar(hot_key[:, h, s, :], iota_key[:, :], key[:, u, 1, 4 * h + s:4 * h + s + 1], None, ALU.is_equal)
                            done.then_inc(hot_c, 1)
                        return part

                    def shared_node(h):
                        def part(i, u, g, tail):
                            first = v.value_load(base_i[0:1, ds(2 * g + h, 1)], min_val=0, max_val=N - 1)
                            v.wait_ge(cnt_ps, 2 * g + h + 3)
                            v.wait_ge(cnt_sb, 2 * g + h + 2)
                            for k, (a0, b0) in enumerate(HSPLIT):
                                column = ps_cnt[h][k][:, :, 0:1]
                                done = nc.vector.tensor_tensor(column, column, count[:, a0:b0, ds(first, 1)], ALU.add)
                            done.then_inc(cnt_fix, 1)
                        return part

                    def statistics(i, u, g, tail):
                        for h in range(2):
                            v.wait_ge(tot_sb, 2 * g + h + 1 + LEAD)
                            half = tot[:, u, h * HALF:(h + 1) * HALF]
                            if tail:
                                half = half.rearrange("f (s p) -> f s p", p=P)
                                for first, last, valid, at in tail_parts[h]:
                                    done = nc.vector.bn_stats(stats[:, at, :], half[:, first:last + 1, 0:valid])
                                done.then_inc(tot_bn, 1)
                            else:
                                nc.vector.bn_stats(stats[:, 2 * g + h, :], half).then_inc(tot_bn, 1)

                    def stage(general):
                        def hot(scalar, u, place):
                            return nc.vector.tensor_scalar(hot_t[:, place, :], d_row[:, u, :], scalar, None, ALU.is_equal)

                        def nodes_at_dst(i, u, g, tail):
                            if tail:
                                v.wait_ge(gathered[u], 16 * SLOTS * i)
                                v.wait_ge(zt_ps, 2 * g + 2)
                                nc.vector.memset(idx[:, u, :], 0).then_inc(tail_set, 1)
                                nc.vector.memset(Z[:, u, :, F:D], 0.0).then_inc(tail_set, 1)
                                nc.vector.memset(d_row[:, u, TAIL:GROUP], -1).then_inc(tail_set, 1)
                                nc.vector.memset(d_edge[:, u, :], -1).then_inc(tail_set, 1)
                                v.wait_ge(tail_set, 4)
                            v.wait_ge(drow_in[u], 16 * i + 16)
                            if general:
                                settle(v)
                                with v.Fori(0, NWB) as r:
                                    v.wait_ge(win_used, g * NWB + r + 1)
                                    hot(win_p[0:WINB, ds(r, 1)], u, 0).then_inc(hot_ready, 1)
                            else:
                                v.wait_ge(tot_ps, 2 * g + 2)
                                hot(base_p[0:WINB, ds(g, 1)], u, u).then_inc(hot_ready, 1)

                        if general:
                            pipelined(v, [(nodes_at_dst, 0), (statistics, 1)], NFULL)
                        else:
                            pipelined(v, [(nodes_at_dst, 0), (statistics, 1), (keys, 0), (shared_node(0), 1), (hots(0), 0),
                                          (shared_node(1), 1), (hots(1), 0)], NFULL)
                    when_fits(v, stage)

                @block.scalar
                def _(a):
                    a.sem_inc(tot_sb, LEAD)
                    for u in range(2):
                        a.sem_inc(tot_out[u], 16)

                    a.sem_inc(cnt_sb, 2)

                    def transposed(i, u, g, tail):
                        for h in range(2):
                            a.wait_ge(zt_ps, 2 * g + h + 1 + LEAD)
                            a.wait_ge(zt_used, 2 * g + h + 1)
                            nc.scalar.activation(ZT[:, h, :], ps_z[h][:, :], ACT.Copy).then_inc(zt_sb, 1)

                    def counts(i, u, g, tail):
                        for h in range(2):
                            first = a.value_load(base_i[0:1, ds(2 * g + h, 1)], min_val=0, max_val=N - 1)
                            a.wait_ge(cnt_fix, 2 * g + h + 1)
                            for k, (a0, b0) in enumerate(HSPLIT):
                                last = nc.scalar.activation(count[:, a0:b0, ds(first, WINH)], ps_cnt[h][k][:, :, :], ACT.Copy)
                            last.then_inc(cnt_sb, 1)

                    def totals(i, u, g, tail):
                        a.wait_ge(tot_out[u], 16 * i + 16)
                        a.wait_ge(tot_bn, 2 * g + 2)
                        for h in range(2):
                            a.wait_ge(tot_ps, 2 * g + h + 1 + LEAD)
                            nc.scalar.activation(tot[:, u, h * HALF:(h + 1) * HALF], ps_tot[h][:, :], ACT.Copy).then_inc(tot_sb, 1)
                        a.wait_ge(tot_sb, 2 * g + 2 + LEAD)
                        a.dma_start(total_d[:, ds(g * GROUP, GROUP)], tot[:, u, :]).then_inc(tot_out[u], 16)

                    def stage(general):
                        pipelined(a, [(transposed, 0), (totals, 0)] if general else
                                  [(transposed, 0), (counts, 1), (totals, 0)], NFULL)
                    when_fits(a, stage)
                    a.wait_ge(tot_out[0], 16 * (PAIRS + 2))
                    a.wait_ge(tot_out[1], 16 * (PAIRS + 1))

                @block.tensor
                def _(pe):
                    pe.sem_inc(zt_ps, LEAD)
                    pe.sem_inc(zt_used, 2)
                    pe.sem_inc(tot_ps, LEAD)
                    pe.sem_inc(win_used, 1)
                    pe.sem_inc(cnt_ps, 2)

                    def stage(general):
                        def rows_at_dst(u, place, h, stop):
                            edges = hot_t[:, place, h * HALF:(h + 1) * HALF].rearrange("w (p s) -> w s p", s=4)
                            return nc.tensor.matmul(ps_tot[h][:, :], B_win[:, place, :], edges, start=False, stop=stop)

                        def group(i, u, g, tail):
                            pe.wait_ge(gathered[u], 16 * SLOTS * i + 16 * SLOTS)
                            pe.wait_ge(edge_in[u], 32 * i + (16 * TAIL_LOADS if tail else 32))
                            for h in range(2):
                                for s in range(4):
                                    last = nc.tensor.transpose(ps_z[h][:, s * P:(s + 1) * P], Z[:, u, 4 * h + s, :], ident[:, :])
                                last.then_inc(zt_ps, 1)
                            for h in range(2):
                                pe.wait_ge(zt_sb, 2 * g + h + 1)
                                pe.wait_ge(tot_sb, 2 * g + h - 1 + LEAD)
                                nc.tensor.matmul(ps_tot[h][:, :], w_edge[:, :], ZT[:, h, :], start=True, stop=False).then_inc(zt_used, 1)
                            if general:
                                def window(r, stop):
                                    pe.wait_ge(hot_ready, g * NWB + r + 1)
                                    pe.wait_ge(bwin_in[0], 16 * (g * NWB + r) + 16)
                                    rows_at_dst(u, 0, 0, stop)
                                    rows_at_dst(u, 0, 1, stop).then_inc(win_used, 1)

                                settle(pe)
                                with pe.Fori(0, NWB - 1) as r:
                                    window(r, False)
                                window(NWB - 1, True)
                                pe.wait_ge(win_used, g * NWB + NWB + 1)
                                pe.sem_inc(tot_ps, 2)
                            else:
                                pe.wait_ge(hot_ready, g + 1)
                                pe.wait_ge(bwin_in[u], 16 * i + 16)
                                for h in range(2):
                                    rows_at_dst(u, u, h, True).then_inc(tot_ps, 1)
                            if not general:
                                for h in range(2):
                                    pe.wait_ge(hot_c, 2 * g + h + 1)
                                    pe.wait_ge(cnt_sb, 2 * g + h + 1)
                                    for k, (a0, b0) in enumerate(HSPLIT):
                                        for s in range(4):
                                            last = nc.tensor.matmul(ps_cnt[h][k][:, :, :], hot_lo[:, h, s, :],
                                                                    hot_key[:, h, s, a0 * WINH:b0 * WINH], start=(s == 0), stop=(s == 3))
                                    last.then_inc(cnt_ps, 1)
                        groups(pe, group)
                    when_fits(pe, stage)

        filt, core = sb("filt", [P, 3]), sb("core", [P, 3])
        with ExitStack() as st:
            mv = sb("mv", [D, 2], fp32, st)
            gb = sb("gb", [D, 2], fp32, st)
            tmp = sb("tmp", [D, 4], fp32, st)
            aff = sb("aff", [D, 3], fp32, st)
            gb_in, bn, rt, aff_out, aff_in = sem("gb_in"), sem("bn"), sem("rt"), sem("aff_out"), sem("aff_in")
            with nc.Block() as block:
                @block.sync
                def _(sp):
                    sp.dma_start(gb[:, 0:1], bn1_g.rearrange("(f a) -> f a", a=1)).then_inc(gb_in, 16)
                    sp.dma_start(gb[:, 1:2], bn1_b.rearrange("(f a) -> f a", a=1)).then_inc(gb_in, 16)
                    sp.wait_ge(bn, 8)
                    sp.dma_start(affine_d[:, :], aff[:, :]).then_inc(aff_out, 16)
                    sp.wait_ge(aff_out, 16)
                    for k in range(2):
                        sp.dma_start(filt[k * F:(k + 1) * F, :], affine_d[0:F, :]).then_inc(aff_in, 16)
                        sp.dma_start(core[k * F:(k + 1) * F, :], affine_d[F:D, :]).then_inc(aff_in, 16)
                    sp.wait_ge(aff_in, 64)

                @block.vector
                def _(v):
                    def step(n, ins):
                        ins.then_inc(bn, 1)
                        v.wait_ge(bn, n)

                    step(1, nc.vector.bn_aggr(mv[:, :], stats[:, :, :].rearrange("f k s -> f (k s)")))
                    step(2, nc.vector.tensor_scalar(tmp[:, 0:1], mv[:, 1:2], EPS, None, ALU.add))
                    v.wait_ge(rt, 1)
                    step(3, nc.vector.reciprocal(tmp[:, 2:3], tmp[:, 1:2]))
                    v.wait_ge(gb_in, 32)
                    step(4, nc.vector.tensor_tensor(aff[:, 0:1], tmp[:, 2:3], gb[:, 0:1], ALU.mult))
                    step(5, nc.vector.tensor_tensor(tmp[:, 3:4], mv[:, 0:1], aff[:, 0:1], ALU.mult))
                    step(6, nc.vector.tensor_tensor(aff[:, 1:2], gb[:, 1:2], tmp[:, 3:4], ALU.subtract))
                    step(7, nc.vector.tensor_scalar(aff[0:F, 0:2], aff[0:F, 0:2], -1.0, None, ALU.mult))
                    step(8, nc.vector.tensor_scalar(aff[:, 2:3], aff[:, 1:2], -1.0, CAP, ALU.mult, ALU.add))

                @block.scalar
                def _(a):
                    a.wait_ge(bn, 2)
                    nc.scalar.activation(tmp[:, 1:2], tmp[:, 0:1], ACT.Sqrt).then_inc(rt, 1)

        class WindowSums:

            def __init__(self, name, st, into, rows):
                self.into, self.rows = into, rows
                self.d_e = sb(name + "_d_e", [P, 2, SLOTS], i32, st)
                self.rel = sb(name + "_rel", [P, 2, SLOTS], fp32, st)
                self.hot = sb(name + "_hot", [P, 2, SLOTS, WIN], fp32, st)
                self.ps = [psum(f"{name}_ps{u}", [rows, WIN], st) for u in range(2)]
                self.d_in = [sem(f"{name}_d_in{u}") for u in range(2)]
                self.d_set, self.d_used = sem(name + "_d_set"), sem(name + "_d_used")
                self.rel_ready, self.hot_ready = sem(name + "_rel_ready"), sem(name + "_hot_ready")
                self.summed, self.added = sem(name + "_summed"), sem(name + "_added")

            def start_vector(self, v):
                v.sem_inc(self.d_used, 2)
                v.sem_inc(self.added, 2)

            def start_tensor(self, pe):
                pe.sem_inc(self.summed, 2)

            def load_dst(self, sp, u, g, tail):
                e0 = g * GROUP
                sp.wait_ge(self.d_used, g + 1)
                settle(sp)
                if tail:
                    sp.wait_ge(self.d_set, 1)
                load_by_edge(sp, lambda p, h, q: by_half(self.d_e, u)[p, h, q], dst, g, tail, self.d_in[u])

            def one_hot(self, v, u, place, base, count):
                nc.vector.tensor_scalar(self.rel[:, place, :], self.d_e[:, u, :], base, None, ALU.subtract).then_inc(self.rel_ready, 1)
                v.wait_ge(self.rel_ready, count + 1)
                return nc.vector.tensor_tensor(self.hot[:, place, :, :],
                                               iota_w[:, :].unsqueeze(1).to_broadcast([P, SLOTS, WIN]),
                                               self.rel[:, place, :].unsqueeze(2).to_broadcast([P, SLOTS, WIN]),
                                               ALU.is_equal)

            def dst_arrived(self, v, i, u, g, tail):
                if tail:
                    v.wait_ge(self.d_used, g + 1)
                    nc.vector.memset(self.d_e[:, u, :], -1).then_inc(self.d_set, 1)
                v.wait_ge(self.d_in[u], 16 * i + 16 * (TAIL_LOADS if tail else 1))

            def hots_fit(self, v, i, u, g, tail):
                self.dst_arrived(v, i, u, g, tail)
                v.wait_ge(self.summed, g + 1)
                self.one_hot(v, u, u, base_bc[:, ds(g, 1), 0], g).then_inc(self.hot_ready, 1)
                v.sem_inc(self.d_used, 1)

            def adds_fit(self, v, u, g):
                first = v.value_load(base_i[0:1, ds(2 * g, 1)], min_val=0, max_val=N - 1)
                v.wait_ge(self.summed, g + 3)
                v.wait_ge(self.added, g + 2)
                window = self.into[0:self.rows, ds(first, WIN)]
                nc.vector.tensor_tensor(window, window, self.ps[u][:, :], ALU.add).then_inc(self.added, 1)

            def all_windows(self, v, i, u, g, tail):
                self.dst_arrived(v, i, u, g, tail)
                settle(v)
                with v.Fori(0, NW) as r:
                    k = g * NW + r
                    v.wait_ge(self.added, k + 2)
                    self.one_hot(v, u, 0, win_c[:, ds(r, 1)], k).then_inc(self.hot_ready, 1)
                    v.wait_ge(self.summed, k + 3)
                    window = self.into[0:self.rows, ds(r * WIN, WIN)]
                    nc.vector.tensor_tensor(window, window, self.ps[0][:, :], ALU.add).then_inc(self.added, 1)
                v.sem_inc(self.d_used, 1)

            def products(self, pe, general, lhs, g, u):
                def tiles(place):
                    for s in range(SLOTS):
                        last = nc.tensor.matmul(self.ps[place][:, :], lhs(s), self.hot[:, place, s, :],
                                                start=(s == 0), stop=(s == SLOTS - 1))
                    return last

                if general:
                    settle(pe)
                    with pe.Fori(0, NW) as r:
                        pe.wait_ge(self.hot_ready, g * NW + r + 1)
                        pe.wait_ge(self.added, g * NW + r + 2)
                        tiles(0).then_inc(self.summed, 1)
                else:
                    pe.wait_ge(self.hot_ready, g + 1)
                    pe.wait_ge(self.added, g + 1)
                    tiles(u).then_inc(self.summed, 1)

        with ExitStack() as st:
            W2 = [P, 2, 2, HALF]
            Ft, Ct = sb("Ft", W2, fp32, st), sb("Ct", W2, fp32, st)
            low_f, low_c = sb("low_f", W2, fp32, st), sb("low_c", W2, fp32, st)
            y = sb("y", W2, fp32, st)
            sig, soft = sb("sig", W2, fp32, st), sb("soft", W2, fp32, st)
            msg_t = sb("msg_t", W2, fp32, st)
            msg = sb("msg", [P, 2, SLOTS, F + 1], fp32, st)
            ps_m = [psum(f"ps_m{u}", [P, 4, P], st) for u in range(2)]
            sums = WindowSums("b", st, agg, F + 1)

            total_in = [sem(f"total_in{b}") for b in range(2)]
            low_f_r, low_c_r, y_r = sem("low_f_r"), sem("low_c_r"), sem("y_r")
            exp_f, exp_c, ln_f, ln_c = sem("exp_f"), sem("exp_c"), sem("ln_f"), sem("ln_c")
            sig_r, soft_r, msg_t_r = sem("sig_r"), sem("soft_r"), sem("msg_t_r")
            msg_ps, msg_sb, ones_set = sem("msg_ps"), sem("msg_sb"), sem("ones_set")


            with nc.Block() as block:
                @block.sync
                def _(sp):
                    def load(n, b, k, last):
                        nu = 1 if last else 2
                        sp.wait_ge(y_r, k + 1)
                        sp.wait_ge(low_c_r, k + 1)
                        settle(sp)
                        for tile, f0 in ((Ft, 0), (Ct, F)):
                            for h in range(2):
                                from_ = total_d[f0:f0 + F, ds(k * (2 * GROUP), nu * GROUP)].rearrange("f (u h e) -> f h u e", u=nu, h=2)
                                sp.dma_start(tile[h * F:(h + 1) * F, b, 0:nu, :], from_[:, h, :, :]).then_inc(total_in[b], 16)

                    def load_dst(n, b, k, last):
                        nu = 1 if last else 2
                        for u in range(nu):
                            sums.load_dst(sp, u, 2 * k + u, last)
                    pipelined(sp, [(load, 0), (load_dst, 2)], PAIRS)

                @block.vector
                def _(v):
                    v.sem_inc(low_c_r, 2)
                    v.sem_inc(soft_r, 2)
                    sums.start_vector(v)

                    def stage(general):
                        def affine(n, b, k, last):
                            nu = 1 if last else 2
                            v.wait_ge(total_in[b], 64 * n + 64)
                            v.wait_ge(exp_c, k + 1)
                            nc.vector.tensor_scalar(low_f[:, b, 0:nu, :], Ft[:, b, 0:nu, :], filt[:, 0:1], filt[:, 2:3],
                                                    ALU.mult, ALU.min).then_inc(low_f_r, 1)
                            nc.vector.tensor_scalar(low_c[:, b, 0:nu, :], Ct[:, b, 0:nu, :], core[:, 0:1], core[:, 2:3],
                                                    ALU.mult, ALU.min).then_inc(low_c_r, 1)

                        def hots(n, b, k, last):
                            nu = 1 if last else 2
                            if not general:
                                for u in range(nu):
                                    sums.hots_fit(v, k, u, 2 * k + u, last)

                        def softplus(n, b, k, last):
                            nu = 1 if last else 2
                            v.wait_ge(ln_c, k + 1)
                            v.wait_ge(y_r, k + 3)
                            nc.vector.tensor_tensor(soft[:, b, 0:nu, :], y[:, b, 0:nu, :], soft[:, b, 0:nu, :],
                                                    ALU.max).then_inc(soft_r, 1)

                        def add(n, b, k, last):
                            nu = 1 if last else 2
                            for u in range(nu):
                                if general:
                                    sums.all_windows(v, k, u, 2 * k + u, last)
                                else:
                                    sums.adds_fit(v, u, 2 * k + u)
                        pipelined(v, [(softplus, 2), (affine, 0), (add, 3), (hots, 2)], PAIRS)
                    when_fits(v, stage)

                @block.scalar
                def _(a):
                    a.preload_act_table_set("natural_log_exp_and_others")
                    a.sem_inc(exp_c, 2)
                    a.sem_inc(msg_sb, 2)

                    def functions(n, b, k, last):
                        nu = 1 if last else 2
                        at = (slice(None), b, slice(0, nu), slice(None))
                        a.wait_ge(low_f_r, k + 1)
                        a.wait_ge(msg_t_r, k + 1)
                        nc.scalar.activation(sig[at], low_f[at], ACT.Exp, bias=filt[:, 1:2]).then_inc(exp_f, 1)
                        a.wait_ge(low_c_r, k + 3)
                        nc.scalar.activation(soft[at], low_c[at], ACT.Exp, bias=core[:, 1:2]).then_inc(exp_c, 1)
                        a.wait_ge(exp_f, k + 1)
                        nc.scalar.activation(sig[at], sig[at], ACT.Ln, bias=1.0).then_inc(ln_f, 1)
                        a.wait_ge(exp_c, k + 3)
                        nc.scalar.activation(soft[at], soft[at], ACT.Ln, bias=1.0).then_inc(ln_c, 1)
                        a.wait_ge(ln_f, k + 1)
                        nc.scalar.activation(sig[at], sig[at], ACT.Exp, scale=-1.0).then_inc(sig_r, 1)

                    def by_edge(n, b, k, last):
                        nu = 1 if last else 2
                        for u in range(nu):
                            a.wait_ge(msg_ps, 2 * k + u + 5)
                            nc.scalar.activation(msg[:, u, :, 0:F].rearrange("p (h c) f -> p c h f", h=2),
                                                 ps_m[u][:, :, :].rearrange("p c (h f) -> p c h f", h=2), ACT.Copy).then_inc(msg_sb, 1)
                    pipelined(a, [(functions, 0), (by_edge, 1)], PAIRS)

                @block.gpsimd
                def _(pool):
                    pool.sem_inc(msg_t_r, 2)
                    pool.sem_inc(y_r, 2)
                    nc.gpsimd.memset(msg[:, :, :, F:F + 1], 1.0).then_inc(ones_set, 1)

                    def core_affine(n, b, k, last):
                        nu = 1 if last else 2
                        pool.wait_ge(total_in[b], 64 * n + 64)
                        pool.wait_ge(soft_r, k + 1)
                        settle(pool)
                        nc.gpsimd.tensor_scalar(y[:, b, 0:nu, :], Ct[:, b, 0:nu, :], core[:, 0:1], core[:, 1:2],
                                                ALU.mult, ALU.add).then_inc(y_r, 1)

                    def multiply(n, b, k, last):
                        nu = 1 if last else 2
                        at = (slice(None), b, slice(0, nu), slice(None))
                        pool.wait_ge(sig_r, k + 1)
                        pool.wait_ge(soft_r, k + 3)
                        pool.wait_ge(msg_ps, 2 * k + 2)
                        nc.gpsimd.tensor_tensor(msg_t[at], sig[at], soft[at], ALU.mult).then_inc(msg_t_r, 1)
                    pipelined(pool, [(core_affine, 0), (multiply, 1)], PAIRS)

                @block.tensor
                def _(pe):
                    pe.sem_inc(msg_ps, 4)
                    sums.start_tensor(pe)

                    def stage(general):
                        pe.wait_ge(ones_set, 1)

                        def pair(n, b, k, last):
                            nu = 1 if last else 2
                            pe.wait_ge(msg_t_r, k + 3)
                            for u in range(nu):
                                pe.wait_ge(msg_sb, 2 * k + u + 1)
                                for c in range(4):
                                    done = nc.tensor.transpose(ps_m[u][:, c, :], msg_t[:, b, u, c * P:(c + 1) * P], ident[:, :])
                                done.then_inc(msg_ps, 1)
                            for u in range(nu):
                                pe.wait_ge(msg_sb, 2 * k + u + 3)
                                sums.products(pe, general, lambda s: msg[:, u, s, :], 2 * k + u, u)
                        pipelined(pe, [(pair, 0)], PAIRS)
                    when_fits(pe, stage)

        dis = sb("dis", [NP, NT])
        out_b = sb("out_b", [NP, NT, F])
        agg2, agg2_l = sb("agg2", [2 * F, N + WIN]), sb("agg2_l", [F, N])
        zeros2 = sem("zeros2")
        with ExitStack() as st:
            U = sb("U", [F + 1, N], fp32, st)
            V = sb("V", [NP, NT, F + 1], fp32, st)
            T1, T2 = sb("T1", [NP, NT, F], fp32, st), sb("T2", [NP, NT, F], fp32, st)
            X1 = sb("X1", [NP, NT, F], fp32, st)
            nrow = sb("nrow", [NP, 6, NT], fp32, st)
            ab = sb("ab", [F + 1, 2], fp32, st)
            mv2 = sb("mv2", [F, 6], fp32, st)
            gb2 = sb("gb2", [F, 2], fp32, st)
            deg_max, few = sb("deg_max", [F + 1, 2], fp32, st), sb("few", [1, 1], i32, st)
            b1_bc = sb("b1_bc", [NP, F], fp32, st)
            NSTAT = -(-N // 512)
            cuts = [N * k // NSTAT for k in range(NSTAT + 1)]
            stats2 = sb("stats2", [F, NSTAT, 6], fp32, st)
            ps_v = [psum(f"ps_v{k}", [NP, 7, F + 1], st) for k in range(4)]
            vchunks = [(c, min(7, NT - 7 * c)) for c in range(-(-NT // 7))]
            assert len(vchunks) <= 4
            p_in, nd, na, v_ps, v_sb, g_out, g_ready = (sem(n) for n in ("p_in", "nd", "na", "v_ps", "v_sb", "g_out", "g_ready"))

            with nc.Block() as block:
                @block.sync
                def _(sp):
                    sp.dma_start(gb2[:, 0:1], bn2_g.rearrange("(f a) -> f a", a=1)).then_inc(p_in, 16)
                    sp.dma_start(gb2[:, 1:2], bn2_b.rearrange("(f a) -> f a", a=1)).then_inc(p_in, 16)
                    sp.dma_start(b1_bc[:, :], b1.unsqueeze(0).to_broadcast([NP, F])).then_inc(p_in, 16)
                    sp.wait_ge(g_ready, 1)
                    sp.dma_start(g_tab.rearrange("(p t) f -> p t f", t=NT), T2[:, :, :]).then_inc(g_out, 16)
                    sp.wait_ge(g_out, 16)

                @block.gpsimd
                def _(pool):
                    nc.gpsimd.memset(agg2[:, :], 0.0).then_inc(zeros2, 1)
                    nc.gpsimd.memset(agg2_l[:, :], 0.0).then_inc(zeros2, 1)
                    pool.wait_ge(zeros2, 2)

                @block.vector
                def _(v):
                    done = [0]

                    def step(ins):
                        done[0] += 1
                        ins.then_inc(nd, 1)
                        v.wait_ge(nd, done[0])

                    def per_node(k):
                        return nrow[:, k, :].unsqueeze(2).to_broadcast([NP, NT, F])

                    step(nc.vector.reduce_max(deg_max[F:F + 1, 0:1], agg[F:F + 1, 0:N], axis=AX.X))
                    step(nc.vector.tensor_scalar(deg_max[F:F + 1, 1:2], deg_max[F:F + 1, 0:1], 255.5, None, ALU.is_lt))
                    step(nc.vector.tensor_copy(few[:, :], deg_max[F:F + 1, 1:2]))
                    step(nc.vector.tensor_tensor(counted_i[:, :], few[:, :], fits_i[:, :], ALU.mult))
                    step(nc.vector.memset(ab[:, 0:1], 1.0))
                    step(nc.vector.memset(ab[:, 1:2], 0.0))
                    for k in range(NSTAT):
                        last = nc.vector.bn_stats(stats2[:, k, :], agg[0:F, cuts[k]:cuts[k + 1]])
                    step(last)
                    step(nc.vector.bn_aggr(mv2[:, 0:2], stats2[:, :, :].rearrange("f k s -> f (k s)")))
                    step(nc.vector.tensor_scalar(mv2[:, 2:3], mv2[:, 1:2], EPS, None, ALU.add))
                    v.wait_ge(na, 1)
                    step(nc.vector.reciprocal(mv2[:, 4:5], mv2[:, 3:4]))
                    v.wait_ge(p_in, 48)
                    step(nc.vector.tensor_tensor(ab[0:F, 0:1], mv2[:, 4:5], gb2[:, 0:1], ALU.mult))
                    step(nc.vector.tensor_tensor(mv2[:, 5:6], mv2[:, 0:1], ab[0:F, 0:1], ALU.mult))
                    step(nc.vector.tensor_tensor(ab[0:F, 1:2], gb2[:, 1:2], mv2[:, 5:6], ALU.subtract))
                    step(nc.vector.tensor_scalar(U[:, :], agg[:, 0:N], ab[:, 0:1], ab[:, 1:2], ALU.mult, ALU.add))
                    v.wait_ge(v_sb, len(vchunks))
                    step(nc.vector.tensor_tensor(T1[:, :, :], V[:, :, 0:F], H[:, :, :], ALU.add))
                    step(nc.vector.tensor_scalar(T2[:, :, :], T1[:, :, :], CAP, None, ALU.min))
                    step(nc.vector.tensor_scalar(nrow[:, 0, :], V[:, :, F], 1.0, None, ALU.max))
                    step(nc.vector.tensor_scalar(nrow[:, 1, :], V[:, :, F], 0.5, None, ALU.is_gt))
                    v.wait_ge(na, 3)
                    step(nc.vector.tensor_tensor(T1[:, :, :], T1[:, :, :], T2[:, :, :], ALU.max))
                    step(nc.vector.tensor_tensor(X1[:, :, :], X[:, :, :], T1[:, :, :], ALU.add))
                    v.wait_ge(na, 4)
                    step(nc.vector.reciprocal(nrow[:, 3, :], nrow[:, 2, :]))
                    step(nc.vector.tensor_tensor(dis[:, :], nrow[:, 3, :], nrow[:, 1, :], ALU.mult))
                    step(nc.vector.reduce_sum(nrow[:, 0, :], X1[:, :, :], axis=AX.X))
                    step(nc.vector.tensor_scalar(nrow[:, 1, :], nrow[:, 0, :], 1.0 / F, None, ALU.mult))
                    step(nc.vector.tensor_tensor(T1[:, :, :], X1[:, :, :], per_node(1), ALU.subtract))
                    step(nc.vector.tensor_tensor(T2[:, :, :], T1[:, :, :], T1[:, :, :], ALU.mult))
                    step(nc.vector.reduce_sum(nrow[:, 0, :], T2[:, :, :], axis=AX.X))
                    step(nc.vector.tensor_scalar(nrow[:, 3, :], nrow[:, 0, :], 1.0 / F, EPS, ALU.mult, ALU.add))
                    v.wait_ge(na, 5)
                    step(nc.vector.reciprocal(nrow[:, 5, :], nrow[:, 4, :]))
                    step(nc.vector.tensor_tensor(T2[:, :, :], T1[:, :, :], per_node(5), ALU.mult))
                    step(nc.vector.tensor_scalar(T1[:, :, :], T2[:, :, :], 0.0, None, ALU.max))
                    nc.vector.tensor_tensor(T2[:, :, :], T1[:, :, :], dis[:, :].unsqueeze(2).to_broadcast([NP, NT, F]),
                                            ALU.mult).then_inc(g_ready, 1)
                    nc.vector.tensor_tensor(out_b[:, :, :], X1[:, :, :], b1_bc[:, :].unsqueeze(1).to_broadcast([NP, NT, F]),
                                            ALU.add)

                @block.scalar
                def _(a):
                    a.wait_ge(nd, 9)
                    nc.scalar.activation(mv2[:, 3:4], mv2[:, 2:3], ACT.Sqrt).then_inc(na, 1)
                    for c, k in vchunks:
                        a.wait_ge(v_ps, c + 1)
                        nc.scalar.activation(V[:, 7 * c:7 * c + k, :], ps_v[c][:, 0:k, :], ACT.Copy).then_inc(v_sb, 1)
                    a.preload_act_table_set("natural_log_exp_and_others")
                    a.wait_ge(nd, 16)
                    nc.scalar.activation(T2[:, :, :], T2[:, :, :], ACT.Exp).then_inc(na, 1)
                    a.wait_ge(na, 2)
                    nc.scalar.activation(T2[:, :, :], T2[:, :, :], ACT.Ln, bias=1.0).then_inc(na, 1)
                    a.wait_ge(nd, 17)
                    nc.scalar.activation(nrow[:, 2, :], nrow[:, 0, :], ACT.Sqrt).then_inc(na, 1)
                    a.wait_ge(nd, 28)
                    nc.scalar.activation(nrow[:, 4, :], nrow[:, 3, :], ACT.Sqrt).then_inc(na, 1)

                @block.tensor
                def _(pe):
                    pe.wait_ge(nd, 14)
                    nodes = U[:, :].rearrange("f (p t) -> f t p", t=NT)
                    for c, k in vchunks:
                        for t in range(k):
                            last = nc.tensor.transpose(ps_v[c][:, t, :], nodes[:, 7 * c + t, :], ident[0:F + 1, 0:F + 1])
                        last.then_inc(v_ps, 1)

        with ExitStack() as st:
            idx2 = sb("idx2", [P, 2, SLOTS], i32, st)
            R = sb("R", [P, 2, SLOTS, F], fp32, st)
            sums = WindowSums("c", st, agg2, F)
            G = sb("G", [P, HI, F], fp32, st)
            G_hm = sb("G_hm", [P, HI, 2, F], bf16, st)
            G_l = sb("G_l", [P, HI, F], bf16, st)
            G_r = sb("G_r", [P, HI, F], fp32, st)
            NCHUNK = 10
            CHUNK = -(-N // NCHUNK)
            dchunks = [(c, c * CHUNK, min(CHUNK, N - c * CHUNK)) for c in range(NCHUNK)]
            cnt_b = sb("cnt_b", [P, 2, HI, CHUNK], bf16, st)
            ps_hm = [psum(f"ps_hm{k}", [P, CHUNK], st) for k in range(2)]
            ps_l = [psum(f"ps_l{k}", [F, CHUNK], st) for k in range(2)]
            g_in, g_zero, split, split_done = sem("g_in"), sem("g_zero"), sem("split"), sem("split_done")
            cvt_v, cvt_a, prod, prod_sb = sem("cvt_v"), sem("cvt_a"), sem("prod"), sem("prod_sb")
            idx2_in = [sem(f"idx2_in{u}") for u in range(2)]
            rows_in = [sem(f"rows_in{u}") for u in range(2)]
            rows_used, idx2_set = sem("rows_used"), sem("idx2_set")

            with nc.Block() as block:
                @block.sync
                def _(sp):
                    def stage(general):
                        if not general:
                            whole = N // P
                            sp.dma_start(G[:, 0:whole, :], g_tab[0:whole * P, :].rearrange("(t p) f -> p t f", p=P)).then_inc(g_in, 16)
                            sp.wait_ge(g_zero, 1)
                            if N % P:
                                sp.dma_start(G[0:N % P, whole, :], g_tab[whole * P:N, :]).then_inc(g_in, 16)
                            return

                        def group(i, u, g, tail):
                            sp.wait_ge(rows_used, g + 1)
                            settle(sp)
                            if tail:
                                sp.wait_ge(idx2_set, 1)
                            load_by_edge(sp, lambda p, h, q: by_half(idx2, u)[p, h, q], src, g, tail, idx2_in[u])
                            sums.load_dst(sp, u, g, tail)
                        groups(sp, group)
                    when_fits(sp, stage, counted_i)

                @block.gpsimd
                def _(pool):
                    def stage(general):
                        if not general:
                            settle(pool)
                            return

                        def group(i, u, g, tail):
                            pool.wait_ge(idx2_in[u], 16 * i + 16 * (TAIL_LOADS if tail else 1))
                            settle(pool)
                            for s in range(SLOTS):
                                pool.indirect_dma_start(R[:, u, s, :], None, g_tab[:, :],
                                                        bass.IndirectOffsetOnAxis(ap=idx2[:, u, s:s + 1], axis=0)).then_inc(rows_in[u], 16)
                        groups(pool, group)
                    when_fits(pool, stage, counted_i)

                T_V = 15

                @block.vector
                def _(v):
                    sums.start_vector(v)

                    def by_product():
                        nc.vector.memset(G[:, N // P:HI, :], 0.0).then_inc(g_zero, 1)
                        v.wait_ge(g_in, 32 if N % P else 16)
                        nc.vector.tensor_copy(G_hm[:, :, 0, :], G[:, :, :]).then_inc(split, 1)
                        v.wait_ge(split, 1)
                        nc.vector.tensor_tensor(G_r[:, :, :], G[:, :, :], G_hm[:, :, 0, :], ALU.subtract).then_inc(split, 1)
                        v.wait_ge(split, 2)
                        nc.vector.tensor_copy(G_hm[:, :, 1, :], G_r[:, :, :]).then_inc(split, 1)
                        v.wait_ge(split, 3)
                        nc.vector.tensor_tensor(G_l[:, :, :], G_r[:, :, :], G_hm[:, :, 1, :], ALU.subtract).then_inc(split_done, 1)
                        for c, d0, n in dchunks:
                            if c >= 2:
                                v.wait_ge(prod, 2 * c - 2)
                            nc.vector.tensor_copy(cnt_b[:, c % 2, 0:T_V, 0:n], count[:, 0:T_V, d0:d0 + n]).then_inc(cvt_v, 1)

                    def stage(general):
                        if not general:
                            by_product()
                            return

                        def group(i, u, g, tail):
                            if tail:
                                v.wait_ge(rows_used, g + 1)
                                nc.vector.memset(idx2[:, u, :], 0).then_inc(idx2_set, 1)
                            sums.all_windows(v, i, u, g, tail)
                        groups(v, group)
                    when_fits(v, stage, counted_i)

                @block.scalar
                def _(a):
                    def stage(general):
                        if general:
                            settle(a)
                            return

                        def convert(c, d0, n):
                            if c >= 2:
                                a.wait_ge(prod, 2 * c - 2)
                            nc.scalar.activation(cnt_b[:, c % 2, T_V:HI, 0:n], count[:, T_V:HI, d0:d0 + n], ACT.Copy).then_inc(cvt_a, 1)

                        def take(c, d0, n):
                            a.wait_ge(prod, 2 * c + 1)
                            nc.scalar.activation(agg2[:, d0:d0 + n], ps_hm[c % 2][:, 0:n], ACT.Copy).then_inc(prod_sb, 1)
                            a.wait_ge(prod, 2 * c + 2)
                            nc.scalar.activation(agg2_l[:, d0:d0 + n], ps_l[c % 2][:, 0:n], ACT.Copy).then_inc(prod_sb, 1)

                        for k in range(len(dchunks) + 1):
                            if k < len(dchunks):
                                convert(*dchunks[k])
                            if k >= 1:
                                take(*dchunks[k - 1])
                    when_fits(a, stage, counted_i)

                @block.tensor
                def _(pe):
                    pe.sem_inc(rows_used, 2)
                    sums.start_tensor(pe)

                    def stage(general):
                        if not general:
                            pe.wait_ge(split_done, 1)
                            for c, d0, n in dchunks:
                                pe.wait_ge(cvt_v, c + 1)
                                pe.wait_ge(cvt_a, c + 1)
                                if c >= 2:
                                    pe.wait_ge(prod_sb, 2 * c - 2)
                                for t in range(HI):
                                    last = nc.tensor.matmul(ps_hm[c % 2][:, 0:n], G_hm[:, t, :, :].rearrange("p k f -> p (k f)"),
                                                            cnt_b[:, c % 2, t, 0:n], start=(t == 0), stop=(t == HI - 1))
                                last.then_inc(prod, 1)
                                for t in range(HI):
                                    last = nc.tensor.matmul(ps_l[c % 2][:, 0:n], G_l[:, t, :],
                                                            cnt_b[:, c % 2, t, 0:n], start=(t == 0), stop=(t == HI - 1))
                                last.then_inc(prod, 1)
                            return

                        def group(i, u, g, tail):
                            pe.wait_ge(rows_in[u], 16 * SLOTS * i + 16 * SLOTS)
                            sums.products(pe, general, lambda s: R[:, u, s, :], g, u)
                            pe.wait_ge(sums.summed, (g + 1) * NW + 2)
                            pe.sem_inc(rows_used, 1)
                        groups(pe, group)
                    when_fits(pe, stage, counted_i)

        with ExitStack() as st:
            W1 = sb("W1", [2 * F, F], fp32, st)
            O = sb("O", [NP, NT, F], fp32, st)
            ps_o = [psum(f"ps_o{k}", [NP, 8, F], st) for k in range(4)]
            ochunks = [(c, min(8, NT - 8 * c)) for c in range(-(-NT // 8))]
            assert len(ochunks) <= 4
            w1_in, o_ps, o_mul, o_sb, stored = (sem(n) for n in ("w1_in", "o_ps", "o_mul", "o_sb", "stored"))

            with nc.Block() as block:
                @block.sync
                def _(sp):
                    for k in range(2):
                        sp.dma_start(W1[k * F:(k + 1) * F, :], w1[:, :]).then_inc(w1_in, 16)
                    sp.wait_ge(o_sb, len(ochunks))
                    sp.dma_start(out.rearrange("(p t) f -> p t f", t=NT), O[:, :, :]).then_inc(stored, 16)
                    sp.wait_ge(stored, 16)

                @block.vector
                def _(v):
                    for c, k in ochunks:
                        at = (slice(None), slice(8 * c, 8 * c + k), slice(None))
                        v.wait_ge(o_ps, c + 1)
                        nc.vector.tensor_tensor(O[at], ps_o[c][:, 0:k, :],
                                                dis[:, 8 * c:8 * c + k].unsqueeze(2).to_broadcast([NP, k, F]), ALU.mult).then_inc(o_mul, 1)
                        v.wait_ge(o_mul, c + 1)
                        nc.vector.tensor_tensor(O[at], O[at], out_b[at], ALU.add).then_inc(o_sb, 1)

                @block.tensor
                def _(pe):
                    pe.wait_ge(w1_in, 32)
                    nodes = agg2[:, 0:N].rearrange("f (p t) -> f t p", t=NT)
                    nodes_l = agg2_l[:, :].rearrange("f (p t) -> f t p", t=NT)
                    for c, k in ochunks:
                        for t in range(k):
                            nc.tensor.matmul(ps_o[c][:, t, :], nodes[:, 8 * c + t, :], W1[:, :], start=True, stop=False)
                            last = nc.tensor.matmul(ps_o[c][:, t, :], nodes_l[:, 8 * c + t, :], W1[0:F, :], start=False, stop=True)
                        last.then_inc(o_ps, 1)


INPUTS = ["x", "src", "dst", "edge_attr_64", "L0_gnn_W_full", "L0_gnn_b_full", "L0_gnn_bn1_g", "L0_gnn_bn1_b",
          "L0_gnn_bn2_g", "L0_gnn_bn2_b", "L1_gnn_W", "L1_gnn_b"]


def kernel(**inputs):
    import concourse.bacc as bacc
    from concourse.bass_utils import run_bass_kernel_spmd as run

    nc = bacc.Bacc("TRN2", target_bir_lowering=False, num_devices=1)
    arrays = {"in_" + k: np.ascontiguousarray(inputs[k]) for k in INPUTS}
    args = [nc.dram_tensor(k, v.shape, mybir.dt.from_np(v.dtype), kind="ExternalInput").ap() for k, v in arrays.items()]
    result = nc.dram_tensor("out_0", inputs["x"].shape, mybir.dt.float32, kind="ExternalOutput").ap()
    build_gnn(nc, *args, result)
    r = run(nc, [arrays], core_ids=[0])
    return r.results[0]["out_0"]
```

```python
import numpy as np

import concourse.bass as bass
from concourse import mybir
from contextlib import ExitStack
from functools import partial

P = 128
SLOTS = 8
GROUP = P * SLOTS
HALF = GROUP // 2
WIN = 64
WINB = 64
WINH = 32
EPS = 1e-5
CAP = 40.0


def build_gnn(nc, x, src, dst, edge_attr, w_full, b_full, bn1_g, bn1_b, bn2_g, bn2_b, w1, b1, out):
    fp32, i32, bf16, i16, u8 = (mybir.dt.float32, mybir.dt.int32, mybir.dt.bfloat16, mybir.dt.int16, mybir.dt.uint8)
    ALU, ACT, AX = mybir.AluOpType, mybir.ActivationFunctionType, mybir.AxisListType

    N, F = x.shape
    E = src.shape[0]
    D = 2 * F
    NG = -(-E // GROUP)
    NFULL = E // GROUP
    TAIL = E - NFULL * GROUP
    PAIRS = NFULL // 2
    assert NFULL % 2 == 0 and 0 < TAIL and NG == NFULL + 1 and NG <= P
    NT = 25
    NP = N // NT
    assert NP * NT == N and NP <= P
    NW, NWB = -(-N // WIN), -(-N // WINB)
    tail_halves = [(n, n // 4, n % 4) for n in (min(HALF, TAIL), max(0, TAIL - HALF))]
    tail_valid = [-(-max(0, tail_halves[s // 4][0] - s % 4) // 4) for s in range(SLOTS)]
    assert tail_halves[1][0] > 0
    HI = -(-N // P)
    SHIFT = (P // WINH).bit_length() - 1
    assert P == WINH << SHIFT

    tail_parts, at = [[], []], 2 * NFULL
    for h in range(2):
        s = 4 * h
        while s < 4 * h + 4:
            last = s
            while last + 1 < 4 * h + 4 and tail_valid[last + 1] == tail_valid[s]:
                last += 1
            tail_parts[h].append((s - 4 * h, last - 4 * h, tail_valid[s], at))
            s, at = last + 1, at + 1
    n_stats = at
    ds = bass.ds

    def pipelined(eng, parts, full):
        longest = max(lag for _, lag in parts)
        fill = max(2, longest + longest % 2)
        assert full % 2 == 0 and full > fill

        def straight(steps):
            for k in steps:
                for fn, lag in parts:
                    if 0 <= k - lag <= full:
                        fn((k - lag) // 2, (k - lag) % 2, k - lag, k - lag == full)

        straight(range(fill))
        with eng.Fori(fill // 2, full // 2) as j:
            for parity in range(2):
                for fn, lag in parts:
                    u = (parity - lag) % 2
                    fn(j + (parity - lag - u) // 2, u, 2 * j + (parity - lag), False)
        straight(range(full, full + 1 + longest))

    def load_by_edge(sp, place, source, g, tail, signal):
        if not tail:
            if len(source.shape) == 1:
                v = source[ds(g * GROUP, GROUP)].rearrange("(h p s) -> p h s", h=2, s=4)
                sp.dma_start(place(slice(0, P), slice(0, 2), slice(0, 4)), v).then_inc(signal, 16)
                return
            for h in range(2):
                v = source[ds(g * GROUP + h * HALF, HALF), :].rearrange("(p s) f -> p s f", s=4)
                sp.dma_start(place(slice(0, P), h, slice(0, 4)), v).then_inc(signal, 16)
            return
        for h, (n, full, rest) in enumerate(tail_halves):
            e0 = g * GROUP + h * HALF
            for p0, p1, k in ((0, full, 4), (full, full + 1, rest)):
                if k and p1 > p0:
                    v = source[e0 + 4 * p0:e0 + 4 * p0 + (p1 - p0) * k]
                    v = v.rearrange("(p s) -> p s", s=k) if len(source.shape) == 1 else v.rearrange("(p s) f -> p s f", s=k)
                    sp.dma_start(place(slice(p0, p1), h, slice(0, k)), v).then_inc(signal, 16)

    TAIL_LOADS = sum((full > 0) + (rest > 0) for _, full, rest in tail_halves)

    h_tab = nc.dram_tensor("h_tab", (N, F), fp32).ap()
    b_tab = nc.dram_tensor("b_tab", (N + WINB, D), fp32).ap()
    total_d = nc.dram_tensor("total_d", (D, NG * GROUP), fp32).ap()
    g_tab = nc.dram_tensor("g_tab", (N, F), fp32).ap()

    ctx = ExitStack()
    with ctx:
        def sb(name, shape, dt=fp32, scope=None):
            return (scope or ctx).enter_context(nc.sbuf_tensor(name, shape, dt))

        def psum(name, shape, scope):
            return scope.enter_context(nc.psum_tensor(name, shape, fp32))

        def sem(name):
            return ctx.enter_context(nc.semaphore(name))

        X = sb("X", [NP, NT, F])
        H = sb("H", [NP, NT, F])
        ident = sb("ident", [P, P])
        base_bc = sb("base_bc", [P, NG, 2])
        base_p = sb("base_p", [P, NG])
        win_p = sb("win_p", [P, NWB])
        win_c = sb("win_c", [P, NW])
        base_i = sb("base_i", [1, NG * 2], i32)
        fits_i = sb("fits_i", [1, 1], i32)
        counted_i = sb("counted_i", [1, 1], i32)
        bounded_i = sb("bounded_i", [1, 1], i32)
        dst_at = sb("dst_at", [P, NG, SLOTS], i32)
        count = sb("count", [P, HI, -(-(N + WINH) // 4) * 4], u8)
        iota_w = sb("iota_w", [P, WIN])
        w_edge = sb("w_edge", [D, D])
        agg = sb("agg", [F + 1, N + WIN])
        stats = sb("stats", [D, n_stats, 6])

        passed = sem("passed")

        def settle(eng):
            eng.sem_inc(passed, 1)

        def when_fits(eng, emit, flag=fits_i):
            fits = eng.value_load(flag[0:1, 0:1], min_val=0, max_val=1)
            with eng.If(fits == 1):
                emit(False)
            with eng.Else():
                emit(True)

        with ExitStack() as st:
            d_rows = sb("d_rows", [NG, GROUP], i32, st)
            w_dst = sb("w_dst", [F + 1, D], fp32, st)
            sq = sb("sq", [NP, NT, F], fp32, st)
            row = sb("row", [NP, 4, NT], fp32, st)
            HT = sb("HT", [F + 1, NT, NP], fp32, st)
            Brows = sb("Brows", [NP, NT, D], fp32, st)
            zero_rows = sb("zero_rows", [WINB, D], fp32, st)
            lo_hi = sb("lo_hi", [NG, 2, 2], fp32, st)
            spread = sb("spread", [NG, 4, P], fp32, st)
            ends = sb("ends", [P, 2, 2 * NG], fp32, st)
            gaps = sb("gaps", [P, 3, 2 * NG], fp32, st)
            part = sb("part", [P, 1], fp32, st)
            flag = sb("flag", [P, 4], fp32, st)
            ps_t = [psum(f"ps_t{i}", [F, 4, NP], st) for i in range(2)]
            ps_b = [psum(f"ps_b{i}", [NP, 4, D], st) for i in range(2)]
            ps_g = psum("ps_g", [P, 4, NG], st)

            x_in, d_in, w_in = sem("x_in"), sem("d_in"), sem("w_in")
            fills_set = sem("fills_set")
            consts, dve, act_ln, act_ht = sem("consts"), sem("dve"), sem("act_ln"), sem("act_ht")
            h_ready, ht_ps, b_ps, b_sb = sem("h_ready"), sem("ht_ps"), sem("b_ps"), sem("b_sb")
            spread_ready, spread_ps, tabs_out = sem("spread_ready"), sem("spread_ps"), sem("tabs_out")
            zero_ready, ones_ready = sem("zero_ready"), sem("ones_ready")
            fills = [(at, min(tail_halves[1][0], GROUP - at)) for at in range(TAIL, GROUP, tail_halves[1][0])]
            chunks = [(c, min(4, NT - 4 * c)) for c in range(-(-NT // 4))]
            table_parts = [(c, min(len(chunks), c + 3)) for c in range(0, len(chunks), 3)]

            with nc.Block() as block:
                @block.sync
                def _(sp):
                    sp.dma_start(X[:, :, :], x.rearrange("(p t) f -> p t f", t=NT)).then_inc(x_in, 16)
                    sp.dma_start(d_rows[0:NFULL, :], dst[0:NFULL * GROUP].rearrange("(g e) -> g e", e=GROUP)).then_inc(d_in, 16)
                    sp.dma_start(d_rows[NFULL:NG, 0:TAIL], dst[NFULL * GROUP:E].rearrange("(g e) -> g e", g=1)).then_inc(d_in, 16)
                    for at, n in fills:
                        sp.dma_start(d_rows[NFULL:NG, at:at + n], dst[E - n:E].rearrange("(g e) -> g e", g=1)).then_inc(d_in, 16)
                    sp.dma_start(w_dst[0:F, :], w_full[F:2 * F, :]).then_inc(w_in, 16)
                    sp.dma_start(w_dst[F:F + 1, :], b_full.rearrange("(a f) -> a f", a=1)).then_inc(w_in, 16)
                    sp.dma_start(w_edge[0:F, :], w_full[0:F, :]).then_inc(w_in, 16)
                    sp.dma_start(w_edge[F:D, :], w_full[2 * F:3 * F, :]).then_inc(w_in, 16)
                    sp.wait_ge(zero_ready, 1)
                    sp.dma_start(b_tab[N:N + WINB, :], zero_rows[:, :]).then_inc(tabs_out, 16)
                    sp.wait_ge(h_ready, 1)
                    sp.dma_start(h_tab.rearrange("(p t) f -> p t f", t=NT), H[:, :, :]).then_inc(tabs_out, 16)
                    for c0, c1 in table_parts:
                        sp.wait_ge(b_sb, c1)
                        t0, t1 = 4 * c0, min(NT, 4 * c1)
                        sp.dma_start(b_tab[0:N, :].rearrange("(p t) f -> p t f", t=NT)[:, t0:t1, :], Brows[:, t0:t1, :]).then_inc(tabs_out, 16)
                    sp.wait_ge(tabs_out, 32 + 16 * len(table_parts))

                @block.gpsimd
                def _(pool):
                    nc.gpsimd.memset(zero_rows[:, :], 0.0).then_inc(zero_ready, 1)
                    nc.gpsimd.memset(ident[:, :], 0.0).then_inc(consts, 1)
                    nc.gpsimd.iota(part[:, :], pattern=[[0, 1]], base=0, channel_multiplier=1,
                                   allow_small_or_imprecise_dtypes=True).then_inc(consts, 1)
                    pool.wait_ge(consts, 2)
                    nc.gpsimd.affine_select(out=ident[:, :], in_=ident[:, :], compare_op=ALU.not_equal, fill=1.0,
                                            base=0, pattern=[[-1, P]], channel_multiplier=1).then_inc(consts, 1)
                    nc.gpsimd.iota(iota_w[:, :], pattern=[[1, WIN]], base=0, channel_multiplier=0,
                                   allow_small_or_imprecise_dtypes=True).then_inc(fills_set, 1)
                    nc.gpsimd.iota(win_p[:, :], pattern=[[WINB, NWB]], base=0, channel_multiplier=1,
                                   allow_small_or_imprecise_dtypes=True).then_inc(fills_set, 1)
                    nc.gpsimd.iota(win_c[:, :], pattern=[[WIN, NW]], base=0, channel_multiplier=0,
                                   allow_small_or_imprecise_dtypes=True).then_inc(fills_set, 1)
                    nc.gpsimd.memset(count[:, :, :].bitcast(i32), 0).then_inc(fills_set, 1)
                    nc.gpsimd.memset(agg[:, :], 0.0).then_inc(fills_set, 1)
                    pool.wait_ge(fills_set, 5)

                @block.vector
                def _(v):
                    done = [0]

                    def step(ins):
                        done[0] += 1
                        ins.then_inc(dve, 1)
                        v.wait_ge(dve, done[0])

                    def per_node(k):
                        return row[:, k, :].unsqueeze(2).to_broadcast([NP, NT, F])

                    nc.vector.memset(HT[F:F + 1, :, :], 1.0).then_inc(ones_ready, 1)
                    v.wait_ge(x_in, 16)
                    step(nc.vector.reduce_sum(row[:, 0, :], X[:, :, :], axis=AX.X))
                    step(nc.vector.tensor_scalar(row[:, 1, :], row[:, 0, :], 1.0 / F, None, ALU.mult))
                    step(nc.vector.tensor_tensor(H[:, :, :], X[:, :, :], per_node(1), ALU.subtract))
                    step(nc.vector.tensor_tensor(sq[:, :, :], H[:, :, :], H[:, :, :], ALU.mult))
                    step(nc.vector.reduce_sum(row[:, 0, :], sq[:, :, :], axis=AX.X))
                    step(nc.vector.tensor_scalar(row[:, 2, :], row[:, 0, :], 1.0 / F, EPS, ALU.mult, ALU.add))
                    v.wait_ge(act_ln, 1)
                    step(nc.vector.reciprocal(row[:, 3, :], row[:, 1, :]))
                    step(nc.vector.tensor_tensor(sq[:, :, :], H[:, :, :], per_node(3), ALU.mult))
                    nc.vector.tensor_scalar(H[:, :, :], sq[:, :, :], 0.0, None, ALU.max).then_inc(h_ready, 1)
                    v.wait_ge(d_in, 16 * (2 + len(fills)))
                    halves = d_rows[:, :].rearrange("g (h e) -> g h e", h=2)
                    nc.vector.tensor_reduce(lo_hi[:, 0, :], halves, axis=AX.X, op=ALU.min)
                    step(nc.vector.tensor_reduce(lo_hi[:, 1, :], halves, axis=AX.X, op=ALU.max))
                    nc.vector.tensor_copy(spread[:, :, :], lo_hi[:, :, :].rearrange("g k h -> g (k h)").unsqueeze(2).to_broadcast([NG, 4, P])).then_inc(spread_ready, 1)
                    v.wait_ge(spread_ps, 1)
                    v.wait_ge(consts, 3)
                    for k in range(2):
                        last = nc.vector.tensor_copy(ends[:, k, :].rearrange("p (g h) -> p h g", h=2), ps_g[:, 2 * k:2 * k + 2, :])
                    step(last)
                    nc.vector.tensor_copy(base_bc[:, :, :], ends[:, 0, :].rearrange("p (g h) -> p g h", h=2))
                    nc.vector.tensor_scalar(base_p[:, :], ends[:, 0, :].rearrange("p (g h) -> p g h", h=2)[:, :, 0], part[:, 0:1], None, ALU.add)
                    nc.vector.tensor_copy(base_i[:, :], ends[0:1, 0, :])
                    step(nc.vector.memset(gaps[:, :, :], 0.0))
                    nc.vector.tensor_tensor(gaps[:, 0, :], ends[:, 1, :], ends[:, 0, :], ALU.subtract)
                    nc.vector.tensor_tensor(gaps[:, 1, 0:NG], ends[:, 1, :].rearrange("p (g h) -> p g h", h=2)[:, :, 1],
                                            ends[:, 0, :].rearrange("p (g h) -> p g h", h=2)[:, :, 0], ALU.subtract)
                    step(nc.vector.tensor_tensor(gaps[:, 2, 1:], ends[:, 1, 0:2 * NG - 1], ends[:, 0, 1:], ALU.subtract))
                    step(nc.vector.tensor_reduce(flag[:, 0:3], gaps[:, :, :], axis=AX.X, op=ALU.max))
                    for k, limit in enumerate((WINH - 0.5, WIN - 0.5, 0.5)):
                        last = nc.vector.tensor_scalar(flag[:, k:k + 1], flag[:, k:k + 1], float(limit), None, ALU.is_lt)
                    step(last)
                    step(nc.vector.tensor_tensor(flag[:, 0:1], flag[:, 0:1], flag[:, 1:2], ALU.mult))
                    step(nc.vector.tensor_tensor(flag[:, 1:2], flag[:, 0:1], flag[:, 2:3], ALU.mult))
                    step(nc.vector.tensor_copy(fits_i[:, :], flag[0:1, 1:2]))

                @block.scalar
                def _(a):
                    a.wait_ge(dve, 6)
                    nc.scalar.activation(row[:, 1, :], row[:, 2, :], ACT.Sqrt).then_inc(act_ln, 1)
                    for c in range(len(chunks) + 1):
                        if c < len(chunks):
                            k = chunks[c][1]
                            a.wait_ge(ht_ps, c + 1)
                            nc.scalar.activation(HT[0:F, 4 * c:4 * c + k, :], ps_t[c % 2][:, 0:k, :], ACT.Copy).then_inc(act_ht, 1)
                        if c >= 1:
                            d, k = chunks[c - 1]
                            a.wait_ge(b_ps, c)
                            nc.scalar.activation(Brows[:, 4 * d:4 * d + k, :], ps_b[d % 2][:, 0:k, :], ACT.Copy).then_inc(b_sb, 1)

                @block.tensor
                def _(pe):
                    pe.wait_ge(consts, 3)
                    pe.wait_ge(spread_ready, 1)
                    for k in range(4):
                        last = nc.tensor.matmul(ps_g[:, k, :], spread[:, k, :], ident[0:NG, 0:NG], start=True, stop=True)
                    last.then_inc(spread_ps, 1)

                    def transposes(c, k):
                        if c >= 2:
                            pe.wait_ge(act_ht, c - 1)
                        for t in range(k):
                            last = nc.tensor.transpose(ps_t[c % 2][:, t, :], H[:, 4 * c + t, :], ident[0:NP, 0:NP])
                        last.then_inc(ht_ps, 1)

                    def products(c, k):
                        pe.wait_ge(act_ht, c + 1)
                        if c >= 2:
                            pe.wait_ge(b_sb, c - 1)
                        for t in range(k):
                            last = nc.tensor.matmul(ps_b[c % 2][:, t, :], HT[:, 4 * c + t, :], w_dst[:, :],
                                                    start=True, stop=True)
                        last.then_inc(b_ps, 1)

                    pe.wait_ge(ones_ready, 1)
                    pe.wait_ge(w_in, 64)
                    pe.wait_ge(h_ready, 1)
                    for c in range(len(chunks) + 1):
                        if c < len(chunks):
                            transposes(*chunks[c])
                        if c >= 1:
                            products(*chunks[c - 1])

        with ExitStack() as st:
            idx = sb("idx", [P, 2, SLOTS], i32, st)
            Z = sb("Z", [P, 2, SLOTS, D], fp32, st)
            ZT = sb("ZT", [D, 2, HALF], fp32, st)
            d_row = sb("d_row", [WINB, 2, GROUP], i32, st)
            hot_t = sb("hot_t", [WINB, 2, GROUP], fp32, st)
            B_win = sb("B_win", [WINB, 2, D], fp32, st)
            tot = sb("tot", [D, 2, GROUP], fp32, st)
            ps_z = [psum(f"ps_z{h}", [D, HALF], st) for h in range(2)]
            ps_tot = [psum(f"ps_tot{h}", [D, HALF], st) for h in range(2)]
            iota_lo, iota_key = sb("iota_lo", [P, P], i16, st), sb("iota_key", [P, HI * WINH], i16, st)
            src_bits = sb("src_bits", [P, 2, 2, SLOTS], i32, st)
            lo_f = sb("lo_f", [P, 2, SLOTS], fp32, st)
            key = sb("key", [P, 2, 2, SLOTS], fp32, st)
            hot_lo = sb("hot_lo", [P, 2, 4, P], bf16, st)
            hot_key = sb("hot_key", [P, 2, 4, HI * WINH], bf16, st)
            HSPLIT = [(0, (HI + 1) // 2), ((HI + 1) // 2, HI)]
            ps_cnt = [[psum(f"ps_cnt{h}{k}", [P, b - a, WINH], st) for k, (a, b) in enumerate(HSPLIT)] for h in range(2)]
            dedge_in = [sem(f"dedge_in{u}") for u in range(2)]
            iotas, bits, key_r, hot_c = sem("iotas"), sem("bits"), sem("key_r"), sem("hot_c")
            cnt_ps, cnt_fix, cnt_sb = sem("cnt_ps"), sem("cnt_fix"), sem("cnt_sb")

            idx_in = [sem(f"idx_in{u}") for u in range(2)]
            edge_in = [sem(f"edge_in{u}") for u in range(2)]
            drow_in = [sem(f"drow_in{u}") for u in range(2)]
            bwin_in = [sem(f"bwin_in{u}") for u in range(2)]
            gathered = [sem(f"gathered{u}") for u in range(2)]
            tot_out = [sem(f"tot_out{u}") for u in range(2)]
            zt_ps, zt_sb, zt_used = sem("zt_ps"), sem("zt_sb"), sem("zt_used")
            hot_ready, win_used, tail_set = sem("hot_ready"), sem("win_used"), sem("tail_set")
            tot_ps, tot_sb, tot_bn = sem("tot_ps"), sem("tot_sb"), sem("tot_bn")
            LEAD = 4

            def by_half(tile, u):
                return tile[:, ds(u, 1), :].rearrange("p a (h s) -> p (a h) s", h=2)

            def groups(eng, group):
                with eng.Fori(0, PAIRS) as i:
                    for u in range(2):
                        group(i, u, 2 * i + u, False)
                group(PAIRS, 0, NFULL, True)

            with nc.Block() as block:
                @block.sync
                def _(sp):
                    def stage(general):
                        def group(i, u, g, tail):
                            e0 = g * GROUP
                            d_cols = TAIL if tail else GROUP
                            if not (isinstance(i, int) and i == 0):
                                sp.wait_ge(gathered[u], 16 * SLOTS * i)
                                settle(sp)
                            if not general:
                                sp.wait_ge(key_r, g + 1)
                                settle(sp)
                            if tail:
                                sp.wait_ge(tail_set, 4)
                            load_by_edge(sp, lambda p, h, q: by_half(idx, u)[p, h, q], src, g, tail, idx_in[u])
                            if not general:
                                load_by_edge(sp, lambda p, h, q: by_half(dst_at, g)[p, h, q], dst, g, tail, dedge_in[u])
                            sp.wait_ge(zt_ps, 2 * g + 2)
                            settle(sp)
                            load_by_edge(sp, lambda p, h, q: Z[:, u, :, F:D].rearrange("p (h q) f -> p h q f", h=2)[p, h, q], edge_attr, g, tail, edge_in[u])
                            sp.wait_ge(tot_ps, 2 * g + 2)
                            settle(sp)
                            sp.dma_start(d_row[:, u, 0:d_cols], dst[ds(e0, d_cols)].unsqueeze(0).to_broadcast([WINB, d_cols])).then_inc(drow_in[u], 16)
                            if general:
                                with sp.Fori(0, NWB) as r:
                                    sp.wait_ge(win_used, g * NWB + r + 1)
                                    settle(sp)
                                    sp.dma_start(B_win[:, 0, :], b_tab[ds(r * WINB, WINB), :]).then_inc(bwin_in[0], 16)
                            else:
                                first = sp.value_load(base_i[0:1, ds(g * 2, 1)], min_val=0, max_val=N - 1)
                                sp.dma_start(B_win[:, u, :], b_tab[ds(first, WINB), :]).then_inc(bwin_in[u], 16)
                        pipelined(sp, [(group, 0)], NFULL)
                    when_fits(sp, stage)

                @block.gpsimd
                def _(pool):
                    def group(i, u, g, tail):
                        pool.wait_ge(zt_ps, 2 * g + 2)
                        pool.wait_ge(idx_in[u], 16 * i + 16 * (TAIL_LOADS if tail else 1))
                        settle(pool)
                        for s in range(SLOTS):
                            pool.indirect_dma_start(Z[:, u, s, 0:F], None, h_tab[:, :],
                                                    bass.IndirectOffsetOnAxis(ap=idx[:, u, s:s + 1], axis=0)).then_inc(gathered[u], 16)
                    nc.gpsimd.iota(iota_lo[:, :], pattern=[[1, P]], base=0, channel_multiplier=0).then_inc(iotas, 1)
                    nc.gpsimd.iota(iota_key[:, :], pattern=[[1, HI * WINH]], base=0, channel_multiplier=0).then_inc(iotas, 1)
                    groups(pool, group)

                @block.vector
                def _(v):
                    v.sem_inc(tot_bn, LEAD)
                    v.sem_inc(key_r, 2)
                    v.wait_ge(iotas, 2)

                    def keys(i, u, g, tail):
                        loads = 16 * (TAIL_LOADS if tail else 1)
                        v.wait_ge(idx_in[u], 16 * i + loads)
                        v.wait_ge(dedge_in[u], 16 * i + loads)
                        nc.vector.tensor_scalar(src_bits[:, u, 0, :], idx[:, u, :], P - 1, None, ALU.bitwise_and)
                        nc.vector.tensor_scalar(src_bits[:, u, 1, :], idx[:, u, :], SHIFT, (1 << 30) - WINH,
                                                ALU.logical_shift_right, ALU.bitwise_and)
                        nc.vector.tensor_tensor(key[:, u, 0, :].rearrange("p (h s) -> p h s", h=2), by_half(dst_at, g),
                                                base_bc[:, ds(g, 1), :].rearrange("p a h -> p (a h)").unsqueeze(2).to_broadcast([P, 2, 4]),
                                                ALU.subtract).then_inc(bits, 1)
                        v.wait_ge(bits, g + 1)
                        nc.vector.tensor_copy(lo_f[:, u, :], src_bits[:, u, 0, :])
                        nc.vector.tensor_tensor(key[:, u, 1, :], key[:, u, 0, :], src_bits[:, u, 1, :], ALU.add).then_inc(key_r, 1)

                    def hots(h):
                        def part(i, u, g, tail):
                            v.wait_ge(key_r, g + 3)
                            v.wait_ge(cnt_ps, 2 * g + h + 1)
                            for s in range(4):
                                nc.vector.tensor_scalar(hot_lo[:, h, s, :], iota_lo[:, :], lo_f[:, u, 4 * h + s:4 * h + s + 1], None, ALU.is_equal)
                                done = nc.vector.tensor_scalar(hot_key[:, h, s, :], iota_key[:, :], key[:, u, 1, 4 * h + s:4 * h + s + 1], None, ALU.is_equal)
                            done.then_inc(hot_c, 1)
                        return part

                    def shared_node(h):
                        def part(i, u, g, tail):
                            first = v.value_load(base_i[0:1, ds(2 * g + h, 1)], min_val=0, max_val=N - 1)
                            v.wait_ge(cnt_ps, 2 * g + h + 3)
                            v.wait_ge(cnt_sb, 2 * g + h + 2)
                            for k, (a0, b0) in enumerate(HSPLIT):
                                column = ps_cnt[h][k][:, :, 0:1]
                                done = nc.vector.tensor_tensor(column, column, count[:, a0:b0, ds(first, 1)], ALU.add)
                            done.then_inc(cnt_fix, 1)
                        return part

                    def statistics(i, u, g, tail):
                        for h in range(2):
                            v.wait_ge(tot_sb, 2 * g + h + 1 + LEAD)
                            half = tot[:, u, h * HALF:(h + 1) * HALF]
                            if tail:
                                half = half.rearrange("f (s p) -> f s p", p=P)
                                for first, last, valid, at in tail_parts[h]:
                                    done = nc.vector.bn_stats(stats[:, at, :], half[:, first:last + 1, 0:valid])
                                done.then_inc(tot_bn, 1)
                            else:
                                nc.vector.bn_stats(stats[:, 2 * g + h, :], half).then_inc(tot_bn, 1)

                    def stage(general):
                        def hot(scalar, u, place):
                            return nc.vector.tensor_scalar(hot_t[:, place, :], d_row[:, u, :], scalar, None, ALU.is_equal)

                        def nodes_at_dst(i, u, g, tail):
                            if tail:
                                v.wait_ge(gathered[u], 16 * SLOTS * i)
                                v.wait_ge(zt_ps, 2 * g + 2)
                                nc.vector.memset(idx[:, u, :], 0).then_inc(tail_set, 1)
                                nc.vector.memset(Z[:, u, :, F:D], 0.0).then_inc(tail_set, 1)
                                nc.vector.memset(d_row[:, u, TAIL:GROUP], -1).then_inc(tail_set, 1)
                                nc.vector.memset(dst_at[:, NFULL, :], -1).then_inc(tail_set, 1)
                                v.wait_ge(tail_set, 4)
                            v.wait_ge(drow_in[u], 16 * i + 16)
                            if general:
                                settle(v)
                                with v.Fori(0, NWB) as r:
                                    v.wait_ge(win_used, g * NWB + r + 1)
                                    hot(win_p[0:WINB, ds(r, 1)], u, 0).then_inc(hot_ready, 1)
                            else:
                                v.wait_ge(tot_ps, 2 * g + 2)
                                hot(base_p[0:WINB, ds(g, 1)], u, u).then_inc(hot_ready, 1)

                        if general:
                            pipelined(v, [(nodes_at_dst, 0), (statistics, 1)], NFULL)
                        else:
                            pipelined(v, [(nodes_at_dst, 0), (statistics, 1), (keys, 0), (shared_node(0), 1), (hots(0), 0),
                                          (shared_node(1), 1), (hots(1), 0)], NFULL)
                    when_fits(v, stage)

                @block.scalar
                def _(a):
                    a.sem_inc(tot_sb, LEAD)
                    for u in range(2):
                        a.sem_inc(tot_out[u], 16)

                    a.sem_inc(cnt_sb, 2)

                    def transposed(i, u, g, tail):
                        for h in range(2):
                            a.wait_ge(zt_ps, 2 * g + h + 1 + LEAD)
                            a.wait_ge(zt_used, 2 * g + h + 1)
                            nc.scalar.activation(ZT[:, h, :], ps_z[h][:, :], ACT.Copy).then_inc(zt_sb, 1)

                    def counts(i, u, g, tail):
                        for h in range(2):
                            first = a.value_load(base_i[0:1, ds(2 * g + h, 1)], min_val=0, max_val=N - 1)
                            a.wait_ge(cnt_fix, 2 * g + h + 1)
                            for k, (a0, b0) in enumerate(HSPLIT):
                                last = nc.scalar.activation(count[:, a0:b0, ds(first, WINH)], ps_cnt[h][k][:, :, :], ACT.Copy)
                            last.then_inc(cnt_sb, 1)

                    def totals(i, u, g, tail):
                        a.wait_ge(tot_out[u], 16 * i + 16)
                        a.wait_ge(tot_bn, 2 * g + 2)
                        for h in range(2):
                            a.wait_ge(tot_ps, 2 * g + h + 1 + LEAD)
                            nc.scalar.activation(tot[:, u, h * HALF:(h + 1) * HALF], ps_tot[h][:, :], ACT.Copy).then_inc(tot_sb, 1)
                        a.wait_ge(tot_sb, 2 * g + 2 + LEAD)
                        a.dma_start(total_d[:, ds(g * GROUP, GROUP)], tot[:, u, :]).then_inc(tot_out[u], 16)

                    def stage(general):
                        pipelined(a, [(transposed, 0), (totals, 0)] if general else
                                  [(transposed, 0), (counts, 1), (totals, 0)], NFULL)
                    when_fits(a, stage)
                    a.wait_ge(tot_out[0], 16 * (PAIRS + 2))
                    a.wait_ge(tot_out[1], 16 * (PAIRS + 1))

                @block.tensor
                def _(pe):
                    pe.sem_inc(zt_ps, LEAD)
                    pe.sem_inc(zt_used, 2)
                    pe.sem_inc(tot_ps, LEAD)
                    pe.sem_inc(win_used, 1)
                    pe.sem_inc(cnt_ps, 2)

                    def stage(general):
                        def rows_at_dst(u, place, h, stop):
                            edges = hot_t[:, place, h * HALF:(h + 1) * HALF].rearrange("w (p s) -> w s p", s=4)
                            return nc.tensor.matmul(ps_tot[h][:, :], B_win[:, place, :], edges, start=False, stop=stop)

                        def group(i, u, g, tail):
                            pe.wait_ge(gathered[u], 16 * SLOTS * i + 16 * SLOTS)
                            pe.wait_ge(edge_in[u], 32 * i + (16 * TAIL_LOADS if tail else 32))
                            for h in range(2):
                                for s in range(4):
                                    last = nc.tensor.transpose(ps_z[h][:, s * P:(s + 1) * P], Z[:, u, 4 * h + s, :], ident[:, :])
                                last.then_inc(zt_ps, 1)
                            for h in range(2):
                                pe.wait_ge(zt_sb, 2 * g + h + 1)
                                pe.wait_ge(tot_sb, 2 * g + h - 1 + LEAD)
                                nc.tensor.matmul(ps_tot[h][:, :], w_edge[:, :], ZT[:, h, :], start=True, stop=False).then_inc(zt_used, 1)
                            if general:
                                def window(r, stop):
                                    pe.wait_ge(hot_ready, g * NWB + r + 1)
                                    pe.wait_ge(bwin_in[0], 16 * (g * NWB + r) + 16)
                                    rows_at_dst(u, 0, 0, stop)
                                    rows_at_dst(u, 0, 1, stop).then_inc(win_used, 1)

                                settle(pe)
                                with pe.Fori(0, NWB - 1) as r:
                                    window(r, False)
                                window(NWB - 1, True)
                                pe.wait_ge(win_used, g * NWB + NWB + 1)
                                pe.sem_inc(tot_ps, 2)
                            else:
                                pe.wait_ge(hot_ready, g + 1)
                                pe.wait_ge(bwin_in[u], 16 * i + 16)
                                for h in range(2):
                                    rows_at_dst(u, u, h, True).then_inc(tot_ps, 1)
                            if not general:
                                for h in range(2):
                                    pe.wait_ge(hot_c, 2 * g + h + 1)
                                    pe.wait_ge(cnt_sb, 2 * g + h + 1)
                                    for k, (a0, b0) in enumerate(HSPLIT):
                                        for s in range(4):
                                            last = nc.tensor.matmul(ps_cnt[h][k][:, :, :], hot_lo[:, h, s, :],
                                                                    hot_key[:, h, s, a0 * WINH:b0 * WINH], start=(s == 0), stop=(s == 3))
                                    last.then_inc(cnt_ps, 1)
                        groups(pe, group)
                    when_fits(pe, stage)

        filt, core = sb("filt", [P, 3]), sb("core", [P, 3])
        W2 = [P, 2, 2, HALF]
        pairs_of_totals = ExitStack()
        Ft, Ct = sb("Ft", W2, fp32, pairs_of_totals), sb("Ct", W2, fp32, pairs_of_totals)
        total_in = [sem(f"total_in{b}") for b in range(2)]

        def load_totals(sp, b, k, nu):
            for tile, f0 in ((Ft, 0), (Ct, F)):
                for h in range(2):
                    from_ = total_d[f0:f0 + F, ds(k * (2 * GROUP), nu * GROUP)].rearrange("f (u h e) -> f h u e", u=nu, h=2)
                    sp.dma_start(tile[h * F:(h + 1) * F, b, 0:nu, :], from_[:, h, :, :]).then_inc(total_in[b], 16)

        with ExitStack() as st:
            mv = sb("mv", [D, 2], fp32, st)
            gb = sb("gb", [D, 2], fp32, st)
            tmp = sb("tmp", [D, 4], fp32, st)
            aff = sb("aff", [D, 3], fp32, st)
            off = sb("off", [D, 2 * n_stats], fp32, st)
            far, size = sb("far", [D, 4], fp32, st), sb("size", [D, 4], fp32, st)
            reach, reach_sb = psum("reach", [1, D], st), sb("reach_sb", [1, 2], fp32, st)
            bound, sq_far, reach_ps = sem("bound"), sem("sq_far"), sem("reach_ps")
            pick, picked = sb("pick", [D, 2, 2, F], fp32, st), sem("picked")
            twice = psum("twice", [P, 2, 3], st)
            gb_in, bn, rt, halved, aff_in = sem("gb_in"), sem("bn"), sem("rt"), sem("halved"), sem("aff_in")
            with nc.Block() as block:
                @block.sync
                def _(sp):
                    sp.dma_start(gb[:, 0:1], bn1_g.rearrange("(f a) -> f a", a=1)).then_inc(gb_in, 16)
                    sp.dma_start(gb[:, 1:2], bn1_b.rearrange("(f a) -> f a", a=1)).then_inc(gb_in, 16)
                    for k in range(2):
                        load_totals(sp, k, k, 2)
                    sp.wait_ge(gb_in, 32)

                @block.vector
                def _(v):
                    def step(n, ins):
                        ins.then_inc(bn, 1)
                        v.wait_ge(bn, n)

                    nc.vector.tensor_copy(pick[:, :, :, :], ident[:, :].rearrange("p (k f) -> p k f", k=2).unsqueeze(2).to_broadcast([D, 2, 2, F])).then_inc(picked, 1)
                    step(1, nc.vector.bn_aggr(mv[:, :], stats[:, :, :].rearrange("f k s -> f (k s)")))
                    step(2, nc.vector.tensor_scalar(tmp[:, 0:1], mv[:, 1:2], EPS, None, ALU.add))
                    def mark(n, ins):
                        ins.then_inc(bound, 1)
                        v.wait_ge(bound, n)

                    sets = stats[:, :, :].rearrange("f k (h c) -> f (k h) c", h=2)
                    mark(1, nc.vector.tensor_scalar(off[:, :], sets[:, :, 1], mv[:, 0:1], None, ALU.subtract))
                    mark(2, nc.vector.tensor_tensor(off[:, :], off[:, :], off[:, :], ALU.mult))
                    nc.vector.tensor_reduce(far[:, 0:1], off[:, :], AX.X, ALU.max).then_inc(bound, 1)
                    mark(4, nc.vector.tensor_reduce(far[:, 1:2], sets[:, :, 2], AX.X, ALU.max))
                    v.wait_ge(rt, 1)
                    step(3, nc.vector.reciprocal(tmp[:, 2:3], tmp[:, 1:2]))
                    v.wait_ge(gb_in, 32)
                    step(4, nc.vector.tensor_tensor(aff[:, 0:1], tmp[:, 2:3], gb[:, 0:1], ALU.mult))
                    step(5, nc.vector.tensor_tensor(tmp[:, 3:4], mv[:, 0:1], aff[:, 0:1], ALU.mult))
                    step(6, nc.vector.tensor_tensor(aff[:, 1:2], gb[:, 1:2], tmp[:, 3:4], ALU.subtract))
                    step(7, nc.vector.tensor_scalar(aff[0:F, 0:2], aff[0:F, 0:2], -1.0, None, ALU.mult))
                    step(8, nc.vector.tensor_scalar(aff[:, 2:3], aff[:, 1:2], -1.0, CAP, ALU.mult, ALU.add))

                    v.wait_ge(halved, 1)
                    nc.vector.tensor_copy(filt[:, :], twice[:, 0, :]).then_inc(aff_in, 1)
                    nc.vector.tensor_copy(core[:, :], twice[:, 1, :]).then_inc(aff_in, 1)

                    v.wait_ge(sq_far, 1)
                    mark(5, nc.vector.tensor_tensor(far[:, 0:1], far[:, 2:3], far[:, 3:4], ALU.add))
                    nc.vector.tensor_copy(size[:, 1:2], gb[:, 1:2]).then_inc(bound, 1)
                    mark(7, nc.vector.tensor_tensor(size[:, 0:1], far[:, 0:1], aff[:, 0:1], ALU.mult))
                    mark(8, nc.vector.tensor_scalar(size[:, 2:4], size[:, 0:2], -1.0, None, ALU.mult))
                    mark(9, nc.vector.tensor_tensor(size[:, 0:2], size[:, 0:2], size[:, 2:4], ALU.max))
                    mark(10, nc.vector.tensor_tensor(size[:, 0:1], size[:, 0:1], size[:, 1:2], ALU.add))
                    v.wait_ge(reach_ps, 1)
                    mark(11, nc.vector.tensor_reduce(reach_sb[:, 0:1], reach[:, :], AX.X, ALU.max))
                    mark(12, nc.vector.tensor_scalar(reach_sb[:, 1:2], reach_sb[:, 0:1], 0.99 * CAP, None, ALU.is_lt))
                    mark(13, nc.vector.tensor_copy(bounded_i[:, :], reach_sb[:, 1:2]))
                    v.wait_ge(aff_in, 2)

                @block.scalar
                def _(a):
                    a.wait_ge(bn, 2)
                    nc.scalar.activation(tmp[:, 1:2], tmp[:, 0:1], ACT.Sqrt).then_inc(rt, 1)
                    a.wait_ge(bound, 4)
                    nc.scalar.activation(far[:, 2:4], far[:, 0:2], ACT.Sqrt).then_inc(sq_far, 1)

                @block.tensor
                def _(pe):
                    pe.wait_ge(picked, 1)
                    pe.wait_ge(bn, 8)
                    for k in range(2):
                        last = nc.tensor.matmul(twice[:, k, :], pick[:, k, :, :].rearrange("p h f -> p (h f)"), aff[:, :], start=True, stop=True)
                    last.then_inc(halved, 1)
                    pe.wait_ge(bound, 10)
                    nc.tensor.transpose(reach[:, :], size[:, 0:1], ident[:, :]).then_inc(reach_ps, 1)

        class WindowSums:

            def __init__(self, name, st, into, rows, places):
                self.into, self.rows = into, rows
                self.d_e = sb(name + "_d_e", [P, 2, SLOTS], i32, st)
                self.rel = sb(name + "_rel", [P, 2, SLOTS], fp32, st)
                self.hot = sb(name + "_hot", [P, places, SLOTS, WIN], fp32, st)
                self.rel_pair = sb(name + "_rel_pair", [P, 2, 2, SLOTS], fp32, st)
                self.ps = [psum(f"{name}_ps{u}", [rows, WIN], st) for u in range(2)]
                self.d_in = [sem(f"{name}_d_in{u}") for u in range(2)]
                self.d_set, self.d_used = sem(name + "_d_set"), sem(name + "_d_used")
                self.rel_ready, self.hot_ready = sem(name + "_rel_ready"), sem(name + "_hot_ready")
                self.summed, self.added = sem(name + "_summed"), sem(name + "_added")

            def start_vector(self, v):
                v.sem_inc(self.d_used, 2)
                v.sem_inc(self.added, 2)

            def start_tensor(self, pe):
                pe.sem_inc(self.summed, 2)

            def load_dst(self, sp, u, g, tail):
                e0 = g * GROUP
                sp.wait_ge(self.d_used, g + 1)
                settle(sp)
                if tail:
                    sp.wait_ge(self.d_set, 1)
                load_by_edge(sp, lambda p, h, q: by_half(self.d_e, u)[p, h, q], dst, g, tail, self.d_in[u])

            def one_hot(self, v, u, place, base, count):
                nc.vector.tensor_scalar(self.rel[:, place, :], self.d_e[:, u, :], base, None, ALU.subtract).then_inc(self.rel_ready, 1)
                v.wait_ge(self.rel_ready, count + 1)
                return nc.vector.tensor_tensor(self.hot[:, place, :, :],
                                               iota_w[:, :].unsqueeze(1).to_broadcast([P, SLOTS, WIN]),
                                               self.rel[:, place, :].unsqueeze(2).to_broadcast([P, SLOTS, WIN]),
                                               ALU.is_equal)

            def dst_arrived(self, v, i, u, g, tail):
                if tail:
                    v.wait_ge(self.d_used, g + 1)
                    nc.vector.memset(self.d_e[:, u, :], -1).then_inc(self.d_set, 1)
                v.wait_ge(self.d_in[u], 16 * i + 16 * (TAIL_LOADS if tail else 1))

            def places_fit(self, v, b, k, last):
                nu = 1 if last else 2
                nc.vector.tensor_tensor(self.rel_pair[:, b, 0:nu, :], dst_at[:, ds(2 * k, nu), :],
                                        base_bc[:, ds(2 * k, nu), 0:1].to_broadcast([P, nu, SLOTS]),
                                        ALU.subtract).then_inc(self.rel_ready, 1)

            def hots_fit(self, v, b, k, last):
                nu = 1 if last else 2
                v.wait_ge(self.summed, 2 * k + 1)
                v.wait_ge(self.rel_ready, k + 1)
                nc.vector.tensor_tensor(self.hot[:, 2 * b:2 * b + nu, :, :].rearrange("p u s w -> p (u s) w"),
                                        iota_w[:, :].unsqueeze(1).to_broadcast([P, nu * SLOTS, WIN]),
                                        self.rel_pair[:, b, 0:nu, :].rearrange("p u s -> p (u s)").unsqueeze(2).to_broadcast([P, nu * SLOTS, WIN]),
                                        ALU.is_equal).then_inc(self.hot_ready, nu)
            def adds_fit(self, v, k, last):
                nu = 1 if last else 2
                firsts = [v.value_load(base_i[0:1, ds(4 * k + 2 * u, 1)], min_val=0, max_val=N - 1) for u in range(nu)]
                for u, first in enumerate(firsts):
                    v.wait_ge(self.summed, 2 * k + u + 3)
                    v.wait_ge(self.added, 2 * k + u + 2)
                    window = self.into[0:self.rows, ds(first, WIN)]
                    nc.vector.tensor_tensor(window, window, self.ps[u][:, :], ALU.add).then_inc(self.added, 1)

            def all_windows(self, v, i, u, g, tail):
                self.dst_arrived(v, i, u, g, tail)
                settle(v)
                with v.Fori(0, NW) as r:
                    k = g * NW + r
                    v.wait_ge(self.added, k + 2)
                    self.one_hot(v, u, 0, win_c[:, ds(r, 1)], k).then_inc(self.hot_ready, 1)
                    v.wait_ge(self.summed, k + 3)
                    window = self.into[0:self.rows, ds(r * WIN, WIN)]
                    nc.vector.tensor_tensor(window, window, self.ps[0][:, :], ALU.add).then_inc(self.added, 1)
                v.sem_inc(self.d_used, 1)

            def products(self, pe, general, lhs, g, b, u):
                def tiles(place, hots):
                    for s in range(SLOTS):
                        last = nc.tensor.matmul(self.ps[place][:, :], lhs(s), self.hot[:, hots, s, :],
                                                start=(s == 0), stop=(s == SLOTS - 1))
                    return last

                if general:
                    settle(pe)
                    with pe.Fori(0, NW) as r:
                        pe.wait_ge(self.hot_ready, g * NW + r + 1)
                        pe.wait_ge(self.added, g * NW + r + 2)
                        tiles(0, 0).then_inc(self.summed, 1)
                else:
                    pe.wait_ge(self.hot_ready, g + 1)
                    pe.wait_ge(self.added, g + 1)
                    tiles(u, 2 * b + u).then_inc(self.summed, 1)

        with ExitStack() as st:
            low = sb("low", [P, 2, 2, 2, HALF], fp32, st)
            low_f, low_c = low[:, :, 0, :, :], low[:, :, 1, :, :]
            y = sb("y", W2, fp32, st)
            logs = sb("logs", [P, 2, 2, 2, HALF], fp32, st)
            sig, soft = logs[:, :, 0, :, :], logs[:, :, 1, :, :]
            msg_t = sb("msg_t", W2, fp32, st)
            msg = sb("msg", [P, 4, SLOTS, F + 1], fp32, st)
            ps_m = [psum(f"ps_m{q}", [P, 4, P], st) for q in range(4)]
            sums = WindowSums("b", st, agg, F + 1, 4)

            low_f_r, low_c_r, y_r = sem("low_f_r"), sem("low_c_r"), sem("y_r")
            exp_f, exp_c, ln_f, ln_c = sem("exp_f"), sem("exp_c"), sem("ln_f"), sem("ln_c")
            sig_r, soft_r, msg_t_r = sem("sig_r"), sem("soft_r"), sem("msg_t_r")
            msg_ps, msg_sb, ones_set = sem("msg_ps"), sem("msg_sb"), sem("ones_set")


            def evacuated(b, u):
                return (msg[:, 2 * b + u, :, 0:F].rearrange("p (h c) f -> p c h f", h=2),
                        ps_m[2 * b + u][:, :, :].rearrange("p c (h f) -> p c h f", h=2))

            with nc.Block() as block:
                @block.sync
                def _(sp):
                    def load(wide, n, b, k, last):
                        nu = 1 if last else 2
                        if isinstance(k, int) and k < 2:
                            return
                        if wide:
                            sp.wait_ge(y_r, k + 1)
                            sp.wait_ge(low_c_r, k + 1)
                        else:
                            sp.wait_ge(exp_c, k + 1)
                            sp.wait_ge(exp_f, k + 1)
                        settle(sp)
                        load_totals(sp, b, k, nu)

                    def load_dst(n, b, k, last):
                        nu = 1 if last else 2
                        for u in range(nu):
                            sums.load_dst(sp, u, 2 * k + u, last)

                    def stage(wide):
                        loads = (partial(load, wide), 0)
                        when_fits(sp, lambda general: pipelined(sp, [loads, (load_dst, 3 if wide else 1)] if general else [loads], PAIRS))
                    when_fits(sp, stage, bounded_i)

                @block.vector
                def _(v):
                    v.sem_inc(low_c_r, 2)
                    v.sem_inc(soft_r, 2)
                    sums.start_vector(v)

                    def stage(wide, general):
                        def affine(n, b, k, last):
                            nu = 1 if last else 2
                            v.wait_ge(total_in[b], 64 * n + 64)
                            v.wait_ge(exp_c, k + 1)
                            nc.vector.tensor_scalar(low_f[:, b, 0:nu, :], Ft[:, b, 0:nu, :], filt[:, 0:1], filt[:, 2:3],
                                                    ALU.mult, ALU.min).then_inc(low_f_r, 1)
                            nc.vector.tensor_scalar(low_c[:, b, 0:nu, :], Ct[:, b, 0:nu, :], core[:, 0:1], core[:, 2:3],
                                                    ALU.mult, ALU.min).then_inc(low_c_r, 1)

                        def places(n, b, k, last):
                            if not general:
                                sums.places_fit(v, b, k, last)

                        def hots(n, b, k, last):
                            if not general:
                                sums.hots_fit(v, b, k, last)

                        def softplus(n, b, k, last):
                            nu = 1 if last else 2
                            v.wait_ge(ln_c, k + 1)
                            v.wait_ge(y_r, k + 3)
                            nc.vector.tensor_tensor(soft[:, b, 0:nu, :], y[:, b, 0:nu, :], soft[:, b, 0:nu, :],
                                                    ALU.max).then_inc(soft_r, 1)

                        def add(n, b, k, last):
                            if not general:
                                sums.adds_fit(v, k, last)
                                return
                            for u in range(1 if last else 2):
                                sums.all_windows(v, k, u, 2 * k + u, last)

                        def by_edge(n, b, k, last):
                            nu = 1 if last else 2
                            for u in range(nu):
                                v.wait_ge(msg_ps, 2 * k + u + 5)
                                nc.vector.tensor_copy(*evacuated(b, u)).then_inc(msg_sb, 1)
                        pipelined(v, [(softplus, 2), (affine, 0), (add, 3), (places, 1), (hots, 2)] if wide else
                                  [(places, 0), (by_edge, 0), (hots, 0), (add, 1)], PAIRS)
                    when_fits(v, lambda wide: when_fits(v, partial(stage, wide)), bounded_i)

                @block.scalar
                def _(a):
                    a.preload_act_table_set("natural_log_exp_and_others")
                    a.sem_inc(exp_c, 2)
                    a.sem_inc(exp_f, 2)
                    a.sem_inc(ln_f, 2)
                    a.sem_inc(msg_sb, 4)

                    def exps(n, b, k, last):
                        nu = 1 if last else 2
                        a.wait_ge(total_in[b], 64 * n + 64)
                        a.wait_ge(ln_f, k + 1)
                        nc.scalar.activation(low_f[:, b, 0:nu, :], Ft[:, b, 0:nu, :], ACT.Exp, bias=filt[:, 1:2],
                                             scale=filt[:, 0:1]).then_inc(exp_f, 1)
                        nc.scalar.activation(low_c[:, b, 0:nu, :], Ct[:, b, 0:nu, :], ACT.Exp, bias=core[:, 1:2],
                                             scale=core[:, 0:1]).then_inc(exp_c, 1)

                    def both_logs(n, b, k, last):
                        nu = 1 if last else 2
                        a.wait_ge(exp_f, k + 3)
                        a.wait_ge(exp_c, k + 3)
                        a.wait_ge(msg_t_r, k + 1)
                        nc.scalar.activation(logs[:, b, :, 0:nu, :], low[:, b, :, 0:nu, :], ACT.Ln, bias=1.0).then_inc(ln_f, 1)

                    def sigmoid(n, b, k, last):
                        nu = 1 if last else 2
                        a.wait_ge(ln_f, k + 3)
                        nc.scalar.activation(sig[:, b, 0:nu, :], sig[:, b, 0:nu, :], ACT.Exp, scale=-1.0).then_inc(sig_r, 1)

                    def functions(n, b, k, last):
                        nu = 1 if last else 2
                        at = (slice(None), b, slice(0, nu), slice(None))
                        a.wait_ge(low_f_r, k + 1)
                        a.wait_ge(msg_t_r, k + 1)
                        nc.scalar.activation(sig[at], low_f[at], ACT.Exp, bias=filt[:, 1:2]).then_inc(exp_f, 1)
                        a.wait_ge(low_c_r, k + 3)
                        nc.scalar.activation(soft[at], low_c[at], ACT.Exp, bias=core[:, 1:2]).then_inc(exp_c, 1)
                        a.wait_ge(exp_f, k + 3)
                        nc.scalar.activation(sig[at], sig[at], ACT.Ln, bias=1.0).then_inc(ln_f, 1)
                        a.wait_ge(exp_c, k + 3)
                        nc.scalar.activation(soft[at], soft[at], ACT.Ln, bias=1.0).then_inc(ln_c, 1)
                        a.wait_ge(ln_f, k + 3)
                        nc.scalar.activation(sig[at], sig[at], ACT.Exp, scale=-1.0).then_inc(sig_r, 1)

                    def by_edge(n, b, k, last):
                        nu = 1 if last else 2
                        for u in range(nu):
                            a.wait_ge(msg_ps, 2 * k + u + 5)
                            nc.scalar.activation(*evacuated(b, u), ACT.Copy).then_inc(msg_sb, 1)

                    def stage(wide):
                        pipelined(a, [(functions, 0), (by_edge, 1)] if wide else [(exps, 0), (sigmoid, 1), (both_logs, 0)], PAIRS)
                    when_fits(a, stage, bounded_i)

                @block.gpsimd
                def _(pool):
                    pool.sem_inc(msg_t_r, 2)
                    pool.sem_inc(y_r, 2)
                    nc.gpsimd.memset(msg[:, :, :, F:F + 1], 1.0).then_inc(ones_set, 1)

                    def core_affine(n, b, k, last):
                        nu = 1 if last else 2
                        pool.wait_ge(total_in[b], 64 * n + 64)
                        pool.wait_ge(soft_r, k + 1)
                        settle(pool)
                        nc.gpsimd.tensor_scalar(y[:, b, 0:nu, :], Ct[:, b, 0:nu, :], core[:, 0:1], core[:, 1:2],
                                                ALU.mult, ALU.add).then_inc(y_r, 1)

                    def multiply(wide, n, b, k, last):
                        nu = 1 if last else 2
                        at = (slice(None), b, slice(0, nu), slice(None))
                        pool.wait_ge(sig_r, k + 1)
                        if wide:
                            pool.wait_ge(soft_r, k + 3)
                        pool.wait_ge(msg_ps, 2 * k + 2)
                        nc.gpsimd.tensor_tensor(msg_t[at], sig[at], soft[at], ALU.mult).then_inc(msg_t_r, 1)

                    def stage(wide):
                        product = partial(multiply, wide)
                        pipelined(pool, [(core_affine, 0), (product, 1)] if wide else [(product, 0)], PAIRS)
                    when_fits(pool, stage, bounded_i)

                @block.tensor
                def _(pe):
                    pe.sem_inc(msg_ps, 4)
                    sums.start_tensor(pe)

                    def stage(general):
                        pe.wait_ge(ones_set, 1)

                        def transposes(n, b, k, last):
                            nu = 1 if last else 2
                            pe.wait_ge(msg_t_r, k + 3)
                            for u in range(nu):
                                pe.wait_ge(msg_sb, 2 * k + u + 1)
                                for c in range(4):
                                    done = nc.tensor.transpose(ps_m[2 * b + u][:, c, :], msg_t[:, b, u, c * P:(c + 1) * P], ident[:, :])
                                done.then_inc(msg_ps, 1)

                        def window_sums(n, b, k, last):
                            nu = 1 if last else 2
                            for u in range(nu):
                                pe.wait_ge(msg_sb, 2 * k + u + 5)
                                sums.products(pe, general, lambda s: msg[:, 2 * b + u, s, :], 2 * k + u, b, u)
                        pipelined(pe, [(transposes, 0), (window_sums, 1)], PAIRS)
                    when_fits(pe, stage)

        pairs_of_totals.close()

        dis = sb("dis", [NP, NT])
        out_b = sb("out_b", [NP, NT, F])
        agg2, agg2_l = sb("agg2", [2 * F, N + WIN]), sb("agg2_l", [F, N])
        zeros2 = sem("zeros2")
        W1, w1_in = sb("W1", [2 * F, F]), sem("w1_in")
        with ExitStack() as st:
            U = sb("U", [F + 1, N], fp32, st)
            V = sb("V", [NP, NT, F + 1], fp32, st)
            T1, T2 = sb("T1", [NP, NT, F], fp32, st), sb("T2", [NP, NT, F], fp32, st)
            X1 = sb("X1", [NP, NT, F], fp32, st)
            nrow = sb("nrow", [NP, 6, NT], fp32, st)
            ab = sb("ab", [F + 1, 2], fp32, st)
            mv2 = sb("mv2", [F, 6], fp32, st)
            gb2 = sb("gb2", [F, 2], fp32, st)
            deg_max, few = sb("deg_max", [F + 1, 2], fp32, st), sb("few", [1, 1], i32, st)
            b1_bc = sb("b1_bc", [NP, F], fp32, st)
            NSTAT = -(-N // 512)
            cuts = [N * k // NSTAT for k in range(NSTAT + 1)]
            stats2 = sb("stats2", [F, NSTAT, 6], fp32, st)
            ps_v = [psum(f"ps_v{k}", [NP, 7, F + 1], st) for k in range(4)]
            vchunks = [(c, min(7, NT - 7 * c)) for c in range(-(-NT // 7))]
            assert len(vchunks) <= 4
            p_in, nd, na, v_ps, v_sb, g_out, g_ready = (sem(n) for n in ("p_in", "nd", "na", "v_ps", "v_sb", "g_out", "g_ready"))

            with nc.Block() as block:
                @block.sync
                def _(sp):
                    sp.dma_start(gb2[:, 0:1], bn2_g.rearrange("(f a) -> f a", a=1)).then_inc(p_in, 16)
                    sp.dma_start(gb2[:, 1:2], bn2_b.rearrange("(f a) -> f a", a=1)).then_inc(p_in, 16)
                    sp.dma_start(b1_bc[:, :], b1.unsqueeze(0).to_broadcast([NP, F])).then_inc(p_in, 16)
                    for k in range(2):
                        sp.dma_start(W1[k * F:(k + 1) * F, :], w1[:, :]).then_inc(w1_in, 16)
                    sp.wait_ge(g_ready, 1)
                    sp.dma_start(g_tab.rearrange("(p t) f -> p t f", t=NT), T2[:, :, :]).then_inc(g_out, 16)
                    sp.wait_ge(g_out, 16)

                @block.gpsimd
                def _(pool):
                    nc.gpsimd.memset(agg2[:, :], 0.0).then_inc(zeros2, 1)
                    nc.gpsimd.memset(agg2_l[:, :], 0.0).then_inc(zeros2, 1)
                    pool.wait_ge(zeros2, 2)

                @block.vector
                def _(v):
                    done = [0]

                    def step(ins):
                        done[0] += 1
                        ins.then_inc(nd, 1)
                        v.wait_ge(nd, done[0])

                    def per_node(k):
                        return nrow[:, k, :].unsqueeze(2).to_broadcast([NP, NT, F])

                    step(nc.vector.memset(ab[:, 0:1], 1.0))
                    step(nc.vector.memset(ab[:, 1:2], 0.0))
                    for k in range(NSTAT):
                        last = nc.vector.bn_stats(stats2[:, k, :], agg[0:F, cuts[k]:cuts[k + 1]])
                    step(last)
                    step(nc.vector.bn_aggr(mv2[:, 0:2], stats2[:, :, :].rearrange("f k s -> f (k s)")))
                    step(nc.vector.tensor_scalar(mv2[:, 2:3], mv2[:, 1:2], EPS, None, ALU.add))
                    v.wait_ge(na, 1)
                    step(nc.vector.reciprocal(mv2[:, 4:5], mv2[:, 3:4]))
                    v.wait_ge(p_in, 48)
                    step(nc.vector.tensor_tensor(ab[0:F, 0:1], mv2[:, 4:5], gb2[:, 0:1], ALU.mult))
                    step(nc.vector.tensor_tensor(mv2[:, 5:6], mv2[:, 0:1], ab[0:F, 0:1], ALU.mult))
                    step(nc.vector.tensor_tensor(ab[0:F, 1:2], gb2[:, 1:2], mv2[:, 5:6], ALU.subtract))
                    step(nc.vector.tensor_scalar(U[:, :], agg[:, 0:N], ab[:, 0:1], ab[:, 1:2], ALU.mult, ALU.add))
                    step(nc.vector.reduce_max(deg_max[F:F + 1, 0:1], agg[F:F + 1, 0:N], axis=AX.X))
                    step(nc.vector.tensor_scalar(deg_max[F:F + 1, 1:2], deg_max[F:F + 1, 0:1], 255.5, None, ALU.is_lt))
                    step(nc.vector.tensor_copy(few[:, :], deg_max[F:F + 1, 1:2]))
                    step(nc.vector.tensor_tensor(counted_i[:, :], few[:, :], fits_i[:, :], ALU.mult))
                    v.wait_ge(v_sb, len(vchunks))
                    step(nc.vector.tensor_tensor(T1[:, :, :], V[:, :, 0:F], H[:, :, :], ALU.add))
                    step(nc.vector.tensor_scalar(T2[:, :, :], T1[:, :, :], CAP, None, ALU.min))
                    step(nc.vector.tensor_scalar(nrow[:, 0, :], V[:, :, F], 1.0, None, ALU.max))
                    step(nc.vector.tensor_scalar(nrow[:, 1, :], V[:, :, F], 0.5, None, ALU.is_gt))
                    v.wait_ge(na, 3)
                    step(nc.vector.tensor_tensor(T1[:, :, :], T1[:, :, :], T2[:, :, :], ALU.max))
                    step(nc.vector.tensor_tensor(X1[:, :, :], X[:, :, :], T1[:, :, :], ALU.add))
                    v.wait_ge(na, 4)
                    step(nc.vector.reciprocal(nrow[:, 3, :], nrow[:, 2, :]))
                    step(nc.vector.tensor_tensor(dis[:, :], nrow[:, 3, :], nrow[:, 1, :], ALU.mult))
                    step(nc.vector.reduce_sum(nrow[:, 0, :], X1[:, :, :], axis=AX.X))
                    step(nc.vector.tensor_scalar(nrow[:, 1, :], nrow[:, 0, :], 1.0 / F, None, ALU.mult))
                    step(nc.vector.tensor_tensor(T1[:, :, :], X1[:, :, :], per_node(1), ALU.subtract))
                    step(nc.vector.tensor_tensor(T2[:, :, :], T1[:, :, :], T1[:, :, :], ALU.mult))
                    step(nc.vector.reduce_sum(nrow[:, 0, :], T2[:, :, :], axis=AX.X))
                    step(nc.vector.tensor_scalar(nrow[:, 3, :], nrow[:, 0, :], 1.0 / F, EPS, ALU.mult, ALU.add))
                    v.wait_ge(na, 5)
                    step(nc.vector.reciprocal(nrow[:, 5, :], nrow[:, 4, :]))
                    step(nc.vector.tensor_tensor(nrow[:, 1, :], nrow[:, 5, :], dis[:, :], ALU.mult))
                    nc.vector.scalar_tensor_tensor(T2[:, :, :], T1[:, :, :], 0.0, per_node(1), ALU.max, ALU.mult).then_inc(g_ready, 1)
                    nc.vector.tensor_tensor(out_b[:, :, :], X1[:, :, :], b1_bc[:, :].unsqueeze(1).to_broadcast([NP, NT, F]),
                                            ALU.add)

                @block.scalar
                def _(a):
                    a.wait_ge(nd, 5)
                    nc.scalar.activation(mv2[:, 3:4], mv2[:, 2:3], ACT.Sqrt).then_inc(na, 1)
                    for c, k in vchunks:
                        a.wait_ge(v_ps, c + 1)
                        nc.scalar.activation(V[:, 7 * c:7 * c + k, :], ps_v[c][:, 0:k, :], ACT.Copy).then_inc(v_sb, 1)
                    a.preload_act_table_set("natural_log_exp_and_others")
                    a.wait_ge(nd, 16)
                    nc.scalar.activation(T2[:, :, :], T2[:, :, :], ACT.Exp).then_inc(na, 1)
                    a.wait_ge(na, 2)
                    nc.scalar.activation(T2[:, :, :], T2[:, :, :], ACT.Ln, bias=1.0).then_inc(na, 1)
                    a.wait_ge(nd, 17)
                    nc.scalar.activation(nrow[:, 2, :], nrow[:, 0, :], ACT.Sqrt).then_inc(na, 1)
                    a.wait_ge(nd, 28)
                    nc.scalar.activation(nrow[:, 4, :], nrow[:, 3, :], ACT.Sqrt).then_inc(na, 1)

                @block.tensor
                def _(pe):
                    pe.wait_ge(nd, 10)
                    nodes = U[:, :].rearrange("f (p t) -> f t p", t=NT)
                    for c, k in vchunks:
                        for t in range(k):
                            last = nc.tensor.transpose(ps_v[c][:, t, :], nodes[:, 7 * c + t, :], ident[0:F + 1, 0:F + 1])
                        last.then_inc(v_ps, 1)

        with ExitStack() as st:
            idx2 = sb("idx2", [P, 2, SLOTS], i32, st)
            R = sb("R", [P, 2, SLOTS, F], fp32, st)
            sums = WindowSums("c", st, agg2, F, 1)
            G = sb("G", [P, HI, F], fp32, st)
            G_hm = sb("G_hm", [P, HI, 2, F], bf16, st)
            G_l = sb("G_l", [P, HI, F], bf16, st)
            TC = 3
            CHUNK = TC * NP
            dchunks = [(c, TC * c, min(TC, NT - TC * c)) for c in range(-(-NT // TC))]
            cnt_b = sb("cnt_b", [P, 2, HI, CHUNK], bf16, st)
            ps_hm = [psum(f"ps_hm{k}", [P, CHUNK], st) for k in range(2)]
            ps_l = [psum(f"ps_l{k}", [F, CHUNK], st) for k in range(2)]
            scaled = sb("scaled", [NP, 2, TC, F], fp32, st)
            ps_o = [psum(f"ps_o{k}", [NP, TC, F], st) for k in range(2)]
            o_ps, o_mul, o_sb, stored = (sem(n) for n in ("o_ps", "o_mul", "o_sb", "stored"))

            def by_t(tile, t0, k):
                return tile[:, 0:N].rearrange("f (p t) -> f t p", t=NT)[:, t0:t0 + k, :]

            def counts_of(part, t0, k):
                return count[:, part, 0:N].rearrange("q h (p t) -> q h t p", t=NT)[:, :, t0:t0 + k, :]

            def counts_into(part, c, k):
                return cnt_b[:, c % 2, part, 0:k * NP].rearrange("q h (t p) -> q h t p", p=NP)

            def output_products(pe, c, t0, k):
                if c >= 2:
                    pe.wait_ge(o_mul, c - 1)
                for t in range(k):
                    nc.tensor.matmul(ps_o[c % 2][:, t, :], by_t(agg2, t0 + t, 1).rearrange("f a p -> f (a p)"), W1[:, :], start=True, stop=False)
                    last = nc.tensor.matmul(ps_o[c % 2][:, t, :], by_t(agg2_l, t0 + t, 1).rearrange("f a p -> f (a p)"), W1[0:F, :], start=False, stop=True)
                last.then_inc(o_ps, 1)

            def output_sums(v, c, t0, k):
                at = (slice(None), slice(t0, t0 + k), slice(None))
                v.wait_ge(o_ps, c + 1)
                nc.vector.tensor_tensor(scaled[:, c % 2, 0:k, :], ps_o[c % 2][:, 0:k, :],
                                        dis[:, t0:t0 + k].unsqueeze(2).to_broadcast([NP, k, F]), ALU.mult).then_inc(o_mul, 1)
                v.wait_ge(o_mul, c + 1)
                nc.vector.tensor_tensor(out_b[at], out_b[at], scaled[:, c % 2, 0:k, :], ALU.add).then_inc(o_sb, 1)

            g_in, g_zero, split, split_done = sem("g_in"), sem("g_zero"), sem("split"), sem("split_done")
            cvt_v, cvt_a, prod, prod_sb = sem("cvt_v"), sem("cvt_a"), sem("prod"), sem("prod_sb")
            idx2_in = [sem(f"idx2_in{u}") for u in range(2)]
            rows_in = [sem(f"rows_in{u}") for u in range(2)]
            rows_used, idx2_set = sem("rows_used"), sem("idx2_set")

            with nc.Block() as block:
                @block.sync
                def _(sp):
                    def stage(general):
                        if not general:
                            whole = N // P
                            sp.dma_start(G[:, 0:whole, :], g_tab[0:whole * P, :].rearrange("(t p) f -> p t f", p=P)).then_inc(g_in, 16)
                            sp.wait_ge(g_zero, 1)
                            if N % P:
                                sp.dma_start(G[0:N % P, whole, :], g_tab[whole * P:N, :]).then_inc(g_in, 16)
                            return

                        def group(i, u, g, tail):
                            sp.wait_ge(rows_used, g + 1)
                            settle(sp)
                            if tail:
                                sp.wait_ge(idx2_set, 1)
                            load_by_edge(sp, lambda p, h, q: by_half(idx2, u)[p, h, q], src, g, tail, idx2_in[u])
                            sums.load_dst(sp, u, g, tail)
                        groups(sp, group)
                    when_fits(sp, stage, counted_i)
                    for c, t0, k in dchunks:
                        sp.wait_ge(o_sb, c + 1)
                        sp.dma_start(out.rearrange("(p t) f -> p t f", t=NT)[:, t0:t0 + k, :],
                                     out_b[:, t0:t0 + k, :]).then_inc(stored, 16)
                    sp.wait_ge(stored, 16 * len(dchunks))

                @block.gpsimd
                def _(pool):
                    def stage(general):
                        if not general:
                            settle(pool)
                            return

                        def group(i, u, g, tail):
                            pool.wait_ge(idx2_in[u], 16 * i + 16 * (TAIL_LOADS if tail else 1))
                            settle(pool)
                            for s in range(SLOTS):
                                pool.indirect_dma_start(R[:, u, s, :], None, g_tab[:, :],
                                                        bass.IndirectOffsetOnAxis(ap=idx2[:, u, s:s + 1], axis=0)).then_inc(rows_in[u], 16)
                        groups(pool, group)
                    when_fits(pool, stage, counted_i)

                T_V = 15

                @block.vector
                def _(v):
                    sums.start_vector(v)

                    def by_product():
                        def convert(c, t0, k):
                            if c >= 2:
                                v.wait_ge(prod, 2 * c - 2)
                            nc.vector.tensor_copy(counts_into(slice(0, T_V), c, k), counts_of(slice(0, T_V), t0, k)).then_inc(cvt_v, 1)

                        nc.vector.memset(G[:, N // P:HI, :], 0.0).then_inc(g_zero, 1)
                        for chunk in dchunks[:2]:
                            convert(*chunk)
                        v.wait_ge(g_in, 32 if N % P else 16)
                        nc.vector.tensor_copy(G_hm[:, :, 0, :], G[:, :, :]).then_inc(split, 1)
                        v.wait_ge(split, 1)
                        nc.vector.tensor_tensor(G[:, :, :], G[:, :, :], G_hm[:, :, 0, :], ALU.subtract).then_inc(split, 1)
                        v.wait_ge(split, 2)
                        nc.vector.tensor_copy(G_hm[:, :, 1, :], G[:, :, :]).then_inc(split, 1)
                        v.wait_ge(split, 3)
                        nc.vector.tensor_tensor(G_l[:, :, :], G[:, :, :], G_hm[:, :, 1, :], ALU.subtract).then_inc(split_done, 1)
                        for chunk in dchunks[2:]:
                            convert(*chunk)
                            if chunk[0] >= 3:
                                output_sums(v, *dchunks[chunk[0] - 3])
                        for chunk in dchunks[-3:]:
                            output_sums(v, *chunk)

                    def stage(general):
                        if not general:
                            by_product()
                            return

                        def group(i, u, g, tail):
                            if tail:
                                v.wait_ge(rows_used, g + 1)
                                nc.vector.memset(idx2[:, u, :], 0).then_inc(idx2_set, 1)
                            sums.all_windows(v, i, u, g, tail)
                        groups(v, group)
                        for chunk in dchunks:
                            output_sums(v, *chunk)
                    when_fits(v, stage, counted_i)

                @block.scalar
                def _(a):
                    def stage(general):
                        if general:
                            settle(a)
                            return

                        def convert(c, t0, k):
                            if c >= 2:
                                a.wait_ge(prod, 2 * c - 2)
                            nc.scalar.activation(counts_into(slice(T_V, HI), c, k), counts_of(slice(T_V, HI), t0, k), ACT.Copy).then_inc(cvt_a, 1)

                        def take(c, t0, k):
                            a.wait_ge(prod, 2 * c + 1)
                            nc.scalar.activation(by_t(agg2, t0, k), ps_hm[c % 2][:, 0:k * NP].rearrange("f (t p) -> f t p", p=NP), ACT.Copy).then_inc(prod_sb, 1)
                            a.wait_ge(prod, 2 * c + 2)
                            nc.scalar.activation(by_t(agg2_l, t0, k), ps_l[c % 2][:, 0:k * NP].rearrange("f (t p) -> f t p", p=NP), ACT.Copy).then_inc(prod_sb, 1)

                        for k in range(len(dchunks) + 1):
                            if k < len(dchunks):
                                convert(*dchunks[k])
                            if k >= 1:
                                take(*dchunks[k - 1])
                    when_fits(a, stage, counted_i)

                @block.tensor
                def _(pe):
                    pe.wait_ge(w1_in, 32)
                    pe.sem_inc(rows_used, 2)
                    sums.start_tensor(pe)

                    def stage(general):
                        if not general:
                            pe.wait_ge(split, 3)
                            for c, t0, k in dchunks:
                                n = k * NP
                                pe.wait_ge(cvt_v, c + 1)
                                pe.wait_ge(cvt_a, c + 1)
                                if c >= 2:
                                    pe.wait_ge(prod_sb, 2 * c - 2)
                                for t in range(HI):
                                    last = nc.tensor.matmul(ps_hm[c % 2][:, 0:n], G_hm[:, t, :, :].rearrange("p k f -> p (k f)"),
                                                            cnt_b[:, c % 2, t, 0:n], start=(t == 0), stop=(t == HI - 1))
                                last.then_inc(prod, 1)
                                if c == 0:
                                    pe.wait_ge(split_done, 1)
                                for t in range(HI):
                                    last = nc.tensor.matmul(ps_l[c % 2][:, 0:n], G_l[:, t, :],
                                                            cnt_b[:, c % 2, t, 0:n], start=(t == 0), stop=(t == HI - 1))
                                last.then_inc(prod, 1)
                                if c >= 1:
                                    pe.wait_ge(prod_sb, 2 * c)
                                    output_products(pe, *dchunks[c - 1])
                            pe.wait_ge(prod_sb, 2 * len(dchunks))
                            output_products(pe, *dchunks[-1])
                            return

                        def group(i, u, g, tail):
                            pe.wait_ge(rows_in[u], 16 * SLOTS * i + 16 * SLOTS)
                            sums.products(pe, general, lambda s: R[:, u, s, :], g, 0, u)
                            pe.wait_ge(sums.summed, (g + 1) * NW + 2)
                            pe.sem_inc(rows_used, 1)
                        groups(pe, group)
                        pe.wait_ge(sums.added, NG * NW + 2)
                        for chunk in dchunks:
                            output_products(pe, *chunk)
                    when_fits(pe, stage, counted_i)


INPUTS = ["x", "src", "dst", "edge_attr_64", "L0_gnn_W_full", "L0_gnn_b_full", "L0_gnn_bn1_g", "L0_gnn_bn1_b",
          "L0_gnn_bn2_g", "L0_gnn_bn2_b", "L1_gnn_W", "L1_gnn_b"]


def kernel(**inputs):
    import concourse.bacc as bacc
    from concourse.bass_utils import run_bass_kernel_spmd as run

    nc = bacc.Bacc("TRN2", target_bir_lowering=False, num_devices=1)
    arrays = {"in_" + k: np.ascontiguousarray(inputs[k]) for k in INPUTS}
    args = [nc.dram_tensor(k, v.shape, mybir.dt.from_np(v.dtype), kind="ExternalInput").ap() for k, v in arrays.items()]
    result = nc.dram_tensor("out_0", inputs["x"].shape, mybir.dt.float32, kind="ExternalOutput").ap()
    build_gnn(nc, *args, result)
    r = run(nc, [arrays], core_ids=[0])
    return r.results[0]["out_0"]
```
